# Optimizing a Trainium2 kernel written in Bass

```python
import numpy as np
import jax
import jax.numpy as jnp

def _softmax(x, axis=-1):
    return jax.nn.softmax(x, axis=axis)

def _gelu(x):
    return jax.nn.gelu(x, approximate=True)

def _silu(x):
    return jax.nn.silu(x)

def _sigmoid(x):
    return jax.nn.sigmoid(x)

def _layernorm(x, axis=-1, eps=1e-05):
    m = jnp.mean(x, axis=axis, keepdims=True)
    v = jnp.var(x, axis=axis, keepdims=True)
    return (x - m) / jnp.sqrt(v + eps)

def _scatter_add(tgt, idx, src, axis=0):
    return tgt.at[idx].add(src)

def _segment_sum(src, seg, n):
    return jax.ops.segment_sum(src, seg, n)
kernel_name = 'mk_sandwich_d2_jaxref_r4_b49410'

def setup_inputs(seed: int=0):
    np.random.seed(seed)
    _w = jnp.asarray

    def _L0_attn_setup():
        import jax, jax.numpy as jnp
        import numpy as np
        H = 256
        M = 256
        FF = 1024
        WIN = 16
        SLOTS = 10
        B, S = (2, 1024)
        EPS_LN = 1e-05
        EPS_NORM = 1e-12

        def _layernorm(x, g, b):
            m = jnp.mean(x, axis=-1, keepdims=True)
            v = jnp.var(x, axis=-1, keepdims=True)
            return (x - m) / jnp.sqrt(v + EPS_LN) * g + b
        key = jax.random.key(seed)
        ks = jax.random.split(key, 12)

        def lin_w(k, out_d, in_d):
            return jax.random.normal(k, (out_d, in_d), jnp.float32) / np.sqrt(in_d)
        return {'x': jax.random.normal(ks[0], (B, S, H), jnp.float32), 'mem_W': lin_w(ks[1], M, M), 'mem_b': jnp.zeros((M,), jnp.float32), 'P': jax.random.normal(ks[2], (SLOTS, M), jnp.float32), 'Wi': lin_w(ks[3], M, H), 'bi': jnp.zeros((M,), jnp.float32), 'Wl1': lin_w(ks[4], M, M), 'bl1': jnp.zeros((M,), jnp.float32), 'Wl2': lin_w(ks[5], M, M), 'bl2': jnp.zeros((M,), jnp.float32), 'Wo': lin_w(ks[6], H, M), 'bo': jnp.zeros((H,), jnp.float32), 'fgate': jnp.ones((1,), jnp.float32), 'lrate': jnp.ones((1,), jnp.float32), 'Wg': lin_w(ks[7], H, 2 * H), 'bg': jnp.zeros((H,), jnp.float32), 'W1': lin_w(ks[8], FF, H), 'b1': jnp.zeros((FF,), jnp.float32), 'W2': lin_w(ks[9], H, FF), 'b2': jnp.zeros((H,), jnp.float32), 'g1': jnp.ones((H,), jnp.float32), 'be1': jnp.zeros((H,), jnp.float32), 'g2': jnp.ones((H,), jnp.float32), 'be2': jnp.zeros((H,), jnp.float32), 'g3': jnp.ones((H,), jnp.float32), 'be3': jnp.zeros((H,), jnp.float32)}
    _L0_attn_in = _L0_attn_setup()

    def _L0_ffn_setup():
        import jax, jax.numpy as jnp
        import numpy as np
        B, L, H, E, I = (4, 512, 256, 8, 1024)
        S = B * L
        CAP_FACTOR_EVAL = 2.0
        MIN_CAP = 4
        _cap = int(np.floor(CAP_FACTOR_EVAL * S / E))
        _cap += _cap % 2
        CAPACITY = max(_cap, MIN_CAP)

        def _layer_norm(x, g, b, eps=1e-05):
            mu = x.mean(-1, keepdims=True)
            var = ((x - mu) ** 2).mean(-1, keepdims=True)
            return (x - mu) * jax.lax.rsqrt(var + eps) * g + b
        key = jax.random.key(seed)
        ks = jax.random.split(key, 8)
        gate_std = float(np.sqrt(0.1 / H))
        return {'inputs': jax.random.normal(ks[0], (B, L, H), jnp.float32), 'gate_weight': jax.random.normal(ks[1], (E, H), jnp.float32) * gate_std, 'ln_gamma': jnp.ones((H,), jnp.float32), 'ln_beta': jnp.zeros((H,), jnp.float32), 'wi': jax.random.normal(ks[2], (E, H, I), jnp.float32) * float(1.0 / np.sqrt(H)), 'wo': jax.random.normal(ks[3], (E, I, H), jnp.float32) * float(1.0 / np.sqrt(I)), 'conf_w1': jax.random.normal(ks[4], (H // 2, H), jnp.float32) * float(np.sqrt(2.0 / (H + H // 2))), 'conf_b1': -jnp.ones((H // 2,), jnp.float32), 'conf_w2': jax.random.normal(ks[5], (1, H // 2), jnp.float32) * float(np.sqrt(2.0 / (1 + H // 2))), 'conf_b2': -jnp.ones((1,), jnp.float32), 'comp_w': jax.random.normal(ks[6], (1, H), jnp.float32) * float(1.0 / np.sqrt(H)), 'comp_b': jnp.zeros((1,), jnp.float32)}
    _L0_ffn_in = _L0_ffn_setup()

    def _L1_attn_setup():
        import jax, jax.numpy as jnp
        import numpy as np
        DIM = 256
        B, N = (8, 1024)
        EPS = 1e-06
        key = jax.random.key(seed)
        k1, k2, k3, k4 = jax.random.split(key, 4)
        x = jax.random.normal(k1, (B, N, DIM), dtype=jnp.float32)
        s = 1.0 / np.sqrt(DIM)
        W_qkv = jax.random.uniform(k2, (3 * DIM, DIM), jnp.float32, -s, s)
        W_out = jax.random.uniform(k3, (DIM, DIM), jnp.float32, -s, s)
        b_out = jax.random.uniform(k4, (DIM,), jnp.float32, -s, s)
        return {'x': x, 'W_qkv': W_qkv, 'W_out': W_out, 'b_out': b_out}
    _L1_attn_in = _L1_attn_setup()

    def _L1_ffn_setup():
        import jax, jax.numpy as jnp
        import numpy as np
        key = jax.random.key(seed)
        ks = jax.random.split(key, 5)
        B, Sq, M, E, H = (4, 512, 256, 8, 1024)
        x = jax.random.normal(ks[0], (B, Sq, M), dtype=jnp.float32)
        wg = jax.random.normal(ks[1], (M, E), dtype=jnp.float32) * (1.0 / np.sqrt(M))
        w1 = jax.random.normal(ks[2], (E, M, H), dtype=jnp.float32) * (1.0 / np.sqrt(M))
        b1 = jnp.zeros((E, H), dtype=jnp.float32)
        w2 = jax.random.normal(ks[3], (E, H, M), dtype=jnp.float32) * (1.0 / np.sqrt(H))
        b2 = jnp.zeros((E, M), dtype=jnp.float32)
        return {'x': x, 'wg': wg, 'w1': w1, 'b1': b1, 'w2': w2, 'b2': b2}
    _L1_ffn_in = _L1_ffn_setup()
    _d = {'L0_attn_x': _L0_attn_in['x'], 'L0_attn_mem_W': _L0_attn_in['mem_W'], 'L0_attn_mem_b': _L0_attn_in['mem_b'], 'L0_attn_P': _L0_attn_in['P'], 'L0_attn_Wi': _L0_attn_in['Wi'], 'L0_attn_bi': _L0_attn_in['bi'], 'L0_attn_Wl1': _L0_attn_in['Wl1'], 'L0_attn_bl1': _L0_attn_in['bl1'], 'L0_attn_Wl2': _L0_attn_in['Wl2'], 'L0_attn_bl2': _L0_attn_in['bl2'], 'L0_attn_Wo': _L0_attn_in['Wo'], 'L0_attn_bo': _L0_attn_in['bo'], 'L0_attn_fgate': _L0_attn_in['fgate'], 'L0_attn_lrate': _L0_attn_in['lrate'], 'L0_attn_Wg': _L0_attn_in['Wg'], 'L0_attn_bg': _L0_attn_in['bg'], 'L0_attn_W1': _L0_attn_in['W1'], 'L0_attn_b1': _L0_attn_in['b1'], 'L0_attn_W2': _L0_attn_in['W2'], 'L0_attn_b2': _L0_attn_in['b2'], 'L0_attn_g1': _L0_attn_in['g1'], 'L0_attn_be1': _L0_attn_in['be1'], 'L0_attn_g2': _L0_attn_in['g2'], 'L0_attn_be2': _L0_attn_in['be2'], 'L0_attn_g3': _L0_attn_in['g3'], 'L0_attn_be3': _L0_attn_in['be3'], 'L0_ffn_gate_weight': _L0_ffn_in['gate_weight'], 'L0_ffn_ln_gamma': _L0_ffn_in['ln_gamma'], 'L0_ffn_ln_beta': _L0_ffn_in['ln_beta'], 'L0_ffn_wi': _L0_ffn_in['wi'], 'L0_ffn_wo': _L0_ffn_in['wo'], 'L0_ffn_conf_w1': _L0_ffn_in['conf_w1'], 'L0_ffn_conf_b1': _L0_ffn_in['conf_b1'], 'L0_ffn_conf_w2': _L0_ffn_in['conf_w2'], 'L0_ffn_conf_b2': _L0_ffn_in['conf_b2'], 'L0_ffn_comp_w': _L0_ffn_in['comp_w'], 'L0_ffn_comp_b': _L0_ffn_in['comp_b'], 'L1_attn_W_qkv': _L1_attn_in['W_qkv'], 'L1_attn_W_out': _L1_attn_in['W_out'], 'L1_attn_b_out': _L1_attn_in['b_out'], 'L1_ffn_wg': _L1_ffn_in['wg'], 'L1_ffn_w1': _L1_ffn_in['w1'], 'L1_ffn_b1': _L1_ffn_in['b1'], 'L1_ffn_w2': _L1_ffn_in['w2'], 'L1_ffn_b2': _L1_ffn_in['b2']}
    _x0 = _d['L0_attn_x']
    _d['L0_attn_x'] = jax.random.normal(jax.random.fold_in(jax.random.key(seed), 1), (8, 1024, 256), dtype=_x0.dtype)
    del _x0
    return _d

def reference(L0_attn_x, L0_attn_mem_W, L0_attn_mem_b, L0_attn_P, L0_attn_Wi, L0_attn_bi, L0_attn_Wl1, L0_attn_bl1, L0_attn_Wl2, L0_attn_bl2, L0_attn_Wo, L0_attn_bo, L0_attn_fgate, L0_attn_lrate, L0_attn_Wg, L0_attn_bg, L0_attn_W1, L0_attn_b1, L0_attn_W2, L0_attn_b2, L0_attn_g1, L0_attn_be1, L0_attn_g2, L0_attn_be2, L0_attn_g3, L0_attn_be3, L0_ffn_gate_weight, L0_ffn_ln_gamma, L0_ffn_ln_beta, L0_ffn_wi, L0_ffn_wo, L0_ffn_conf_w1, L0_ffn_conf_b1, L0_ffn_conf_w2, L0_ffn_conf_b2, L0_ffn_comp_w, L0_ffn_comp_b, L1_attn_W_qkv, L1_attn_W_out, L1_attn_b_out, L1_ffn_wg, L1_ffn_w1, L1_ffn_b1, L1_ffn_w2, L1_ffn_b2):

    def _L0_attn_ref(x, mem_W, mem_b, P, Wi, bi, Wl1, bl1, Wl2, bl2, Wo, bo, fgate, lrate, Wg, bg, W1, b1, W2, b2, g1, be1, g2, be2, g3, be3):
        import jax, jax.numpy as jnp
        import numpy as np
        H = 256
        M = 256
        FF = 1024
        WIN = 16
        SLOTS = 10
        B, S = (2, 1024)
        EPS_LN = 1e-05
        EPS_NORM = 1e-12

        def _layernorm(x, g, b):
            m = jnp.mean(x, axis=-1, keepdims=True)
            v = jnp.var(x, axis=-1, keepdims=True)
            return (x - m) / jnp.sqrt(v + EPS_LN) * g + b
        b, s, h = x.shape
        k_full = jnp.concatenate([x, jnp.broadcast_to(P, (b,) + P.shape)], axis=1)
        idx = jnp.arange(s)[:, None] + jnp.arange(-WIN, 1)[None, :]
        valid = idx >= 0
        k_win = k_full[:, jnp.maximum(idx, 0)]
        scores = jnp.einsum('bsh,bswh->bsw', x, k_win) * h ** (-0.5)
        scores = jnp.where(valid[None], scores, -jnp.inf)
        attn_out = jnp.einsum('bsw,bswh->bsh', jax.nn.softmax(scores, axis=-1), k_win)
        x1 = _layernorm(x + attn_out, g1, be1)
        kv = k_full.reshape(-1, h)
        kn = kv / jnp.maximum(jnp.linalg.norm(kv, axis=-1, keepdims=True), EPS_NORM)
        kp = kn @ Wi.T + bi
        vp = kp
        hdd = jax.nn.silu(kp @ Wl1.T + bl1)
        hdd = jax.nn.silu(hdd @ Wl2.T + bl2)
        pred = hdd @ mem_W.T + mem_b
        diff = pred - vp
        n, m = diff.shape
        grad_W = 2.0 / (n * m) * diff.T @ hdd
        W_new = (1.0 - fgate) * mem_W + lrate * grad_W
        mem_out = hdd @ W_new.T + mem_b
        mo = (mem_out @ Wo.T + bo).reshape(b, -1, h)[:, :s]
        gate = jax.nn.sigmoid(jnp.concatenate([x1, mo], axis=-1) @ Wg.T + bg)
        combined = gate * x1 + (1.0 - gate) * mo
        x2 = _layernorm(x1 + combined, g2, be2)
        ff = jax.nn.silu(x2 @ W1.T + b1) @ W2.T + b2
        return _layernorm(x2 + ff, g3, be3)

    def _L0_ffn_ref(inputs, gate_weight, ln_gamma, ln_beta, wi, wo, conf_w1, conf_b1, conf_w2, conf_b2, comp_w, comp_b):
        import jax, jax.numpy as jnp
        import numpy as np
        B, L, H, E, I = (4, 512, 256, 8, 1024)
        S = B * L
        CAP_FACTOR_EVAL = 2.0
        MIN_CAP = 4
        _cap = int(np.floor(CAP_FACTOR_EVAL * S / E))
        _cap += _cap % 2
        CAPACITY = max(_cap, MIN_CAP)

        def _layer_norm(x, g, b, eps=1e-05):
            mu = x.mean(-1, keepdims=True)
            var = ((x - mu) ** 2).mean(-1, keepdims=True)
            return (x - mu) * jax.lax.rsqrt(var + eps) * g + b
        tokens = inputs.reshape(-1, H)
        residual = tokens
        tokens = _layer_norm(tokens, ln_gamma, ln_beta)
        complexity_score = jax.nn.sigmoid(tokens @ comp_w.T + comp_b).mean()
        hdn = jax.nn.relu(tokens @ conf_w1.T + conf_b1)
        confidence_score = jax.nn.sigmoid(hdn @ conf_w2.T + conf_b2).mean()
        logits = tokens.astype(jnp.float32) @ gate_weight.astype(jnp.float32).T
        probs = jax.nn.softmax(logits, axis=-1)
        top1 = jnp.argmax(logits, axis=-1)
        onehot = jax.nn.one_hot(top1, E, dtype=jnp.int32)
        rank_e = jnp.cumsum(onehot, axis=0) - onehot
        rank = jnp.sum(rank_e * onehot, axis=-1)
        keep = rank < CAPACITY
        weight = jnp.take_along_axis(probs, top1[:, None], axis=-1)[:, 0]
        weight = (weight * keep).astype(tokens.dtype)
        slot = jnp.where(keep, rank, 0)
        dispatch = jnp.zeros((E, CAPACITY, H), tokens.dtype)
        dispatch = dispatch.at[top1, slot].add(tokens * keep[:, None])
        h = jax.nn.gelu(jnp.einsum('ech,ehi->eci', dispatch, wi), approximate=False)
        expert_out = jnp.einsum('eci,eih->ech', h, wo)
        combined = weight[:, None] * expert_out[top1, slot]
        out = (residual + combined).reshape(inputs.shape)
        return out

    def _L1_attn_ref(x, W_qkv, W_out, b_out):
        import jax, jax.numpy as jnp
        import numpy as np
        DIM = 256
        B, N = (8, 1024)
        EPS = 1e-06
        qkv = jnp.einsum('bnd,ed->bne', x, W_qkv)
        q, k, v = jnp.split(qkv, 3, axis=-1)
        q = jax.nn.relu(q) + EPS
        k = jax.nn.relu(k) + EPS
        kv = jnp.einsum('bnd,bne->bde', k, v)
        z = 1.0 / (jnp.einsum('bnd,bd->bn', q, k.sum(axis=1)) + EPS)
        attn = jnp.einsum('bnd,bde,bn->bne', q, kv, z)
        return jnp.einsum('bne,fe->bnf', attn, W_out) + b_out

    def _L1_ffn_ref(x, wg, w1, b1, w2, b2):
        import jax, jax.numpy as jnp
        import numpy as np
        B, Sq, M = x.shape
        E = wg.shape[1]
        S = B * Sq
        C = S // E
        xt = x.reshape(S, M)
        gates = jax.nn.softmax(xt @ wg, axis=-1)
        expert_idx = jnp.argmax(gates, axis=-1)
        mask1 = jax.nn.one_hot(expert_idx, E, dtype=xt.dtype)
        locations = jnp.cumsum(mask1, axis=0) - 1.0
        pos = jnp.sum(locations * mask1, axis=1).astype(jnp.int32)
        keep = (pos < C).astype(xt.dtype)
        gate_val = jnp.sum(gates * mask1, axis=1) * keep
        slot = expert_idx.astype(jnp.int32) * C + jnp.clip(pos, 0, C - 1)
        disp = jnp.zeros((E * C, M), dtype=xt.dtype).at[slot].add(xt * keep[:, None])
        disp = disp.reshape(E, C, M)
        h = jax.nn.relu(jnp.einsum('ecm,emh->ech', disp, w1) + b1[:, None, :])
        eo = jnp.einsum('ech,ehm->ecm', h, w2) + b2[:, None, :]
        out = eo.reshape(E * C, M)[slot] * gate_val[:, None]
        return out.reshape(B, Sq, M)
    x = L0_attn_x
    x = x + _layernorm(_L0_attn_ref(_layernorm(x, axis=-1), L0_attn_mem_W, L0_attn_mem_b, L0_attn_P, L0_attn_Wi, L0_attn_bi, L0_attn_Wl1, L0_attn_bl1, L0_attn_Wl2, L0_attn_bl2, L0_attn_Wo, L0_attn_bo, L0_attn_fgate, L0_attn_lrate, L0_attn_Wg, L0_attn_bg, L0_attn_W1, L0_attn_b1, L0_attn_W2, L0_attn_b2, L0_attn_g1, L0_attn_be1, L0_attn_g2, L0_attn_be2, L0_attn_g3, L0_attn_be3), axis=-1)
    x = x + _layernorm(_L0_ffn_ref(_layernorm(x, axis=-1), L0_ffn_gate_weight, L0_ffn_ln_gamma, L0_ffn_ln_beta, L0_ffn_wi, L0_ffn_wo, L0_ffn_conf_w1, L0_ffn_conf_b1, L0_ffn_conf_w2, L0_ffn_conf_b2, L0_ffn_comp_w, L0_ffn_comp_b), axis=-1)
    x = x + _layernorm(_L1_attn_ref(_layernorm(x, axis=-1), L1_attn_W_qkv, L1_attn_W_out, L1_attn_b_out), axis=-1)
    x = x + _layernorm(_L1_ffn_ref(_layernorm(x, axis=-1), L1_ffn_wg, L1_ffn_w1, L1_ffn_b1, L1_ffn_w2, L1_ffn_b2), axis=-1)
    return x

_drawn_inputs = setup_inputs


def setup_inputs(seed=0):
    import zlib

    import numpy as np

    out = dict(_drawn_inputs(seed))
    spreads = {'L0_attn_mem_b': (0.0, 2.0),
     'L0_attn_bi': (0.0, 0.8),
     'L0_attn_bl1': (0.0, 0.8),
     'L0_attn_bl2': (0.0, 0.764),
     'L0_attn_bo': (0.0, 2.0),
     'L0_attn_bg': (0.0, 2.0),
     'L0_attn_b1': (0.0, 0.1),
     'L0_attn_b2': (0.0, 0.1),
     'L0_attn_g1': (1.0, 0.6),
     'L0_attn_be1': (0.0, 2.0),
     'L0_attn_g2': (1.0, 0.2),
     'L0_attn_be2': (0.0, 0.1),
     'L0_attn_g3': (1.0, 0.2),
     'L0_attn_be3': (0.0, 0.1),
     'L0_ffn_ln_gamma': (1.0, 0.2),
     'L0_ffn_ln_beta': (0.0, 0.1),
     'L0_ffn_conf_b1': (-1.0, 0.2),
     'L1_ffn_b1': (0.0, 0.278),
     'L1_ffn_b2': (0.0, 0.1)}
    factors = {'L0_attn_mem_W': 8.0,
     'L0_attn_P': 69.064,
     'L0_attn_Wi': 8.0,
     'L0_attn_Wl1': 8.0,
     'L0_attn_Wl2': 8.0}
    for name, (base, spread) in spreads.items():
        noise = np.random.default_rng([zlib.crc32(name.encode()), seed]).standard_normal(out[name].shape)
        drawn = base * np.exp(spread * noise) if base else spread * noise
        out[name] = jnp.asarray(drawn.astype(out[name].dtype))
    for name, factor in factors.items():
        out[name] = (out[name] * factor).astype(out[name].dtype)
    return out
```

```python
from contextlib import ExitStack

import concourse.bass as bass
from concourse import mybir

F = mybir.dt.float32
R = mybir.dt.float32r
BF = mybir.dt.bfloat16
U = mybir.dt.uint32
I = mybir.dt.int32
ALU = mybir.AluOpType
ACT = mybir.ActivationFunctionType
AX = mybir.AxisListType

T = 8192
H = 256
G = 16
E = 8
PW = 264
EPS = 1e-5
N_MEM = 8 * 1034
NEG = -1.0e30
FAR = 1.0e6


class Token:

    def __init__(self, queue, at):
        self.queue, self.at = queue, at


class Landed:

    def __init__(self, sem, value):
        self.sem, self.value = sem, value


class Engine:

    def __init__(self, sem):
        self.sem, self.ops, self.marked = sem, [], set()

    def put(self, fn, w, sem=None):
        for t in w:
            if isinstance(t, Token):
                t.queue.marked.add(t.at)
        assert all(isinstance(t, (Token, Landed)) for t in w)
        self.ops.append((fn, w, sem))
        return Token(self, len(self.ops) - 1)

    def matmul(self, out, lhsT, rhs, w=(), **k):
        return self.put(lambda e: e.matmul(out, lhsT, rhs, **k), w)

    def transpose(self, out, in_, identity, w=()):
        return self.put(lambda e: e.transpose(out, in_, identity), w)

    def activation(self, out, in_, func, w=(), **k):
        return self.put(lambda e: e.activation(out, in_, func, **k), w)

    def tensor_tensor(self, out, in0, in1, op, w=()):
        return self.put(lambda e: e.tensor_tensor(out, in0, in1, op), w)

    def tensor_scalar(self, out, in0, s1, s2, op0, op1=ALU.bypass, w=()):
        return self.put(lambda e: e.tensor_scalar(out, in0, s1, s2, op0, op1), w)

    def scalar_tensor_tensor(self, out, in0, s, in1, op0, op1, w=()):
        return self.put(lambda e: e.scalar_tensor_tensor(out, in0, s, in1, op0, op1), w)

    def tensor_reduce(self, out, in_, axis, op, w=()):
        return self.put(lambda e: e.tensor_reduce(out, in_, axis, op), w)

    def tensor_copy(self, out, in_, w=()):
        return self.put(lambda e: e.tensor_copy(out, in_), w)

    def reciprocal(self, out, in_, w=()):
        return self.put(lambda e: e.reciprocal(out, in_), w)

    def memset(self, out, value, w=()):
        return self.put(lambda e: e.memset(out, value), w)

    def bn_stats(self, out, in_, w=()):
        return self.put(lambda e: e.bn_stats(out, in_), w)

    def bn_aggr(self, out, in_, w=()):
        return self.put(lambda e: e.bn_aggr(out, in_), w)

    def iota(self, out, w=(), **k):
        return self.put(lambda e: e.iota(out, **k), w)

    def affine_select(self, w=(), **k):
        return self.put(lambda e: e.affine_select(**k), w)

    def number(self):
        self.count, n = [], 0
        for i in range(len(self.ops)):
            n += i in self.marked
            self.count.append(n)

    def write(self, eng):
        seen = {}
        for i, (fn, w, sem) in enumerate(self.ops):
            need = {}
            for t in w:
                s, v = (t.queue.sem, t.queue.count[t.at]) if isinstance(t, Token) else (t.sem, t.value)
                if v > max(seen.get(id(s), 0), need.get(id(s), (None, 0))[1]):
                    need[id(s)] = (s, v)
            for k, (s, v) in need.items():
                eng.wait_ge(s, v)
                seen[k] = v
            ins = fn(eng)
            if sem is not None:
                ins.then_inc(sem, 16)
            elif i in self.marked:
                ins.then_inc(self.sem, 1)


class Tile:

    def __init__(self, ap, name):
        self.ap, self.last, self.held, self.name = ap, [], False, name


class Store:

    def __init__(self, tiles):
        self.idle = list(tiles)
        self.name = tiles[0].name

    def take(self):
        assert self.idle, "no tile left: " + self.name
        t = self.idle.pop(0)
        t.held = True
        return t

    def give(self, t, *last):
        assert t.held
        t.held = False
        t.last = list(last)
        self.idle.append(t)


def build(nc, io, stop=None):
    ctx = ExitStack()
    with ctx:
        def sb(name, shape, dt=F):
            return ctx.enter_context(nc.sbuf_tensor(name, shape, dt))

        def new_sem(name):
            return ctx.enter_context(nc.semaphore(name))

        def dram(name, shape, dt=F):
            return nc.dram_tensor(name, shape, dt, kind="Internal").ap()

        pe, act, ve, po, sp = (Engine(new_sem("q_" + n)) for n in ("pe", "act", "dve", "pool", "sp"))

        landed = {}
        stores = []

        def sent_on(sem, store):
            landed[id(sem)] = landed.get(id(sem), 0) + 16
            t = Landed(sem, landed[id(sem)])
            if store:
                stores.append(t)
            return t

        def dma(queue, sem, dst, src, w=(), store=False):
            queue.put(lambda e: e.dma_start(dst, src), w, sem)
            return sent_on(sem, store)

        def scatter(sem, dst, idx, src, bound, w=()):
            po.put(lambda e: e.indirect_dma_start(dst, bass.IndirectOffsetOnAxis(idx, 0), src, None,
                                                  bounds_check=bound, oob_is_err=False), w, sem)
            return sent_on(sem, True)

        def tiles(name, n, shape, dt=F):
            whole = sb(name, [128, n] + shape, dt)
            return Store([Tile(whole[:, i], name) for i in range(n)])

        d_h = dram("d_h", [G, 128, 2, 1024], R)
        d_p1 = dram("d_p1", [E * 512, PW])
        d_p2 = dram("d_p2", [E * 1024, PW])
        d_x1 = dram("d_x1", [T, H])
        out = io["out"]

        units = Store([Tile(ctx.enter_context(nc.psum_tensor(f"ps{i}", [128, 1024], F))[:, :], "psum")
                       for i in range(4)])

        wslot = [sb(f"wslot{i}", [128, 8192], R) for i in range(2)]
        small = sb("small", [128, 5200], R)
        stage = tiles("stage", 1, [2048])
        ft = tiles("ft", 11, [1024])
        rt = tiles("rt", 9, [1024], R)
        borrowed = [Tile(wslot[1][:, 4096 + i * 1024:5120 + i * 1024], "rt") for i in range(4)]
        rt.idle += borrowed
        hk = None
        pay = tiles("pay", 2, [4, PW])
        ident = sb("ident", [128, 128])
        tri = sb("tri", [128, 128], BF)
        ones = sb("ones", [128, 128], BF)
        oner = sb("oner", [128, 2], R)
        mask = sb("mask", [128, 2, 160])
        desc = sb("desc", [128, 8])
        offs = sb("offs", [128, 2, 8])
        ids = sb("ids", [128, 64], I)
        half = sb("half", [128, 8])
        ecol = sb("ecol", [128, 32])
        mean = sb("mean", [128, 64])
        rstd = sb("rstd", [128, 64])
        ks = sb("ks", [128, 64])
        base = sb("base", [128, 2, 8])
        hsum = sb("hsum", [128, 2, 18])
        cols = sb("cols", [128, 64])
        rows = sb("rows", [128, 12, 256])
        bst = tiles("bst", 3, [4, 6])
        sm = tiles("sm", 8, [64])
        rtl = tiles("rtl", 6, [64])
        ohs = tiles("ohs", 2, [32], BF)

        def setup():
            c = {}
            a = po.memset(ident[:, :], 0.0)
            c["ident"] = po.affine_select(out=ident[:, :], in_=ident[:, :], compare_op=ALU.not_equal, fill=1.0,
                base=0, pattern=[[-1, 128]], channel_multiplier=1, w=(a,))
            a = ve.memset(ones[:, :], 1.0)
            c["tri"] = po.affine_select(out=tri[:, :], in_=ones[:, :], compare_op=ALU.is_gt, fill=0.0, base=0,
                pattern=[[1, 128]], channel_multiplier=-1, w=(a,))
            a = ve.memset(mask[:, :, :], 0.0)
            b = po.affine_select(out=mask[:, :, :], in_=mask[:, :, :], compare_op=ALU.is_ge, fill=NEG, base=32,
                pattern=[[0, 2], [-1, 160]], channel_multiplier=1, w=(a,))
            b = po.affine_select(out=mask[:, :, :], in_=mask[:, :, :], compare_op=ALU.is_ge, fill=NEG, base=-16,
                pattern=[[0, 2], [1, 160]], channel_multiplier=-1, w=(b,))
            c["mask"] = po.memset(mask[:, 1, 0:32], NEG, w=(b,))
            po.iota(desc[:, :], pattern=[[-1, 8]], base=8, channel_multiplier=0, allow_small_or_imprecise_dtypes=True)
            po.iota(offs[:, 0, :], pattern=[[512, 8]], base=0, channel_multiplier=0,
                allow_small_or_imprecise_dtypes=True)
            po.iota(offs[:, 1, :], pattern=[[1024, 8]], base=0, channel_multiplier=0,
                allow_small_or_imprecise_dtypes=True)
            po.iota(ids[:, :], pattern=[[128, 64]], base=0, channel_multiplier=1)
            po.memset(half[:, 0:4], -0.5)
            po.memset(half[:, 4:8], 0.5)
            po.memset(base[:, :, :], 0.0)
            c["pool"] = po.memset(ecol[:, :], 2.718281828459045)
            a = ve.memset(cols[:, 60:61], 0.0)
            c["oner"] = act.activation(oner[:, :], ones[:, 0:2], ACT.Copy, w=(a,))
            return c

        C = setup()

        s_w = new_sem("s_w")

        def load(dst, src, *w):
            return dma(sp, s_w, dst, src, w=(*w,))

        def col(at, name, n=2):
            load(cols[:, at:at + n], io[name])
            return cols[:, at:at + n]

        def row(at, name):
            load(rows[:, at, :], io[name].partition_broadcast(128))
            return rows[:, at, :]

        memb_c, bi_c, bl1_c, bl2_c, bo_c = (col(2 * i, n) for i, n in enumerate(
            ("mem_b_c", "bi_c", "bl1_c", "bl2_c", "bo_c")))
        b1_c = col(10, "b1_c", 8)
        lng_c, lnb_c = col(18, "ln_g_c"), col(20, "ln_b_c")
        load(cols[:, 22:23], io["fgate"].partition_broadcast(128))
        load(cols[:, 23:24], io["lrate"].partition_broadcast(128))
        rows_in = [row(i, n) for i, n in enumerate(
            ("g1", "be1", "g2", "be2", "g3", "be3", "b2", "bo", "bg", "b_out"))]
        g1_r, be1_r, g2_r, be2_r, g3_r, be3_r, b2_r, bo_r, bg_r, bout_r = rows_in
        mb_row = sb("mb_row", [1, 512])
        load(mb_row[0:1, 0:256], io["mem_b"].partition_broadcast(1))
        load(mb_row[0:1, 256:512], io["bi"].partition_broadcast(1))
        gwT = sb("gwT", [128, 2, 8])
        wgT = sb("wgT", [128, 2, 8])
        load(gwT[:, :, :], io["gate_wT"].rearrange("(c p) e -> p c e", p=128))
        w_small = load(wgT[:, :, :], io["wg"].rearrange("(c p) e -> p c e", p=128))

        def f32(ap):
            return ap.bitcast(F)

        def v3(ap, a, b):
            return ap.rearrange("p (a b) -> p a b", a=a, b=b)

        def split(hi, lo, src, *w, engine="v"):
            a = act.activation(hi, src, ACT.Copy, w=(*w,))
            put = ve if engine == "v" else po
            b = put.tensor_tensor(lo, src, f32(hi), ALU.subtract, w=(a,))
            return a, b

        def evac(hi, lo, ps, *w):
            a = act.activation(hi, ps, ACT.Copy, w=(*w,))
            b = ve.tensor_tensor(lo, ps, f32(hi), ALU.subtract, w=(a,))
            return a, b

        stage_sem = {id(t): new_sem(f"s_st{i}") for i, t in enumerate(stage.idle)}

        def chunks(ap, n):
            return ap.rearrange("(c p) n -> p c n", p=128)

        def ff_weights(slot, w1, w2, *w, w2_waits=()):
            s = wslot[slot]
            parts = dict(w1h=v3(s[:, 0:2048], 2, 1024), w1l=v3(s[:, 2048:4096], 2, 1024),
                         w2h=v3(s[:, 4096:6144], 8, 256), w2l=v3(s[:, 6144:8192], 8, 256))
            st = stage.take()
            t = dma(sp, stage_sem[id(st)], v3(st.ap, 2, 1024), chunks(w1, 1024), w=(*st.last,))
            a, b = split(s[:, 0:2048], s[:, 2048:4096], st.ap, t, *w)
            stage.give(st, a, b)
            parts["t1"] = b
            st2 = stage.take()
            t = dma(sp, stage_sem[id(st2)], v3(st2.ap, 8, 256), chunks(w2, 256), w=(*st2.last,))
            a, b = split(s[:, 4096:6144], s[:, 6144:8192], st2.ap, t, *w, *w2_waits)
            stage.give(st2, a, b)
            parts["t2"] = b
            return parts

        def stats(x, out_mv, *w):
            st = bst.take()
            t = None
            for i in range(4):
                t = ve.bn_stats(st.ap[:, i, :], x[:, i, :], w=(*w, *st.last))
            w = ()
            for i in range(4):
                b = ve.bn_aggr(out_mv[:, i, :], st.ap[:, i, :], w=(t,))
            bst.give(st, b)
            return b, t

        def rsqrt(dst, var, tmp, *w):
            a = po.tensor_scalar(tmp, var, EPS, None, ALU.add, w=(*w,))
            return po.tensor_tensor(dst, tmp, half[:, 0:4], ALU.pow, w=(a, C["pool"]))

        def norm(dst, x, m, r, *w):
            for i in range(4):
                t = ve.tensor_scalar(dst[:, i, :], x[:, i, :], m[:, i:i + 1], r[:, i:i + 1], ALU.subtract, ALU.mult,
                    w=(*w,))
            return t

        def transposes(ps, x, *w, n=4):
            for i in range(n):
                for c in range(2):
                    t = pe.transpose(ps[:, c * 512 + i * 128:c * 512 + i * 128 + 128], x[:, i, c * 128:(c + 1) * 128],
                        ident[:, :], w=(*w, C["ident"]))
            return t

        def to_tokens(ps, xT, *w):
            for i in range(4):
                for c in range(2):
                    t = pe.transpose(ps[:, i * 256 + c * 128:i * 256 + c * 128 + 128], xT[:,
                        c * 512 + i * 128:c * 512 + i * 128 + 128], ident[:, :], w=(*w, C["ident"]))
            return t

        def three(o, pairs, start, stop, w=()):
            ops = []
            for lh, ll, rh, rl in pairs:
                ops += [(lh, rh), (lh, rl), (ll, rh)]
            for j, (a, b) in enumerate(ops):
                t = pe.matmul(o, a, b, start=start and j == 0, stop=stop and j == len(ops) - 1, skip_group_check=True,
                    w=(*w,))
            return t

        def wide(ps, wh, wl, xh, xl, n, w, oc):
            return three(ps, [(wh[:, c, oc * 128:oc * 128 + 128], wl[:, c, oc * 128:oc * 128 + 128],
                               xh[:, c * 512:c * 512 + n], xl[:, c * 512:c * 512 + n]) for c in range(2)],
                         True, True, w)

        def ff(xh, xl, W, func, bias, done, *w):
            o = None
            pend = []
            pieces = []

            def second(j, fh, fl, th, tl):
                nonlocal o
                if o is None:
                    o = units.take()
                for i in range(4):
                    for k in range(2):
                        c = 2 * j + k
                        t = three(o.ap[:, i * 256:(i + 1) * 256],
                                  [(fh.ap[:, k * 512 + i * 128:k * 512 + i * 128 + 128],
                                    fl.ap[:, k * 512 + i * 128:k * 512 + i * 128 + 128],
                                    W["w2h"][:, c, :], W["w2l"][:, c, :])],
                                  j == 0 and k == 0 and i % 2 == 0, j == 3 and k == 1,
                                  (th, tl, W["t2"], *o.last))
                rt.give(fh, t)
                rt.give(fl, t)
                return t

            for j in range(4):
                ps = units.take()
                for k in range(2):
                    t = wide(ps.ap[:, k * 512:(k + 1) * 512], W["w1h"], W["w1l"], xh, xl, 512,
                             (*w, W["t1"], *ps.last), 2 * j + k)
                f, fh, fl = ft.take(), rt.take(), rt.take()
                for k in range(2):
                    b = bias[:, 2 * j + k:2 * j + k + 1] if bias is not None else 0.0
                    a = act.activation(f.ap[:, k * 512:(k + 1) * 512], ps.ap[:, k * 512:(k + 1) * 512], func, bias=b,
                        w=(t, *f.last))
                for k in range(2):
                    b = bias[:, 2 * j + k:2 * j + k + 1] if bias is not None else 0.0
                    th = act.activation(fh.ap[:, k * 512:(k + 1) * 512], ps.ap[:, k * 512:(k + 1) * 512], func,
                        bias=b, w=(*fh.last,))
                units.give(ps, th)
                tl = (ve if j % 2 else po).tensor_tensor(fl.ap, f.ap, f32(fh.ap), ALU.subtract, w=(a, th, *fl.last))
                ft.give(f, tl)
                pend.append((j, fh, fl, th, tl))
                last_in = t
                yield
                if j >= 1:
                    second(*pend.pop(0))
                    yield
            done["x"] = last_in
            done["t"] = second(*pend.pop(0))
            done["o"] = o
            yield

        def route(which, cap, xT, wT, dst_slot, dst_w, *w):
            ps = units.take()
            for i in range(4):
                for c in range(2):
                    t = pe.matmul(ps.ap[:, i * 8:i * 8 + 8], xT[:, c * 512 + i * 128:c * 512 + i * 128 + 128], wT[:,
                        c, :], start=c == 0, stop=c == 1, w=(w_small, *w, *ps.last))
            last_x = t
            lg, cd, s, oh = rtl.take(), rtl.take(), sm.take(), ohs.take()
            L, X = v3(lg.ap[:, 0:32], 4, 8), v3(lg.ap[:, 32:64], 4, 8)
            code, sl = v3(cd.ap[:, 0:32], 4, 8), v3(cd.ap[:, 32:64], 4, 8)
            mx, cm, se = s.ap[:, 0:4], s.ap[:, 4:8], s.ap[:, 8:12]
            slf = s.ap[:, 12:16]
            t = ve.tensor_copy(L, v3(ps.ap[:, 0:32], 4, 8), w=(t, *lg.last))
            units.give(ps, t)
            t1 = ve.tensor_reduce(mx, L, AX.X, ALU.max, w=(t, *s.last))
            mxb = mx.unsqueeze(2).to_broadcast([128, 4, 8])
            t2 = ve.tensor_tensor(X, L, mxb, ALU.subtract, w=(t1,))
            t3 = ve.tensor_scalar(code, X, 0.0, None, ALU.is_equal, w=(t2, *cd.last))
            tp = po.tensor_tensor(lg.ap[:, 0:32], ecol[:, :], lg.ap[:, 32:64], ALU.pow, w=(t2, C["pool"]))
            t4 = ve.tensor_tensor(code, code, desc[:, :].unsqueeze(1).to_broadcast([128, 4, 8]), ALU.mult, w=(t3,))
            t5 = ve.tensor_reduce(cm, code, AX.X, ALU.max, w=(t4,))
            t6 = ve.tensor_tensor(v3(oh.ap, 4, 8), code, cm.unsqueeze(2).to_broadcast([128, 4, 8]), ALU.is_equal,
                w=(t5, *oh.last))
            yield
            ps = units.take()
            for i in range(5):
                ops = [(ones, k) for k in range(min(i, 4))] + ([(tri, i)] if i < 4 else [])
                for n, (m, k) in enumerate(ops):
                    t = pe.matmul(ps.ap[:, i * 8:i * 8 + 8], m[:, :], oh.ap[:, k * 8:k * 8 + 8], start=n == 0,
                        stop=n == len(ops) - 1, w=(t6, C["tri"], *ps.last))
            t1 = ve.tensor_tensor(sl, v3(ps.ap[:, 0:32], 4, 8), base[:, which, :].unsqueeze(1).to_broadcast([128, 4,
                8]), ALU.add, w=(t, base_t[which], C["pool"]))
            t2 = ve.tensor_tensor(base[:, which, :], base[:, which, :], ps.ap[:, 32:40], ALU.add, w=(t1,))
            base_t[which] = t2
            units.give(ps, t2)
            t3 = ve.tensor_scalar(code, sl, float(cap), FAR, ALU.is_ge, ALU.mult, w=(t1,))
            t4 = ve.tensor_tensor(sl, sl, offs[:, which, :].unsqueeze(1).to_broadcast([128, 4, 8]), ALU.add, w=(t3,))
            t5 = ve.tensor_tensor(sl, sl, code, ALU.add, w=(t4,))
            t6 = ve.tensor_tensor(sl, sl, v3(oh.ap, 4, 8), ALU.mult, w=(t5,))
            t7 = ve.tensor_reduce(slf, sl, AX.X, ALU.add, w=(t6,))
            t8 = ve.tensor_copy(dst_slot, slf, w=(t7,))
            t9 = ve.tensor_reduce(se, L, AX.X, ALU.add, w=(tp,))
            t10 = ve.reciprocal(dst_w, se, w=(t9,))
            ohs.give(oh, t6)
            rtl.give(lg, t10)
            rtl.give(cd, t8)
            sm.give(s, t10)
            return last_x, t8, t10

        base_t = [C["pool"], C["pool"]]

        pay_sem = {id(t): new_sem(f"s_pay{i}") for i, t in enumerate(pay.idle)}
        ft_sem = {id(t): new_sem(f"s_ft{i}") for i, t in enumerate(ft.idle)}
        rt_sem = {id(t): new_sem(f"s_rt{i}") for i, t in enumerate(rt.idle)}
        out_sem = {id(t): new_sem(f"s_out{i}") for i, t in enumerate(pay.idle)}
        scat_sem = {id(t): new_sem(f"s_sc{i}") for i, t in enumerate(pay.idle + ft.idle)}
        s_b1 = new_sem("s_b1")
        s_fill = new_sem("s_fill")

        def tok_rows(ap, g):
            return ap[g * 512:(g + 1) * 512, :].rearrange("(t p) n -> p t n", p=128)

        def load_x(src, g, *w):
            t = ft.take()
            ld = dma(sp, ft_sem[id(t)], v3(t.ap, 4, 256), tok_rows(src, g), w=(*t.last, *w))
            return t, ld

        def run(gens, lag):
            live, i, r = [], 0, 0
            while live or i < len(gens):
                if i < len(gens) and (r % lag == 0 or not live):
                    live.append(gens[i])
                    i += 1
                for g in list(live):
                    try:
                        next(g)
                    except StopIteration:
                        live.remove(g)
                r += 1

        def fill():
            f = pay.take()
            a = ve.memset(f.ap[:, :, :], 0.0)
            b = ve.memset(f.ap[:, :, 260:261].bitcast(U), 1000000, w=(a,))
            for d, n in ((d_p1, E), (d_p2, 2 * E)):
                for i in range(n):
                    t = dma(sp, s_fill, tok_rows(d, i), f.ap[:, :, :], w=(b,), store=True)
            pay.give(f, t)
            return t

        filled = fill()

        w1p_h, w1p_l = v3(small[:, 0:512], 2, 256), v3(small[:, 512:1024], 2, 256)
        wl2_h, wl2_l = v3(small[:, 1024:1536], 2, 256), v3(small[:, 1536:2048], 2, 256)
        a12_h, a12_l = v3(small[:, 2048:3072], 2, 512), v3(small[:, 3072:4096], 2, 512)
        wg1_h, wg1_l = v3(small[:, 4096:4608], 2, 256), v3(small[:, 4608:5120], 2, 256)

        def load_f(name, t=None):
            t = t or ft.take()
            ld = dma(sp, ft_sem[id(t)], v3(t.ap[:, 0:512], 2, 256), chunks(io[name], 256), w=(*t.last,))
            return t, v3(t.ap[:, 0:512], 2, 256), ld

        def mm256(ps, lhs, rhs, w, start=True, stop=True):
            for oc in range(2):
                for c in range(2):
                    t = pe.matmul(ps[:, oc * 512:oc * 512 + 256], lhs[:, c, oc * 128:oc * 128 + 128], rhs[:, c, :],
                        start=start and c == 0, stop=stop and c == 1, w=(*w,))
            return t

        def two(ps):
            return ps.rearrange("p (a b) -> p a b", a=2)[:, :, 0:256]

        def prepare():
            r = {}
            wi, wi_v, t1 = load_f("Wi")
            wl1, wl1_v, t2 = load_f("Wl1T")
            ps = units.take()
            t = mm256(ps.ap, wi_v, wl1_v, (t1, t2, *ps.last))
            a, b = evac(w1p_h, w1p_l, two(ps.ap), t)
            units.give(ps, a, b)
            r["w1p"] = b
            ps = units.take()
            for oc in range(2):
                for c in range(2):
                    t = pe.matmul(ps.ap[:, oc:oc + 1], wl1_v[:, c, oc * 128:oc * 128 + 128], bi_c[:, c:c + 1],
                        start=c == 0, stop=c == 1, w=(w_small, *ps.last))
            r["b1p"] = ve.tensor_tensor(cols[:, 24:26], ps.ap[:, 0:2], bl1_c, ALU.add, w=(t,))
            units.give(ps, r["b1p"])
            ft.give(wi, t)
            ft.give(wl1, t)
            wl2, wl2_v, t1 = load_f("Wl2T")
            a, b = split(wl2_h, wl2_l, wl2_v, t1)
            r["wl2"] = b
            ft.give(wl2, a, b)
            return r

        P = prepare()
        b1p = cols[:, 24:26]

        gram = units.take()

        def hidden(kT, n, acc, *w):
            ps = units.take()
            for oc in range(2):
                t = wide(ps.ap[:, oc * 512:oc * 512 + n], w1p_h, w1p_l, kT[0].ap, kT[1].ap, n,
                         (*w, P["w1p"], *ps.last), oc)
            rt.give(kT[0], t)
            rt.give(kT[1], t)
            f, fh, fl = ft.take(), rt.take(), rt.take()
            for dst in (f, fh):
                for oc in range(2):
                    a = act.activation(dst.ap[:, oc * 512:oc * 512 + n], ps.ap[:, oc * 512:oc * 512 + n], ACT.Silu,
                        bias=b1p[:, oc:oc + 1], w=(t, P["b1p"], *dst.last))
            units.give(ps, a)
            tl = None
            for oc in range(2):
                s = slice(oc * 512, oc * 512 + n)
                tl = ve.tensor_tensor(fl.ap[:, s], f.ap[:, s], f32(fh.ap[:, s]), ALU.subtract, w=(a, *fl.last))
            ft.give(f, tl)
            yield
            ps = units.take()
            for oc in range(2):
                t = wide(ps.ap[:, oc * 512:oc * 512 + n], wl2_h, wl2_l, fh.ap, fl.ap, n,
                         (tl, P["wl2"], *ps.last), oc)
            rt.give(fh, t)
            rt.give(fl, t)
            h, hh = ft.take(), rt.take()
            m = n if n == 512 else 10
            for oc in range(2):
                a1 = act.activation(h.ap[:, oc * 512:oc * 512 + m], ps.ap[:, oc * 512:oc * 512 + m], ACT.Silu,
                    bias=bl2_c[:, oc:oc + 1], accum_out=acc[oc], w=(t, w_small, *h.last))
            if n == 512:
                for oc in range(2):
                    a = act.activation(hh.ap[:, oc * 512:oc * 512 + n], ps.ap[:, oc * 512:oc * 512 + n], ACT.Silu,
                        bias=bl2_c[:, oc:oc + 1], w=(*hh.last,))
            else:
                a = a1
            units.give(ps, a)
            return h, hh, a1, a

        def slots_of_memory():
            x, kt = ft.take(), ft.take()
            z = ve.memset(x.ap[:, 0:256], 0.0, w=(*x.last,))
            ld = dma(sp, ft_sem[id(x)], x.ap[0:10, 0:256], io["P"], w=(z,))
            s = sm.take()
            a = act.activation(x.ap[:, 256:512], x.ap[:, 0:256], ACT.Square, accum_out=s.ap[:, 0:1], w=(ld, z))
            b = po.tensor_tensor(s.ap[:, 1:2], s.ap[:, 0:1], half[:, 4:5], ALU.pow, w=(a, C["pool"]))
            b = ve.tensor_scalar(s.ap[:, 2:3], s.ap[:, 1:2], 1e-12, None, ALU.max, w=(b,))
            b = ve.reciprocal(s.ap[:, 3:4], s.ap[:, 2:3], w=(b,))
            kn = ve.tensor_scalar(x.ap[:, 512:768], x.ap[:, 0:256], s.ap[:, 3:4], None, ALU.mult, w=(b,))
            sm.give(s, kn)
            ps = units.take()
            for c in range(2):
                t = pe.transpose(ps.ap[:, c * 512:c * 512 + 128], x.ap[:, 512 + c * 128:512 + c * 128 + 128], ident[:,
                    :], w=(kn, C["ident"], *ps.last))
            kh, kl = rt.take(), rt.take()
            for c in range(2):
                q = slice(c * 512, c * 512 + 128)
                a, b = evac(kh.ap[:, q], kl.ap[:, q], ps.ap[:, q], t)
            units.give(ps, a, b)
            hg = hidden((kh, kl), 128, [hsum[:, 0, 16:17], hsum[:, 1, 16:17]], a, b)
            while True:
                try:
                    next(hg)
                except StopIteration as e:
                    h, hh, a1, _ = e.value
                    break
            rt.give(hh, *hh.last)
            ps = units.take()
            for c in range(2):
                t = pe.transpose(ps.ap[0:10, c * 128:c * 128 + 128], h.ap[:, c * 512:c * 512 + 10], ident[:, :],
                    w=(a1, *ps.last))
            ft.give(h, t)
            rh, rl, ll = rt.take(), rt.take(), rt.take()
            z = ve.memset(kt.ap, 0.0, w=(*kt.last,))
            z1 = ve.tensor_copy(kt.ap[0:10, 0:256], ps.ap[0:10, 0:256], w=(z, t))
            z2 = ve.tensor_copy(kt.ap[:, 256:512], x.ap[:, 512:768], w=(kn, z))
            z3 = ve.tensor_scalar(kt.ap[0:10, 512:768], ps.ap[0:10, 0:256], 8.0, None, ALU.mult, w=(z2,))
            units.give(ps, z3)
            a, b = split(rh.ap[:, 0:512], rl.ap[:, 0:512], kt.ap[:, 0:512], z1, z2, *rh.last, *rl.last)
            a, b2 = split(ll.ap[:, 0:256], ll.ap[:, 256:512], kt.ap[:, 512:768], z3, *ll.last)
            ft.give(kt, a, b, b2)
            ft.give(x, z2, a)
            for c in range(2):
                t = three(gram.ap[:, c * 512:(c + 1) * 512],
                          [(ll.ap[:, c * 128:c * 128 + 128], ll.ap[:, 256 + c * 128:256 + c * 128 + 128],
                            rh.ap[:, 0:512], rl.ap[:, 0:512])], True, False, (b, b2, *gram.last))
            for q in (rh, rl, ll):
                rt.give(q, t)
            return a1

        pt = slots_of_memory()
        hstore = []

        def first(g):
            x, ld = load_x(io["x"], g)
            yield
            s = sm.take()
            mv = v3(s.ap[:, 0:8], 4, 2)
            xv = v3(x.ap, 4, 256)
            c4 = slice(4 * g, 4 * g + 4)
            t, _ = stats(xv, mv, ld, *s.last)
            t0 = ve.tensor_copy(mean[:, c4], mv[:, :, 0], w=(t,))
            r = rsqrt(rstd[:, c4], mv[:, :, 1], s.ap[:, 8:12], t)
            a = po.tensor_tensor(s.ap[:, 12:16], mv[:, :, 1], half[:, 4:8], ALU.pow, w=(t,))
            a = po.tensor_tensor(s.ap[:, 16:20], s.ap[:, 12:16], rstd[:, c4], ALU.mult, w=(a, r))
            b = ve.tensor_scalar(s.ap[:, 20:24], s.ap[:, 16:20], 16.0, 1e-12, ALU.mult, ALU.max, w=(a,))
            b = ve.reciprocal(s.ap[:, 24:28], s.ap[:, 20:24], w=(b,))
            b = ve.tensor_tensor(s.ap[:, 28:32], s.ap[:, 24:28], rstd[:, c4], ALU.mult, w=(b,))
            kn = ft.take()
            t = norm(v3(kn.ap, 4, 256), xv, mean[:, c4], s.ap[:, 28:32], b, t0, *kn.last)
            sm.give(s, t)
            ft.give(x, t)
            yield
            knv = v3(kn.ap, 4, 256)
            ps = units.take()
            tt = transposes(ps.ap, knv, t, *ps.last)
            kh, kl = rt.take(), rt.take()
            a, b = evac(kh.ap, kl.ap, ps.ap, tt, *kh.last, *kl.last)
            units.give(ps, a, b)
            rows_h, rows_l = [rt.take(), rt.take()], [rt.take(), rt.take()]
            for k in range(2):
                rv, lv = v3(rows_h[k].ap, 2, 512), v3(rows_l[k].ap, 2, 512)
                ka = act.activation(rv[:, :, 256:512], knv[:, 2 * k:2 * k + 2, :], ACT.Copy, w=(t, *rows_h[k].last))
                kb = po.tensor_tensor(lv[:, :, 256:512], knv[:, 2 * k:2 * k + 2, :], f32(rv[:, :, 256:512]),
                    ALU.subtract, w=(ka, *rows_l[k].last))
            ft.give(kn, tt, kb)
            yield
            h, hh, a1, a = yield from hidden((kh, kl), 512, [hsum[:, 0, g:g + 1], hsum[:, 1, g:g + 1]], a, b)
            hl = rt.take()
            b = po.tensor_tensor(hl.ap, h.ap, f32(hh.ap), ALU.subtract, w=(a, *hl.last))
            o1 = dma(sp, rt_sem[id(hh)], f32(d_h[g, :, 0, :]), f32(hh.ap), w=(a,), store=True)
            o2 = dma(sp, rt_sem[id(hl)], f32(d_h[g, :, 1, :]), f32(hl.ap), w=(b,), store=True)
            hstore.append((o1, o2))
            rt.give(hh, o1, b)
            rt.give(hl, o2)
            yield
            ps = units.take()
            t = to_tokens(ps.ap, h.ap, a1, *ps.last)
            ft.give(h, t, b)
            for k in range(2):
                rv, lv = v3(rows_h[k].ap, 2, 512), v3(rows_l[k].ap, 2, 512)
                src = v3(ps.ap[:, k * 512:(k + 1) * 512], 2, 256)
                a, b = evac(rv[:, :, 0:256], lv[:, :, 0:256], src, t)
            units.give(ps, a, b)
            yield
            for i in range(4):
                rh, rl = rows_h[i // 2].ap, rows_l[i // 2].ap
                o = (i % 2) * 512
                for c in range(2):
                    t = three(gram.ap[:, c * 512:(c + 1) * 512],
                              [(rh[:, o + c * 128:o + c * 128 + 128], rl[:, o + c * 128:o + c * 128 + 128],
                                rh[:, o:o + 512], rl[:, o:o + 512])], False, g == G - 1 and i == 3, (a, b, kb))
            for q in rows_h + rows_l:
                rt.give(q, t)
            first_done[g] = t

        first_done = {}
        sent = [[], []]
        run([first(g) for g in range(G)], 3)

        def middle():
            wo, wo_v, t_wo = load_f("WoT")
            mwt, mwt_v, t_mwt = load_f("mem_WT")
            wit, wit_v, t_wit = load_f("WiT")
            mw, mw_v, t_mw = load_f("mem_W")
            wg2, wg2_v, t_wg2 = load_f("Wg2T")
            wg1, wg1_v, t_wg1 = load_f("Wg1T")
            a, b = split(wg1_h, wg1_l, wg1_v, t_wg1)
            ft.give(wg1, a, b)
            wg1_t = b
            rep = ft.take()
            for c in range(2):
                a = ve.tensor_copy(rep.ap[:, c * 128:(c + 1) * 128], memb_c[:, c:c + 1].to_broadcast([128, 128]),
                    w=(w_small, *rep.last))
            ps = units.take()
            for c in range(2):
                t = pe.matmul(ps.ap[:, 0:256], rep.ap[:, c * 128:(c + 1) * 128], wo_v[:, c, :], start=c == 0,
                    stop=c == 1, w=(a, t_wo, *ps.last))
            for oc in range(2):
                for c in range(2):
                    t = pe.matmul(ps.ap[:, 512 + oc:513 + oc], wo_v[:, c, oc * 128:oc * 128 + 128], memb_c[:,
                        c:c + 1], start=c == 0, stop=c == 1)
            cb = ve.tensor_tensor(bias_mg[:, 0:256], ps.ap[:, 0:256], bo_r, ALU.add, w=(t,))
            b = ve.tensor_tensor(cols[:, 26:28], ps.ap[:, 512:514], bo_c, ALU.add, w=(cb,))
            for c in range(2):
                d = ve.tensor_copy(rep.ap[:, 256 + c * 128:256 + (c + 1) * 128], cols[:,
                    26 + c:27 + c].to_broadcast([128, 128]), w=(b,))
            units.give(ps, b)
            ps = units.take()
            for c in range(2):
                t = pe.matmul(ps.ap[:, 0:256], rep.ap[:, 256 + c * 128:256 + (c + 1) * 128], wg2_v[:, c, :],
                    start=c == 0, stop=c == 1, w=(d, t_wg2, *ps.last))
            bg = ve.tensor_tensor(bias_mg[:, 256:512], ps.ap[:, 0:256], bg_r, ALU.add, w=(t,))
            units.give(ps, bg)
            ft.give(rep, t)
            a = ve.tensor_scalar(cols[:, 28:29], cols[:, 22:23], -1.0, 1.0, ALU.mult, ALU.add, w=(w_small,))
            sc = ve.tensor_scalar(cols[:, 29:30], cols[:, 23:24], 2.0 / (N_MEM * 256), None, ALU.mult)
            mws = ve.tensor_scalar(mw_v, mw_v, cols[:, 28:29], None, ALU.mult, w=(a, t_mw))
            p8 = ve.tensor_scalar(hsum[:, :, 17:18], hsum[:, :, 16:17], 8.0, None, ALU.mult, w=(pt,))
            hs = ve.tensor_reduce(cols[:, 30:32], hsum[:, :, 0:16], AX.X, ALU.add, w=(hs_done[0],))
            hs = ve.tensor_tensor(cols[:, 32:34], cols[:, 30:32], hsum[:, :, 17], ALU.add, w=(hs, p8))
            r0 = ve.tensor_tensor(mb_row[0:1, 0:256], mb_row[0:1, 0:256], mb_row[0:1, 256:512], ALU.subtract,
                w=(w_small,))
            gs = ft.take()
            ga = act.activation(gs.ap, gram.ap, ACT.Copy, w=(first_done[G - 1], *gs.last))
            units.give(gram, ga)
            ps = units.take()
            for c in range(2):
                t = pe.matmul(ps.ap[0:1, c * 128:c * 128 + 128], cols[:, 32 + c:33 + c], ident[:, :], start=True,
                    stop=True, w=(hs, *ps.last))
            hr = ve.tensor_copy(mb_row[0:1, 256:512], ps.ap[0:1, 0:256], w=(t, r0))
            for c in range(2):
                for q in range(2):
                    t = pe.transpose(ps.ap[:, 512 + q * 256 + c * 128:512 + q * 256 + c * 128 + 128], gs.ap[:,
                        c * 512 + 256 + q * 128:c * 512 + 256 + q * 128 + 128], ident[:, :], w=(ga,))
            g2 = ft.take()
            gt = ve.tensor_scalar(g2.ap[:, 0:512], ps.ap[:, 512:1024], -1.0, None, ALU.mult, w=(t, *g2.last))
            units.give(ps, gt, hr)
            g2v = v3(g2.ap[:, 0:512], 2, 256)
            gsv = v3(gs.ap, 2, 512)
            ps = units.take()
            for m in range(2):
                o = ps.ap[:, m * 512:m * 512 + 256]
                for c in range(2):
                    pe.matmul(o, mwt_v[:, c, m * 128:m * 128 + 128], gsv[:, c, 0:256], start=c == 0, stop=False,
                        w=(ga, t_mwt, *ps.last))
                for c in range(2):
                    pe.matmul(o, wit_v[:, c, m * 128:m * 128 + 128], g2v[:, c, :], start=False, stop=False, w=(gt,
                        t_wit))
                t = pe.matmul(o, mb_row[0:1, m * 128:m * 128 + 128], mb_row[0:1, 256:512], start=False, stop=True,
                    w=(hr, r0))
            wn = ve.scalar_tensor_tensor(mw_v, two(ps.ap), cols[:, 29:30], mw_v, ALU.mult, ALU.add, w=(t, sc, mws))
            units.give(ps, wn)
            for q in (mwt, wit, gs, g2):
                ft.give(q, t)
            ps, ps2 = units.take(), units.take()
            t = mm256(ps.ap, wo_v, mw_v, (wn, t_wo, *ps.last))
            t2 = mm256(ps2.ap, mw_v, wo_v, (wn, *ps2.last))
            a1 = ft.take()
            a1v = v3(a1.ap[:, 0:512], 2, 256)
            b1 = act.activation(a1v, two(ps.ap), ACT.Copy, w=(t, *a1.last))
            units.give(ps, b1)
            ea, eb = evac(a12_h[:, :, 0:256], a12_l[:, :, 0:256], two(ps2.ap), t2)
            units.give(ps2, ea, eb)
            ft.give(mw, t2)
            ft.give(wo, t2)
            ps = units.take()
            t = mm256(ps.ap, a1v, wg2_v, (b1, t_wg2, *ps.last))
            fa, fb = evac(a12_h[:, :, 256:512], a12_l[:, :, 256:512], two(ps.ap), t)
            units.give(ps, fa, fb)
            ft.give(a1, t)
            ft.give(wg2, t)
            return (eb, fb, wg1_t), bg

        bias_mg = rows[:, 10:12, :].rearrange("p a b -> p (a b)")
        hs_done = [Token(act, len(act.ops) - 1)]
        A12_t, bmg_t = middle()
        WA = ff_weights(0, io["W1T"], io["W2T"])

        last_group = {}

        def load_h(g):
            hh, hl = rt.take(), rt.take()
            t1 = dma(sp, rt_sem[id(hh)], f32(hh.ap), f32(d_h[g, :, 0, :]), w=(*hh.last, hstore[g][0]))
            t2 = dma(sp, rt_sem[id(hl)], f32(hl.ap), f32(d_h[g, :, 1, :]), w=(*hl.last, hstore[g][1]))
            return hh, hl, t1, t2

        def affine(x, gr, br, *w):
            a = po.tensor_tensor(x, x, gr.unsqueeze(1).to_broadcast([128, 4, 256]), ALU.mult, w=(*w,))
            return po.tensor_tensor(x, x, br.unsqueeze(1).to_broadcast([128, 4, 256]), ALU.add, w=(a,))

        def layernorm(dst, x, *w):
            s = sm.take()
            mv = v3(s.ap[:, 0:8], 4, 2)
            t, _ = stats(x, mv, *w, *s.last)
            r = rsqrt(s.ap[:, 12:16], mv[:, :, 1], s.ap[:, 8:12], t)
            t = norm(dst, x, mv[:, :, 0], s.ap[:, 12:16], r)
            return t, s

        def second(g):
            x, ld = load_x(io["x"], g)
            yield
            c4 = slice(4 * g, 4 * g + 4)
            xv = v3(x.ap, 4, 256)
            xl = ft.take()
            xlv = v3(xl.ap, 4, 256)
            tx = norm(xlv, xv, mean[:, c4], rstd[:, c4], ld, *xl.last)
            th = ve.tensor_copy(halo[:, 0, :], halo[:, 4, :], w=(*halo_free,)) if g % 2 else None
            th = ve.tensor_copy(halo[:, 1:5, :], xlv[96:128, :, :], w=(tx, *halo_free, *([th] if th else [])))
            yield
            ps = units.take()
            t = transposes(ps.ap, xlv, tx, *ps.last)
            xT = ft.take()
            ta = act.activation(xT.ap, ps.ap, ACT.Copy, w=(t, *xT.last))
            units.give(ps, ta)
            yield
            ps = units.take()
            for i in range(4):
                for part in range(2):
                    for c in range(2):
                        q = xT.ap[:, c * 512 + i * 128:c * 512 + i * 128 + 128]
                        if part:
                            k = q
                        elif i:
                            k = xT.ap[:, c * 512 + i * 128 - 32:c * 512 + i * 128]
                        elif g % 2:
                            k = last_group["xT"].ap[:, c * 512 + 480:c * 512 + 512]
                        else:
                            k = xT.ap[:, c * 512:c * 512 + 32]
                        o = ps.ap[:, i * 256 + 32 * part:i * 256 + (160 if part else 32)]
                        t = pe.matmul(o, q, k, start=c == 0 and part == 0 and i % 2 == 0, stop=c == 1,
                            skip_group_check=True, w=(ta, *ps.last))
            if g % 2:
                ft.give(last_group["xT"], t)
                ft.give(xT, t)
            else:
                last_group["xT"] = xT
            sc = ft.take()
            scv = v3(sc.ap[:, 0:640], 4, 160)
            psv = v3(ps.ap, 4, 256)[:, :, 0:160]
            s = sm.take()
            n0 = 0 if g % 2 else 1
            if n0:
                a = ve.tensor_tensor(scv[:, 0, :], psv[:, 0, :], mask[:, 1, :], ALU.add, w=(t, C["mask"], *sc.last))
            a = ve.tensor_tensor(scv[:, n0:4, :], psv[:, n0:4, :], mask[:, 0, :].unsqueeze(1).to_broadcast([128,
                4 - n0, 160]), ALU.add, w=(t, C["mask"], *sc.last))
            units.give(ps, a)
            b = ve.tensor_reduce(s.ap[:, 0:4], scv, AX.X, ALU.max, w=(a, *s.last))
            b = ve.tensor_scalar(s.ap[:, 4:8], s.ap[:, 0:4], -1.0 / 16.0, None, ALU.mult, w=(b,))
            for i in range(4):
                ex = act.activation(scv[:, i, :], scv[:, i, :], ACT.Exp, bias=s.ap[:, 4 + i:5 + i], scale=1.0 / 16.0,
                    accum_out=s.ap[:, 8 + i:9 + i], w=(b,))
            ri = ve.reciprocal(s.ap[:, 12:16], s.ap[:, 8:12], w=(ex,))
            yield
            ps = units.take()
            for i in range(4):
                t = pe.transpose(ps.ap[:, i * 128:(i + 1) * 128], scv[:, i, 32:160], ident[:, :], w=(ex, *ps.last))
                t = pe.transpose(ps.ap[0:32, 512 + i * 128:512 + (i + 1) * 128], scv[:, i, 0:32], ident[:, :])
            ft.give(sc, t)
            pT = ft.take()
            ta = act.activation(pT.ap[:, 0:512], ps.ap[:, 0:512], ACT.Copy, w=(t, *pT.last))
            tb = act.activation(pT.ap[0:32, 512:1024], ps.ap[0:32, 512:1024], ACT.Copy)
            units.give(ps, tb)
            yield
            ps = units.take()
            for i in range(4):
                o = ps.ap[:, i * 256:(i + 1) * 256]
                first_of_batch = i == 0 and g % 2 == 0
                pe.matmul(o, pT.ap[:, i * 128:(i + 1) * 128], xlv[:, i, :], start=i % 2 == 0, stop=first_of_batch,
                    skip_group_check=True, w=(ta, tb, *ps.last))
                if not first_of_batch:
                    before = halo[:, i, :]
                    t = pe.matmul(o, pT.ap[0:32, 512 + i * 128:512 + (i + 1) * 128], before, start=False, stop=True,
                        skip_group_check=True, w=(th,))
            halo_free[:] = [t]
            ft.give(pT, t)
            for i in range(4):
                a = ve.scalar_tensor_tensor(xlv[:, i, :], ps.ap[:, i * 256:(i + 1) * 256], s.ap[:, 12 + i:13 + i],
                    xlv[:, i, :], ALU.mult, ALU.add, w=(t, ri))
            units.give(ps, a)
            sm.give(s, a)
            t, s = layernorm(xlv, xlv, a)
            sm.give(s, t)
            x1 = xl
            x1v = xlv
            t1 = affine(x1v, g1_r, be1_r, t, w_small)
            hh, hl, th1, th2 = load_h(g)
            yield
            ps = units.take()
            t = transposes(ps.ap, x1v, t1, *ps.last)
            x1h, x1l = rt.take(), rt.take()
            a, b = evac(x1h.ap, x1l.ap, ps.ap, t, *x1h.last, *x1l.last)
            units.give(ps, a, b)
            yield
            mg = [ft.take(), ft.take()]
            for k in range(2):
                ps = units.take()
                for i in (2 * k, 2 * k + 1):
                    q = slice((i % 2) * 512, (i % 2) * 512 + 512)
                    three(ps.ap[:, q], [(hh.ap[:, c * 512 + i * 128:c * 512 + i * 128 + 128],
                                         hl.ap[:, c * 512 + i * 128:c * 512 + i * 128 + 128],
                                         a12_h[:, c, :], a12_l[:, c, :]) for c in range(2)], True, False,
                          (th1, th2, *A12_t, *ps.last))
                    q = slice((i % 2) * 512 + 256, (i % 2) * 512 + 512)
                    t = three(ps.ap[:, q], [(x1h.ap[:, c * 512 + i * 128:c * 512 + i * 128 + 128],
                                             x1l.ap[:, c * 512 + i * 128:c * 512 + i * 128 + 128],
                                             wg1_h[:, c, :], wg1_l[:, c, :]) for c in range(2)], False, True, (a, b))
                pv = v3(ps.ap, 2, 512)
                for n in range(2):
                    d = v3(mg[n].ap, 4, 256)[:, 2 * k:2 * k + 2, :]
                    m = ve.tensor_tensor(d, pv[:, :, n * 256:n * 256 + 256], bias_mg[:,
                        n * 256:n * 256 + 256].unsqueeze(1).to_broadcast([128, 2, 256]), ALU.add, w=(t, bmg_t,
                            *mg[n].last))
                units.give(ps, m)
            for q in (hh, hl, x1h, x1l):
                rt.give(q, t)
            mo, gt = mg
            th = act.activation(gt.ap, gt.ap, ACT.Tanh, scale=0.5, w=(m,))
            d = ft.take()
            td = po.tensor_tensor(d.ap, x1.ap, mo.ap, ALU.subtract, w=(m, *d.last))
            ts = po.tensor_tensor(mo.ap, x1.ap, mo.ap, ALU.add, w=(td,))
            ft.give(x1, ts)
            u = ve.scalar_tensor_tensor(d.ap, gt.ap, 1.0, d.ap, ALU.add, ALU.mult, w=(th, td))
            ft.give(gt, u)
            r = ve.scalar_tensor_tensor(mo.ap, d.ap, 0.5, mo.ap, ALU.mult, ALU.add, w=(u, ts))
            ft.give(d, r)
            x2 = mo
            x2v = v3(x2.ap, 4, 256)
            t, s = layernorm(x2v, x2v, r)
            sm.give(s, t)
            t2 = affine(x2v, g2_r, be2_r, t)
            yield
            ps = units.take()
            t = transposes(ps.ap, x2v, t2, *ps.last)
            x2h, x2l = rt.take(), rt.take()
            a, b = evac(x2h.ap, x2l.ap, ps.ap, t, *x2h.last, *x2l.last)
            units.give(ps, a, b)
            tb = po.tensor_tensor(x2v, x2v, b2_r.unsqueeze(1).to_broadcast([128, 4, 256]), ALU.add, w=(t,))
            yield
            done = {}
            yield from ff(x2h.ap, x2l.ap, WA, ACT.Silu, b1_c, done, a, b)
            rt.give(x2h, done["x"])
            rt.give(x2l, done["x"])
            o = done["o"]
            r = ve.tensor_tensor(x2.ap, x2.ap, o.ap, ALU.add, w=(done["t"], tb))
            units.give(o, r)
            ff_done[g] = done["t"]
            t, s = layernorm(x2v, x2v, r)
            sm.give(s, t)
            t = affine(x2v, g3_r, be3_r, t)
            t, s = layernorm(x2v, x2v, t)
            sm.give(s, t)
            p = pay.take()
            pv = p.ap
            tn = ve.tensor_tensor(pv[:, :, 0:256], x2v, xv, ALU.add, w=(t, *p.last))
            ft.give(x2, tn)
            ft.give(x, tn)
            yield
            s = sm.take()
            mv = v3(s.ap[:, 0:8], 4, 2)
            t, _ = stats(pv[:, :, 0:256], mv, tn, *s.last)
            r = rsqrt(s.ap[:, 12:16], mv[:, :, 1], s.ap[:, 8:12], t)
            b = po.tensor_tensor(s.ap[:, 16:20], s.ap[:, 12:16], s.ap[:, 12:16], ALU.mult, w=(r,))
            b = po.tensor_tensor(s.ap[:, 20:24], s.ap[:, 16:20], mv[:, :, 1], ALU.mult, w=(b,))
            b = rsqrt(s.ap[:, 24:28], s.ap[:, 20:24], s.ap[:, 28:32], b)
            b = po.tensor_tensor(s.ap[:, 32:36], s.ap[:, 24:28], s.ap[:, 12:16], ALU.mult, w=(b,))
            t1 = ve.tensor_copy(pv[:, :, 256], mv[:, :, 0], w=(t,))
            t2 = ve.tensor_copy(pv[:, :, 257], s.ap[:, 12:16], w=(r,))
            t3 = ve.tensor_copy(pv[:, :, 258], s.ap[:, 32:36], w=(b,))
            t4 = ve.tensor_copy(pv[:, :, 260].bitcast(U), ids[:, c4].bitcast(U), w=(C["pool"],))
            t4 = ve.memset(pv[:, :, 261:264], 0.0)
            tk = ft.take()
            tkv = v3(tk.ap, 4, 256)
            t = norm(tkv, pv[:, :, 0:256], mv[:, :, 0], s.ap[:, 32:36], b, *tk.last)
            df = ft.take()
            tq = ve.tensor_tensor(df.ap, pv[:, :, 0:256], tkv, ALU.add, w=(t, *df.last))
            od = dma(sp, ft_sem[id(df)], tok_rows(d_x1, g), v3(df.ap, 4, 256), w=(tq,), store=True)
            ft.give(df, od)
            sm.give(s, t, t2, t3)
            x1_default.append(od)
            yield
            ps = units.take()
            tt = transposes(ps.ap, tkv, t, *ps.last)
            ft.give(tk, tt, tq)
            tT = ft.take()
            for c in range(2):
                ta = act.activation(tT.ap[:, c * 512:(c + 1) * 512], ps.ap[:, c * 512:(c + 1) * 512], ACT.Identity,
                    scale=lng_c[:, c:c + 1], bias=lnb_c[:, c:c + 1], w=(tt, *tT.last))
            units.give(ps, ta)
            yield
            s = sm.take()
            su = s.ap[:, 0:4].bitcast(U)
            lx, t_s, t_w = yield from route(0, 512, tT.ap, gwT, su, pv[:, :, 259], ta, *s.last)
            ft.give(tT, lx)
            for i in range(4):
                tz = scatter(scat_sem[id(p)], d_p1, su[:, i:i + 1], pv[:, i, :], E * 512 - 1, w=(t_s, t_w, t1, t2, t3,
                    t4, filled))
            pay.give(p, tz)
            sm.give(s, tz)
            sent[0].append(tz)

        halo = sb("halo", [32, 5, 256])
        halo_free = []
        ff_done = {}
        x1_default = []
        run([second(g) for g in range(G if stop != "A1" else 1)], 11)

        for b in borrowed:
            rt.idle.remove(b)

        def job(e_, i, cap, src, ready, WF, func, bias, dst, gate_only):
            p = pay.take()
            pv = p.ap
            r0 = e_ * cap + i * 512
            ld = dma(sp, pay_sem[id(p)], pv, src[r0:r0 + 512, :].rearrange("(t p) n -> p t n", p=128), w=(*p.last,
                *ready))
            yield
            tk = ft.take()
            tkv = v3(tk.ap, 4, 256)
            sc = 258 if not gate_only else 257
            for k in range(4):
                t = ve.tensor_scalar(tkv[:, k, :], pv[:, k, 0:256], pv[:, k, 256:257], pv[:, k, sc:sc + 1],
                    ALU.subtract, ALU.mult, w=(ld, *tk.last))
            ps = units.take()
            t = transposes(ps.ap, tkv, t, *ps.last)
            ft.give(tk, t)
            th, tl = rt.take(), rt.take()
            if gate_only:
                a, b = evac(th.ap, tl.ap, ps.ap, t, *th.last, *tl.last)
                units.give(ps, a, b)
            else:
                f = ft.take()
                for d in (f, th):
                    for c in range(2):
                        a = act.activation(d.ap[:, c * 512:(c + 1) * 512], ps.ap[:, c * 512:(c + 1) * 512],
                            ACT.Identity, scale=lng_c[:, c:c + 1], bias=lnb_c[:, c:c + 1], w=(t, *d.last))
                units.give(ps, a)
                b = ve.tensor_tensor(tl.ap, f.ap, f32(th.ap), ALU.subtract, w=(a, *tl.last))
                ft.give(f, b)
            yield
            W = WF()
            done = {}
            yield from ff(th.ap, tl.ap, W, func, bias, done, a, b)
            rt.give(th, done["x"])
            rt.give(tl, done["x"])
            o = done["o"]
            job_done[(cap, e_, i)] = done["t"]
            q = ft.take()
            qv = v3(q.ap, 4, 256)
            s = sm.take()
            mv = v3(s.ap[:, 0:8], 4, 2)
            if gate_only:
                t = ve.tensor_tensor(qv, v3(o.ap, 4, 256), W["b2"].unsqueeze(1).to_broadcast([128, 4, 256]), ALU.add,
                    w=(done["t"], W["tb2"], *q.last))
                units.give(o, t)
                W["free_b2"].last = [t]
                t, _ = stats(qv, mv, t, *s.last)
                gt = pv[:, :, 259]
                b = po.tensor_tensor(s.ap[:, 16:20], gt, gt, ALU.mult, w=(ld,))
                b = po.tensor_tensor(s.ap[:, 20:24], s.ap[:, 16:20], mv[:, :, 1], ALU.mult, w=(b, t))
                b = rsqrt(s.ap[:, 24:28], s.ap[:, 20:24], s.ap[:, 28:32], b)
                b = po.tensor_tensor(s.ap[:, 12:16], s.ap[:, 24:28], gt, ALU.mult, w=(b,))
            else:
                for k in range(4):
                    t = ve.tensor_scalar(qv[:, k, :], pv[:, k, 0:256], pv[:, k, 256:257], pv[:, k, 257:258],
                        ALU.subtract, ALU.mult, w=(*q.last,))
                for k in range(4):
                    t = ve.scalar_tensor_tensor(qv[:, k, :], o.ap[:, k * 256:(k + 1) * 256], pv[:, k, 259:260], qv[:,
                        k, :], ALU.mult, ALU.add, w=(done["t"], t))
                units.give(o, t)
                t, _ = stats(qv, mv, t, *s.last)
                b = rsqrt(s.ap[:, 12:16], mv[:, :, 1], s.ap[:, 8:12], t)
            t = norm(qv, qv, mv[:, :, 0], s.ap[:, 12:16], b)
            sm.give(s, t)
            t = ve.tensor_tensor(qv, qv, pv[:, :, 0:256], ALU.add, w=(t,))
            yield
            s = sm.take()
            su = s.ap[:, 0:4].bitcast(U)
            tn = ve.tensor_copy(su, pv[:, :, 260].bitcast(U), w=(ld, *s.last))
            pay.give(p, t, tn)
            for k in range(4):
                z = scatter(scat_sem[id(q)], dst, su[:, k:k + 1], qv[:, k, :], T - 1, w=(t, tn, *defaults[cap]))
            ft.give(q, z)
            sm.give(s, z)
            defaults[(cap, "last")].append(z)

        job_done = {}
        defaults = {512: list(x1_default), (512, "last"): [], (1024, "last"): []}

        def experts0():
            Ws = {}

            def prefetch(n):
                if n < E:
                    w = (ff_done[G - 1],) if n == 1 else ((job_done[(512, n - 2, 0)],) if n > 1 else ())
                    Ws[n] = ff_weights((n + 1) % 2, io["wi"][n], io["wo"][n], *w,
                                       w2_waits=[x for b in borrowed for x in b.last] if n == 0 else ())

            def one(n):
                gen = job(n, 0, 512, d_p1, sent[0], lambda: Ws[n], ACT.Gelu, None, d_x1, False)
                next(gen)
                if n == 0:
                    prefetch(0)
                    prefetch(1)
                yield
                yield from gen
                prefetch(n + 2)

            return [one(n) for n in range(E)]

        if stop != "A":
            run(experts0(), 9)

        wq_h, wq_l = v3(small[:, 0:1536], 2, 768), v3(small[:, 1536:3072], 2, 768)
        kw = [(v3(small[:, 3072 + i * 1032:3072 + i * 1032 + 516], 2, 258),
               v3(small[:, 3072 + i * 1032 + 516:3072 + (i + 1) * 1032], 2, 258)) for i in range(2)]
        kw_t = [[], []]

        def layer1():
            st = stage.take()
            ld = dma(sp, stage_sem[id(st)], v3(st.ap[:, 0:1536], 2, 768), chunks(io["WqkvT"], 768), w=(*st.last,))
            a, b = split(small[:, 0:1536], small[:, 1536:3072], st.ap[:, 0:1536], ld)
            stage.give(st, a, b)
            wout, wout_v, t_wout = load_f("WoutT")
            return b, wout, wout_v, t_wout

        qstate = {}

        def attn1(bt):
            grp = []
            kvps = None
            for j in range(2):
                g = 2 * bt + j
                x, ld = load_x(d_x1, g, *defaults[(512, "last")])
                xv = v3(x.ap, 4, 256)
                yield
                xn = ft.take()
                t, s = layernorm(v3(xn.ap, 4, 256), xv, ld)
                sm.give(s, t)
                ps = units.take()
                t = transposes(ps.ap, v3(xn.ap, 4, 256), t, *ps.last)
                ft.give(xn, t)
                xh, xl = rt.take(), rt.take()
                a, b = evac(xh.ap, xl.ap, ps.ap, t, *xh.last, *xl.last)
                units.give(ps, a, b)
                yield
                ps = units.take()
                for oc in range(2):
                    t = wide(ps.ap[:, oc * 512:(oc + 1) * 512], wq_h, wq_l, xh.ap, xl.ap, 512, (a, b, wq_t, *ps.last),
                        oc)
                q, qh, ql = ft.take(), rt.take(), rt.take()
                tq = ve.tensor_scalar(q.ap, ps.ap, 0.0, 1e-6, ALU.max, ALU.add, w=(t, *q.last))
                units.give(ps, tq)
                q1, q2 = split(qh.ap, ql.ap, q.ap, tq, *qh.last, *ql.last, engine="p")
                ft.give(q, q1, q2)
                grp.append((x, xv, qh, ql, q1, q2))
                yield
                for k in range(2):
                    ps = units.take()
                    for i in (2 * k, 2 * k + 1):
                        t = three(ps.ap[:, (i % 2) * 512:(i % 2) * 512 + 512],
                                  [(xh.ap[:, c * 512 + i * 128:c * 512 + i * 128 + 128],
                                    xl.ap[:, c * 512 + i * 128:c * 512 + i * 128 + 128],
                                    wq_h[:, c, 256:768], wq_l[:, c, 256:768]) for c in range(2)], True, True,
                                  (*ps.last,))
                    if k == 1:
                        rt.give(xh, t)
                        rt.give(xl, t)
                    f, fh, fl = ft.take(), rt.take(), rt.take()
                    pv, fv, hv, lv = (v3(z.ap, 2, 512) for z in (ps, f, fh, fl))
                    t1 = ve.tensor_scalar(fv[:, :, 0:256], pv[:, :, 0:256], 0.0, 1e-6, ALU.max, ALU.add, w=(t, *f.last))
                    t2 = act.activation(fv[:, :, 256:512], pv[:, :, 256:512], ACT.Copy, w=(t1,))
                    units.give(ps, t1, t2)
                    a1, b1 = split(fh.ap, fl.ap, f.ap, t1, t2, *fh.last, *fl.last, engine="pv"[k])
                    ft.give(f, a1, b1)
                    yield
                    if kvps is None:
                        kvps = units.take()
                    for i in range(2):
                        st0 = j == 0 and k == 0 and i == 0
                        last = j == 1 and k == 1 and i == 1
                        for c in range(2):
                            vh, vl = (z[:, i, 256 + c * 128:256 + c * 128 + 128] for z in (hv, lv))
                            three(kvps.ap[:, c * 256:(c + 1) * 256], [(vh, vl, hv[:, i, 0:256], lv[:, i, 0:256])],
                                  st0 and c == 0, last, (a1, b1, *kvps.last))
                        for c in range(2):
                            kh_, kl_ = (z[:, i, c * 128:c * 128 + 128] for z in (hv, lv))
                            o = kvps.ap[:, 512 + 2 * c:514 + 2 * c]
                            pe.matmul(o, kh_, oner[:, :], start=st0 and c == 0, stop=False, skip_group_check=True,
                                w=(C["oner"],))
                            t = pe.matmul(o, kl_, oner[:, :], start=False, stop=last, skip_group_check=True)
                    rt.give(fh, t)
                    rt.give(fl, t)
            yield
            kvf = ft.take()
            kt = act.activation(kvf.ap[:, 0:512], kvps.ap[:, 0:512], ACT.Copy, w=(t, *kvf.last))
            kt2 = act.activation(kvf.ap[:, 512:516], kvps.ap[:, 512:516], ACT.Copy)
            units.give(kvps, kt2)
            ps = units.take()
            t = mm256(ps.ap, v3(kvf.ap[:, 0:512], 2, 256), wout_v, (kt, t_wout, *ps.last))
            kh, kl = kw[bt % 2]
            a, b = evac(kh[:, :, 0:256], kl[:, :, 0:256], two(ps.ap), t, *kw_t[bt % 2])
            units.give(ps, a, b)
            kc = v3(kvf.ap[:, 512:516], 2, 2)
            a2, b2 = split(kh[:, :, 256:258], kl[:, :, 256:258], kc, kt2)
            ft.give(kvf, a2, b2, t)
            yield
            for j in range(2):
                g = 2 * bt + j
                x, xv, qh, ql, q1, q2 = grp[j]
                r = ft.take()
                rv = v3(r.ap, 4, 256)
                s = sm.take()
                for k in range(2):
                    ps = units.take()
                    for i in (2 * k, 2 * k + 1):
                        t = three(ps.ap[:, (i % 2) * 512:(i % 2) * 512 + 258],
                                  [(qh.ap[:, c * 512 + i * 128:c * 512 + i * 128 + 128],
                                    ql.ap[:, c * 512 + i * 128:c * 512 + i * 128 + 128],
                                    kh[:, c, :], kl[:, c, :]) for c in range(2)], True, True,
                                  (q1, q2, a, b, a2, b2, *ps.last))
                    pv = v3(ps.ap, 2, 512)
                    z0 = s.ap[:, 4 * k:4 * k + 2]
                    z1 = s.ap[:, 4 * k + 2:4 * k + 4]
                    d = ve.tensor_scalar(z0, pv[:, :, 256], 1e-6, None, ALU.add, w=(t, *s.last))
                    d = ve.reciprocal(z1, z0, w=(d,))
                    for i in range(2):
                        m = ve.scalar_tensor_tensor(rv[:, 2 * k + i, :], pv[:, i, 0:256], z1[:, i:i + 1], bout_r,
                            ALU.mult, ALU.add, w=(d, w_small, *r.last))
                    units.give(ps, m)
                rt.give(qh, t)
                rt.give(ql, t)
                sm.give(s, m)
                if j == 1:
                    kw_t[bt % 2] = [t]
                yield
                t, s = layernorm(rv, rv, m)
                sm.give(s, t)
                p = pay.take()
                pv = p.ap
                tn = ve.tensor_tensor(pv[:, :, 0:256], rv, xv, ALU.add, w=(t, *p.last))
                ft.give(r, tn)
                ft.give(x, tn)
                od = dma(sp, out_sem[id(p)], tok_rows(out, g), pv[:, :, 0:256], w=(tn,), store=True)
                out_default.append(od)
                s = sm.take()
                mv = v3(s.ap[:, 0:8], 4, 2)
                t, _ = stats(pv[:, :, 0:256], mv, tn, *s.last)
                rr = rsqrt(s.ap[:, 12:16], mv[:, :, 1], s.ap[:, 8:12], t)
                c4 = slice(4 * g, 4 * g + 4)
                t1 = ve.tensor_copy(pv[:, :, 256], mv[:, :, 0], w=(t,))
                t4 = ve.tensor_copy(pv[:, :, 260].bitcast(U), ids[:, c4].bitcast(U))
                t4 = ve.memset(pv[:, :, 261:264], 0.0)
                t4 = ve.memset(pv[:, :, 258], 0.0)
                t2 = ve.tensor_copy(pv[:, :, 257], s.ap[:, 12:16], w=(rr,))
                xn = ft.take()
                t = norm(v3(xn.ap, 4, 256), pv[:, :, 0:256], mv[:, :, 0], s.ap[:, 12:16], rr, *xn.last)
                sm.give(s, t, t2)
                yield
                ps = units.take()
                tt = transposes(ps.ap, v3(xn.ap, 4, 256), t, *ps.last)
                ft.give(xn, tt)
                tT = ft.take()
                ta = act.activation(tT.ap, ps.ap, ACT.Copy, w=(tt, *tT.last))
                units.give(ps, ta)
                yield
                s = sm.take()
                su = s.ap[:, 0:4].bitcast(U)
                lx, t_s, t_w = yield from route(1, 1024, tT.ap, wgT, su, pv[:, :, 259], ta, *s.last)
                ft.give(tT, lx)
                for i in range(4):
                    tz = scatter(scat_sem[id(p)], d_p2, su[:, i:i + 1], pv[:, i, :], E * 1024 - 1, w=(t_s, t_w, t1,
                        t2, t4))
                pay.give(p, tz, od)
                sm.give(s, tz)
                sent[1].append(tz)

        out_default = []
        if stop not in ("A", "A1", "B"):
            wq_t, wout, wout_v, t_wout = layer1()
            for b in borrowed:
                b.last = [job_done[(512, 6, 0)]]
            rt.idle += borrowed
            run([attn1(bt) for bt in range(8)], 17)
            for b in borrowed:
                rt.idle.remove(b)
            ft.give(wout, *[])
            defaults[1024] = list(out_default)
            b1e = sb("b1e", [128, 64])
            b1e_t = dma(sp, s_b1, b1e[:, :], io["eb1_c"])
            b2e = [Tile(rows[:, i, :], "b2e") for i in range(2)]
            s_b2 = [new_sem(f"s_b2{i}") for i in range(2)]

            def experts1():
                Ws = {}

                def prefetch(n):
                    if n >= E:
                        return
                    w = (job_done[(1024, n - 2, 1)],) if n > 1 else (job_done[(512, 6 + n, 0)],)
                    W = ff_weights((n + 1) % 2, io["w1"][n], io["w2"][n], *w,
                                   w2_waits=[x for b in borrowed for x in b.last] if n == 0 else ())
                    bt = b2e[n % 2]
                    W["b2"], W["free_b2"] = bt.ap, bt
                    W["tb2"] = dma(sp, s_b2[n % 2], bt.ap, io["eb2"][n].partition_broadcast(128), w=(*bt.last, *w))
                    Ws[n] = W

                def one(n, i):
                    gen = job(n, i, 1024, d_p2, sent[1], lambda: Ws[n], ACT.Relu,
                              b1e[:, 8 * n:8 * n + 8], out, True)
                    next(gen)
                    if n == 0 and i == 0:
                        prefetch(0)
                        prefetch(1)
                    yield
                    yield from gen
                    if i == 1:
                        prefetch(n + 2)

                return [one(n, i) for n in range(E) for i in range(2)]

            act.activation(cols[:, 61:62], cols[:, 60:61], ACT.Copy, w=(b1e_t,))
            run(experts1(), 9)

        if stop:
            t = dma(sp, s_b1, out, d_x1, w=(*stores,), store=True)

        for q in (pe, act, ve, po, sp):
            q.number()
        block = ctx.enter_context(nc.Block())

        @block.tensor
        def _(eng):
            pe.write(eng)

        @block.scalar
        def _(eng):
            act.write(eng)

        @block.vector
        def _(eng):
            ve.write(eng)

        @block.gpsimd
        def _(eng):
            po.write(eng)

        @block.sync
        def _(eng):
            sp.write(eng)
            for sem in {id(t.sem): t.sem for t in stores}.values():
                eng.wait_ge(sem, landed[id(sem)])


def layouts(i):
    import numpy as np

    def t(a):
        return np.ascontiguousarray(np.asarray(a).T)

    def c(a):
        return np.ascontiguousarray(np.asarray(a).reshape(-1, 128).T)

    a = {k[8:]: np.asarray(v) for k, v in i.items() if k.startswith("L0_attn_")}
    f = {k[7:]: np.asarray(v) for k, v in i.items() if k.startswith("L0_ffn_")}
    q = {k[8:]: np.asarray(v) for k, v in i.items() if k.startswith("L1_attn_")}
    e = {k[7:]: np.asarray(v) for k, v in i.items() if k.startswith("L1_ffn_")}
    wg = t(a["Wg"])
    return {
        "x": a["x"].reshape(8192, 256), "P": a["P"], "mem_b": a["mem_b"], "bi": a["bi"],
        "mem_b_c": c(a["mem_b"]), "bi_c": c(a["bi"]), "bl1_c": c(a["bl1"]), "bl2_c": c(a["bl2"]), "bo_c": c(a["bo"]),
        "b1_c": c(a["b1"]), "ln_g_c": c(f["ln_gamma"]), "ln_b_c": c(f["ln_beta"]),
        "fgate": a["fgate"], "lrate": a["lrate"],
        "g1": a["g1"], "be1": a["be1"], "g2": a["g2"], "be2": a["be2"], "g3": a["g3"], "be3": a["be3"],
        "b2": a["b2"], "bo": a["bo"], "bg": a["bg"], "b_out": q["b_out"],
        "Wi": a["Wi"], "WiT": t(a["Wi"]), "Wl1T": t(a["Wl1"]), "Wl2T": t(a["Wl2"]), "WoT": t(a["Wo"]),
        "mem_W": a["mem_W"], "mem_WT": t(a["mem_W"]),
        "Wg1T": np.ascontiguousarray(wg[0:256]), "Wg2T": np.ascontiguousarray(wg[256:512]),
        "W1T": t(a["W1"]), "W2T": t(a["W2"]),
        "gate_wT": t(f["gate_weight"]), "wi": f["wi"], "wo": f["wo"],
        "WqkvT": t(q["W_qkv"]), "WoutT": t(q["W_out"]),
        "wg": e["wg"], "w1": e["w1"], "w2": e["w2"],
        "eb1_c": c(e["b1"]), "eb2": e["b2"],
    }


def kernel(**inputs):
    import numpy as np
    import concourse.bacc as bacc
    from concourse.bass_utils import run_bass_kernel_spmd

    nc = bacc.Bacc("TRN2", target_bir_lowering=False, num_devices=1)
    arrays, io = {}, {}
    for name, a in layouts(inputs).items():
        a = np.ascontiguousarray(a)
        arrays["in_" + name] = a
        io[name] = nc.dram_tensor("in_" + name, a.shape, mybir.dt.from_np(a.dtype), kind="ExternalInput").ap()
    io["out"] = nc.dram_tensor("out_x", (T, H), F, kind="ExternalOutput").ap()
    build(nc, io)
    r = run_bass_kernel_spmd(nc, [arrays], core_ids=[0])
    return r.results[0]["out_x"].reshape(8, 1024, 256)
```

```python
from contextlib import ExitStack

import concourse.bass as bass
from concourse import mybir

F = mybir.dt.float32
R = mybir.dt.float32r
BF = mybir.dt.bfloat16
U = mybir.dt.uint32
I = mybir.dt.int32
ALU = mybir.AluOpType
ACT = mybir.ActivationFunctionType
AX = mybir.AxisListType

T = 8192
H = 256
G = 16
E = 8
PW = 264
EPS = 1e-5
N_MEM = 8 * 1034
NEG = -1.0e30
FAR = 1.0e6


class Token:

    def __init__(self, queue, at):
        self.queue, self.at = queue, at

    def when(self):
        return self.queue.end[self.at]


class Landed:

    def __init__(self, sem, value, end):
        self.sem, self.value, self.end = sem, value, end

    def when(self):
        return self.end


def wide_of(ap):
    n = 1
    for k in ap.shape[1:]:
        n *= k
    return n


class Engine:

    def __init__(self, sem, per=1.0, fixed=60):
        self.sem, self.ops, self.marked = sem, [], set()
        self.per, self.fixed, self.clock, self.end = per, fixed, 0, []

    def put(self, fn, w, cost, sem=None):
        for t in w:
            if isinstance(t, Token):
                t.queue.marked.add(t.at)
        assert all(isinstance(t, (Token, Landed)) for t in w)
        self.ops.append((fn, w, sem))
        start = max([self.clock] + [t.when() + 60 for t in w])
        self.clock = start + cost
        self.end.append(self.clock)
        return Token(self, len(self.ops) - 1)

    def cost(self, out, k=1.0):
        return self.fixed + self.per * k * wide_of(out)

    def matmul(self, out, lhsT, rhs, w=(), **k):
        c = wide_of(out) * (0.42 if rhs.dtype != F else 1.68)
        return self.put(lambda e: e.matmul(out, lhsT, rhs, **k), w, c)

    def transpose(self, out, in_, identity, w=()):
        return self.put(lambda e: e.transpose(out, in_, identity), w, wide_of(out) * 0.84)

    def activation(self, out, in_, func, w=(), **k):
        return self.put(lambda e: e.activation(out, in_, func, **k), w, self.cost(out))

    def tensor_tensor(self, out, in0, in1, op, w=()):
        return self.put(lambda e: e.tensor_tensor(out, in0, in1, op), w, self.cost(out, 80 if op == ALU.pow else 1))

    def tensor_scalar(self, out, in0, s1, s2, op0, op1=ALU.bypass, w=()):
        return self.put(lambda e: e.tensor_scalar(out, in0, s1, s2, op0, op1), w, self.cost(out))

    def scalar_tensor_tensor(self, out, in0, s, in1, op0, op1, w=()):
        return self.put(lambda e: e.scalar_tensor_tensor(out, in0, s, in1, op0, op1), w, self.cost(out, 1.2))

    def tensor_reduce(self, out, in_, axis, op, w=()):
        return self.put(lambda e: e.tensor_reduce(out, in_, axis, op), w, self.cost(in_))

    def tensor_copy(self, out, in_, w=()):
        return self.put(lambda e: e.tensor_copy(out, in_), w, self.cost(out, 0.5))

    def reciprocal(self, out, in_, w=()):
        return self.put(lambda e: e.reciprocal(out, in_), w, self.cost(out))

    def memset(self, out, value, w=()):
        return self.put(lambda e: e.memset(out, value), w, self.cost(out, 0.5))

    def bn_stats(self, out, in_, w=()):
        return self.put(lambda e: e.bn_stats(out, in_), w, self.cost(in_))

    def bn_aggr(self, out, in_, w=()):
        return self.put(lambda e: e.bn_aggr(out, in_), w, 75)

    def iota(self, out, w=(), **k):
        return self.put(lambda e: e.iota(out, **k), w, self.cost(out))

    def affine_select(self, w=(), **k):
        return self.put(lambda e: e.affine_select(**k), w, 300)

    def number(self):
        self.count, n = [], 0
        for i in range(len(self.ops)):
            n += i in self.marked
            self.count.append(n)

    def write(self, eng):
        seen = {}
        for i, (fn, w, sem) in enumerate(self.ops):
            need = {}
            for t in w:
                s, v = (t.queue.sem, t.queue.count[t.at]) if isinstance(t, Token) else (t.sem, t.value)
                if v > max(seen.get(id(s), 0), need.get(id(s), (None, 0))[1]):
                    need[id(s)] = (s, v)
            for k, (s, v) in need.items():
                eng.wait_ge(s, v)
                seen[k] = v
            ins = fn(eng)
            if sem is not None:
                ins.then_inc(sem, 16)
            elif i in self.marked:
                ins.then_inc(self.sem, 1)


class Tile:

    def __init__(self, ap, name):
        self.ap, self.last, self.held, self.name = ap, [], False, name


class Store:

    def __init__(self, tiles):
        self.idle = list(tiles)
        self.name = tiles[0].name

    def take(self):
        assert self.idle, "no tile left: " + self.name
        t = self.idle.pop(0)
        t.held = True
        return t

    def give(self, t, *last):
        assert t.held
        t.held = False
        t.last = list(last)
        self.idle.append(t)

    def has(self, n=1):
        return lambda: len(self.idle) >= n


class Turn:

    def __init__(self, n):
        self.n = n

    def free(self):
        return self.n > 0

    def enter(self):
        assert self.n > 0
        self.n -= 1

    def leave(self):
        self.n += 1


def ready_at(y):
    if y is None:
        return 0
    return y.when() if isinstance(y, (Token, Landed)) else max(t.when() for t in y)


def run(gens, live_max, name=""):
    live, i = [], 0
    while live or i < len(gens):
        while i < len(gens) and len(live) < live_max:
            live.append([0, None, gens[i], i])
            i += 1
        able = [x for x in live if x[1] is None or x[1]()]
        assert able, "all wait: " + name
        x = min(able, key=lambda x: (x[0], x[3]))
        x[1] = None
        try:
            y = next(x[2])
            if callable(y):
                x[1] = y
            else:
                x[0] = ready_at(y)
        except StopIteration:
            live.remove(x)


def build(nc, io, stop=None):
    ctx = ExitStack()
    with ctx:
        def sb(name, shape, dt=F):
            return ctx.enter_context(nc.sbuf_tensor(name, shape, dt))

        def new_sem(name):
            return ctx.enter_context(nc.semaphore(name))

        def dram(name, shape, dt=F):
            return nc.dram_tensor(name, shape, dt, kind="Internal").ap()

        pe, act, ve, po, sp = (Engine(new_sem("q_" + n), per, fixed) for n, per, fixed in (
            ("pe", 0, 0), ("act", 0.83, 100), ("dve", 1.05, 60), ("pool", 2.1, 130), ("sp", 0, 0)))

        landed = {}
        stores = []

        def sent_on(sem, store, end):
            landed[id(sem)] = landed.get(id(sem), 0) + 16
            t = Landed(sem, landed[id(sem)], end)
            if store:
                stores.append(t)
            return t

        def dma(queue, sem, dst, src, w=(), store=False):
            queue.put(lambda e: e.dma_start(dst, src), w, 60, sem)
            return sent_on(sem, store, queue.clock + 4500)

        def scatter(sem, dst, idx, src, bound, w=()):
            po.put(lambda e: e.indirect_dma_start(dst, bass.IndirectOffsetOnAxis(idx, 0), src, None,
                                                  bounds_check=bound, oob_is_err=False), w, 1040, sem)
            return sent_on(sem, True, po.clock + 3000)

        def tiles(name, n, shape, dt=F):
            whole = sb(name, [128, n] + shape, dt)
            return Store([Tile(whole[:, i], name) for i in range(n)])

        d_h = dram("d_h", [G, 128, 2, 1024], R)
        d_p1 = dram("d_p1", [E * 512, PW])
        d_p2 = dram("d_p2", [E * 1024, PW])
        d_x1 = dram("d_x1", [T, H])
        out = io["out"]

        units = Store([Tile(ctx.enter_context(nc.psum_tensor(f"ps{i}", [128, 1024], F))[:, :], "psum")
                       for i in range(4)])

        wslot = [sb(f"wslot{i}", [128, 8192], R) for i in range(2)]
        small = sb("small", [128, 5200], R)
        stage = tiles("stage", 1, [2048])
        ft = tiles("ft", 11, [1024])
        rt = tiles("rt", 9, [1024], R)
        borrowed = [Tile(wslot[1][:, 4096 + i * 1024:5120 + i * 1024], "rt") for i in range(4)]
        lent = [Tile(small[:, i * 1024:(i + 1) * 1024], "rt") for i in range(5)]
        tiles_w = ft.idle + rt.idle
        rt.idle += borrowed
        pay = tiles("pay", 2, [4, PW])
        ident = sb("ident", [128, 128])
        tri = sb("tri", [128, 128], BF)
        ones = sb("ones", [128, 128], BF)
        oner = sb("oner", [128, 2], R)
        mask = sb("mask", [128, 2, 160])
        desc = sb("desc", [128, 8])
        offs = sb("offs", [128, 2, 8])
        ids = sb("ids", [128, 64], I)
        half = sb("half", [128, 8])
        ecol = sb("ecol", [128, 32])
        mean = sb("mean", [128, 64])
        rstd = sb("rstd", [128, 64])
        ks = sb("ks", [128, 64])
        base = sb("base", [128, 2, 8])
        hsum = sb("hsum", [128, 2, 18])
        cols = sb("cols", [128, 64])
        rows = sb("rows", [128, 12, 256])
        bst = tiles("bst", 3, [4, 6])
        sm = tiles("sm", 8, [64])
        rtl = tiles("rtl", 6, [64])
        ohs = tiles("ohs", 2, [32], BF)

        def setup():
            c = {}
            a = po.memset(ident[:, :], 0.0)
            c["ident"] = po.affine_select(out=ident[:, :], in_=ident[:, :], compare_op=ALU.not_equal, fill=1.0,
                base=0, pattern=[[-1, 128]], channel_multiplier=1, w=(a,))
            a = ve.memset(ones[:, :], 1.0)
            c["tri"] = po.affine_select(out=tri[:, :], in_=ones[:, :], compare_op=ALU.is_gt, fill=0.0, base=0,
                pattern=[[1, 128]], channel_multiplier=-1, w=(a,))
            a = ve.memset(mask[:, :, :], 0.0)
            b = po.affine_select(out=mask[:, :, :], in_=mask[:, :, :], compare_op=ALU.is_ge, fill=NEG, base=32,
                pattern=[[0, 2], [-1, 160]], channel_multiplier=1, w=(a,))
            b = po.affine_select(out=mask[:, :, :], in_=mask[:, :, :], compare_op=ALU.is_ge, fill=NEG, base=-16,
                pattern=[[0, 2], [1, 160]], channel_multiplier=-1, w=(b,))
            c["mask"] = po.memset(mask[:, 1, 0:32], NEG, w=(b,))
            po.iota(desc[:, :], pattern=[[-1, 8]], base=8, channel_multiplier=0, allow_small_or_imprecise_dtypes=True)
            po.iota(offs[:, 0, :], pattern=[[512, 8]], base=0, channel_multiplier=0,
                allow_small_or_imprecise_dtypes=True)
            po.iota(offs[:, 1, :], pattern=[[1024, 8]], base=0, channel_multiplier=0,
                allow_small_or_imprecise_dtypes=True)
            po.iota(ids[:, :], pattern=[[128, 64]], base=0, channel_multiplier=1)
            po.memset(half[:, 0:4], -0.5)
            po.memset(half[:, 4:8], 0.5)
            po.memset(base[:, :, :], 0.0)
            c["pool"] = po.memset(ecol[:, :], 2.718281828459045)
            a = ve.memset(cols[:, 60:61], 0.0)
            c["oner"] = act.activation(oner[:, :], ones[:, 0:2], ACT.Copy, w=(a,))
            return c

        C = setup()

        s_w = new_sem("s_w")

        def load(dst, src, *w):
            return dma(sp, s_w, dst, src, w=(*w,))

        def col(at, name, n=2):
            load(cols[:, at:at + n], io[name])
            return cols[:, at:at + n]

        def row(at, name):
            load(rows[:, at, :], io[name].partition_broadcast(128))
            return rows[:, at, :]

        memb_c, bi_c, bl1_c, bl2_c, bo_c = (col(2 * i, n) for i, n in enumerate(
            ("mem_b_c", "bi_c", "bl1_c", "bl2_c", "bo_c")))
        b1_c = col(10, "b1_c", 8)
        lng_c, lnb_c = col(18, "ln_g_c"), col(20, "ln_b_c")
        load(cols[:, 22:23], io["fgate"].partition_broadcast(128))
        load(cols[:, 23:24], io["lrate"].partition_broadcast(128))
        rows_in = [row(i, n) for i, n in enumerate(
            ("g1", "be1", "g2", "be2", "g3", "be3", "b2", "bo", "bg", "b_out"))]
        g1_r, be1_r, g2_r, be2_r, g3_r, be3_r, b2_r, bo_r, bg_r, bout_r = rows_in
        mb_row = sb("mb_row", [1, 512])
        load(mb_row[0:1, 0:256], io["mem_b"].partition_broadcast(1))
        load(mb_row[0:1, 256:512], io["bi"].partition_broadcast(1))
        gwT = sb("gwT", [128, 2, 8])
        wgT = sb("wgT", [128, 2, 8])
        load(gwT[:, :, :], io["gate_wT"].rearrange("(c p) e -> p c e", p=128))
        w_small = load(wgT[:, :, :], io["wg"].rearrange("(c p) e -> p c e", p=128))

        def f32(ap):
            return ap.bitcast(F)

        def v3(ap, a, b):
            return ap.rearrange("p (a b) -> p a b", a=a, b=b)

        def split(hi, lo, src, *w, engine="v"):
            a = act.activation(hi, src, ACT.Copy, w=(*w,))
            put = ve if engine == "v" else po
            b = put.tensor_tensor(lo, src, f32(hi), ALU.subtract, w=(a,))
            return a, b

        def evac(hi, lo, ps, *w):
            a = act.activation(hi, ps, ACT.Copy, w=(*w,))
            b = ve.tensor_tensor(lo, ps, f32(hi), ALU.subtract, w=(a,))
            return a, b

        def evac_(hi, lo, ps, *w):
            n = 512
            a0 = act.activation(hi[:, 0:n], ps[:, 0:n], ACT.Copy, w=(*w,))
            a1 = act.activation(hi[:, n:2 * n], ps[:, n:2 * n], ACT.Copy)
            yield a0
            b0 = ve.tensor_tensor(lo[:, 0:n], ps[:, 0:n], f32(hi[:, 0:n]), ALU.subtract, w=(a0,))
            b1 = ve.tensor_tensor(lo[:, n:2 * n], ps[:, n:2 * n], f32(hi[:, n:2 * n]), ALU.subtract, w=(a1,))
            return a1, b1

        def turned(x, t, lo_hi=True):
            yield room(r=2)
            yield units.has()
            h, l = rt.take(), rt.take()
            ps = units.take()
            tt = transposes(ps.ap, x, t, *ps.last)
            yield tt
            a, b = yield from evac_(h.ap, l.ap, ps.ap, tt, *h.last, *l.last)
            units.give(ps, a, b)
            return h, l, a, b, tt

        def room(f=0, r=0, u=0, s=0):
            return lambda: (len(ft.idle) >= f and len(rt.idle) >= r and len(units.idle) >= u
                            and len(sm.idle) >= s)

        stage_sem = {id(t): new_sem(f"s_st{i}") for i, t in enumerate(stage.idle)}

        def chunks(ap, n):
            return ap.rearrange("(c p) n -> p c n", p=128)

        def ff_weights(slot, w1, w2, *w, w2_waits=()):
            s = wslot[slot]
            parts = dict(w1h=v3(s[:, 0:2048], 2, 1024), w1l=v3(s[:, 2048:4096], 2, 1024),
                         w2h=v3(s[:, 4096:6144], 8, 256), w2l=v3(s[:, 6144:8192], 8, 256))
            st = stage.take()
            t = dma(sp, stage_sem[id(st)], v3(st.ap, 2, 1024), chunks(w1, 1024), w=(*st.last,))
            a, b = split(s[:, 0:2048], s[:, 2048:4096], st.ap, t, *w)
            stage.give(st, a, b)
            parts["t1"] = b
            st2 = stage.take()
            t = dma(sp, stage_sem[id(st2)], v3(st2.ap, 8, 256), chunks(w2, 256), w=(*st2.last,))
            a, b = split(s[:, 4096:6144], s[:, 6144:8192], st2.ap, t, *w, *w2_waits)
            stage.give(st2, a, b)
            parts["t2"] = b
            return parts

        def stats(x, out_mv, *w):
            st = bst.take()
            t = None
            for i in range(4):
                t = ve.bn_stats(st.ap[:, i, :], x[:, i, :], w=(*w, *st.last))
            w = ()
            for i in range(4):
                b = ve.bn_aggr(out_mv[:, i, :], st.ap[:, i, :], w=(t,))
            bst.give(st, b)
            return b, t

        def rsqrt(dst, var, tmp, *w):
            a = po.tensor_scalar(tmp, var, EPS, None, ALU.add, w=(*w,))
            return po.tensor_tensor(dst, tmp, half[:, 0:4], ALU.pow, w=(a, C["pool"]))

        def norm(dst, x, m, r, *w):
            for i in range(4):
                t = ve.tensor_scalar(dst[:, i, :], x[:, i, :], m[:, i:i + 1], r[:, i:i + 1], ALU.subtract, ALU.mult,
                    w=(*w,))
            return t

        def transposes(ps, x, *w, n=4):
            for i in range(n):
                for c in range(2):
                    t = pe.transpose(ps[:, c * 512 + i * 128:c * 512 + i * 128 + 128], x[:, i, c * 128:(c + 1) * 128],
                        ident[:, :], w=(*w, C["ident"]))
            return t

        def to_tokens(ps, xT, *w):
            for i in range(4):
                for c in range(2):
                    t = pe.transpose(ps[:, i * 256 + c * 128:i * 256 + c * 128 + 128], xT[:,
                        c * 512 + i * 128:c * 512 + i * 128 + 128], ident[:, :], w=(*w, C["ident"]))
            return t

        def three(o, pairs, start, stop, w=()):
            ops = []
            for lh, ll, rh, rl in pairs:
                ops += [(lh, rh), (lh, rl), (ll, rh)]
            for j, (a, b) in enumerate(ops):
                t = pe.matmul(o, a, b, start=start and j == 0, stop=stop and j == len(ops) - 1, skip_group_check=True,
                    w=(*w,))
            return t

        def wide(ps, wh, wl, xh, xl, n, w, oc):
            return three(ps, [(wh[:, c, oc * 128:oc * 128 + 128], wl[:, c, oc * 128:oc * 128 + 128],
                               xh[:, c * 512:c * 512 + n], xl[:, c * 512:c * 512 + n]) for c in range(2)],
                         True, True, w)

        def ff(xh, xl, W, func, bias, done, *w):
            o = None
            pend = []

            def second(j, fh, fl, th, tl):
                for i in range(4):
                    for k in range(2):
                        c = 2 * j + k
                        t = three(o.ap[:, i * 256:(i + 1) * 256],
                                  [(fh.ap[:, k * 512 + i * 128:k * 512 + i * 128 + 128],
                                    fl.ap[:, k * 512 + i * 128:k * 512 + i * 128 + 128],
                                    W["w2h"][:, c, :], W["w2l"][:, c, :])],
                                  j == 0 and k == 0 and i % 2 == 0, j == 3 and k == 1,
                                  (th, tl, W["t2"], *o.last))
                rt.give(fh, t)
                rt.give(fl, t)
                return t

            for j in range(4):
                yield room(f=1, r=2, u=2 if o is None else 1)
                if o is None:
                    o = units.take()
                f, fh, fl = ft.take(), rt.take(), rt.take()
                ps = units.take()
                ts = []
                for k in range(2):
                    ts.append(wide(ps.ap[:, k * 512:(k + 1) * 512], W["w1h"], W["w1l"], xh, xl, 512,
                                   (*w, W["t1"], *ps.last), 2 * j + k))
                last_in = ts[1]
                yield ts[0]
                aa = []
                for k in range(2):
                    b = bias[:, 2 * j + k:2 * j + k + 1] if bias is not None else 0.0
                    s = slice(k * 512, (k + 1) * 512)
                    th = act.activation(fh.ap[:, s], ps.ap[:, s], func, bias=b, w=(ts[k], *fh.last))
                    a = act.activation(f.ap[:, s], ps.ap[:, s], func, bias=b, w=(*f.last,))
                    aa.append(a)
                units.give(ps, a)
                yield aa[0]
                for k in range(2):
                    s = slice(k * 512, (k + 1) * 512)
                    tl = (ve if (j + k) % 4 else po).tensor_tensor(fl.ap[:, s], f.ap[:, s], f32(fh.ap[:, s]),
                        ALU.subtract, w=(aa[k], *fl.last))
                    if k == 0:
                        t0 = tl
                ft.give(f, t0, tl)
                pend.append((j, fh, fl, t0, tl))
                if j >= 1:
                    yield pend[0][4]
                    second(*pend.pop(0))
            yield tl
            done["x"] = last_in
            done["t"] = second(*pend.pop(0))
            done["o"] = o
            yield done["t"]

        routed = [0, 0]

        def route(which, g, cap, xT, wT, dst_slot, dst_w, *w):
            yield lambda: routed[which] == g
            yield units.has()
            yield lambda: len(rtl.idle) >= 2 and len(ohs.idle) >= 1 and len(sm.idle) >= 1
            ps = units.take()
            for i in range(4):
                for c in range(2):
                    t = pe.matmul(ps.ap[:, i * 8:i * 8 + 8], xT[:, c * 512 + i * 128:c * 512 + i * 128 + 128], wT[:,
                        c, :], start=c == 0, stop=c == 1, w=(w_small, *w, *ps.last))
            last_x = t
            lg, cd, s, oh = rtl.take(), rtl.take(), sm.take(), ohs.take()
            L, X = v3(lg.ap[:, 0:32], 4, 8), v3(lg.ap[:, 32:64], 4, 8)
            code, sl = v3(cd.ap[:, 0:32], 4, 8), v3(cd.ap[:, 32:64], 4, 8)
            mx, cm, se = s.ap[:, 0:4], s.ap[:, 4:8], s.ap[:, 8:12]
            slf = s.ap[:, 12:16]
            yield t
            t = ve.tensor_copy(L, v3(ps.ap[:, 0:32], 4, 8), w=(t, *lg.last))
            units.give(ps, t)
            t1 = ve.tensor_reduce(mx, L, AX.X, ALU.max, w=(t, *s.last))
            mxb = mx.unsqueeze(2).to_broadcast([128, 4, 8])
            t2 = ve.tensor_tensor(X, L, mxb, ALU.subtract, w=(t1,))
            t3 = ve.tensor_scalar(code, X, 0.0, None, ALU.is_equal, w=(t2, *cd.last))
            tp = po.tensor_tensor(lg.ap[:, 0:32], ecol[:, :], lg.ap[:, 32:64], ALU.pow, w=(t2, C["pool"]))
            t4 = ve.tensor_tensor(code, code, desc[:, :].unsqueeze(1).to_broadcast([128, 4, 8]), ALU.mult, w=(t3,))
            t5 = ve.tensor_reduce(cm, code, AX.X, ALU.max, w=(t4,))
            t6 = ve.tensor_tensor(v3(oh.ap, 4, 8), code, cm.unsqueeze(2).to_broadcast([128, 4, 8]), ALU.is_equal,
                w=(t5, *oh.last))
            yield t6
            yield units.has()
            ps = units.take()
            for i in range(5):
                ops = [(ones, k) for k in range(min(i, 4))] + ([(tri, i)] if i < 4 else [])
                for n, (m, k) in enumerate(ops):
                    t = pe.matmul(ps.ap[:, i * 8:i * 8 + 8], m[:, :], oh.ap[:, k * 8:k * 8 + 8], start=n == 0,
                        stop=n == len(ops) - 1, w=(t6, C["tri"], *ps.last))
            yield t
            t1 = ve.tensor_tensor(sl, v3(ps.ap[:, 0:32], 4, 8), base[:, which, :].unsqueeze(1).to_broadcast([128, 4,
                8]), ALU.add, w=(t, base_t[which], C["pool"]))
            t2 = ve.tensor_tensor(base[:, which, :], base[:, which, :], ps.ap[:, 32:40], ALU.add, w=(t1,))
            base_t[which] = t2
            units.give(ps, t2)
            t3 = ve.tensor_scalar(code, sl, float(cap), FAR, ALU.is_ge, ALU.mult, w=(t1,))
            t4 = ve.tensor_tensor(sl, sl, offs[:, which, :].unsqueeze(1).to_broadcast([128, 4, 8]), ALU.add, w=(t3,))
            t5 = ve.tensor_tensor(sl, sl, code, ALU.add, w=(t4,))
            t6 = ve.tensor_tensor(sl, sl, v3(oh.ap, 4, 8), ALU.mult, w=(t5,))
            t7 = ve.tensor_reduce(slf, sl, AX.X, ALU.add, w=(t6,))
            t8 = ve.tensor_copy(dst_slot, slf, w=(t7,))
            t9 = ve.tensor_reduce(se, L, AX.X, ALU.add, w=(tp,))
            t10 = ve.reciprocal(dst_w, se, w=(t9,))
            ohs.give(oh, t6)
            rtl.give(lg, t10)
            rtl.give(cd, t8)
            sm.give(s, t10)
            routed[which] += 1
            return last_x, t8, t10

        base_t = [C["pool"], C["pool"]]

        pay_sem = {id(t): new_sem(f"s_pay{i}") for i, t in enumerate(pay.idle)}
        ft_sem = {id(t): new_sem(f"s_ft{i}") for i, t in enumerate(tiles_w + borrowed + lent)}
        rt_sem = ft_sem
        out_sem = {id(t): new_sem(f"s_out{i}") for i, t in enumerate(pay.idle)}
        scat_sem = {id(t): new_sem(f"s_sc{i}") for i, t in enumerate(pay.idle + ft.idle)}
        s_b1 = new_sem("s_b1")
        s_fill = new_sem("s_fill")

        def tok_rows(ap, g):
            return ap[g * 512:(g + 1) * 512, :].rearrange("(t p) n -> p t n", p=128)

        def load_x(src, g, *w):
            t = ft.take()
            ld = dma(sp, ft_sem[id(t)], v3(t.ap, 4, 256), tok_rows(src, g), w=(*t.last, *w))
            return t, ld

        def fill():
            f = pay.take()
            a = ve.memset(f.ap[:, :, :], 0.0)
            b = ve.memset(f.ap[:, :, 260:261].bitcast(U), 1000000, w=(a,))
            for d, n in ((d_p1, E), (d_p2, 2 * E)):
                for i in range(n):
                    t = dma(sp, s_fill, tok_rows(d, i), f.ap[:, :, :], w=(b,), store=True)
            pay.give(f, t)
            return t

        filled = fill()

        w1p_h, w1p_l = v3(small[:, 0:512], 2, 256), v3(small[:, 512:1024], 2, 256)
        wl2_h, wl2_l = v3(small[:, 1024:1536], 2, 256), v3(small[:, 1536:2048], 2, 256)
        a12_h, a12_l = v3(small[:, 2048:3072], 2, 512), v3(small[:, 3072:4096], 2, 512)
        wg1_h, wg1_l = v3(small[:, 4096:4608], 2, 256), v3(small[:, 4608:5120], 2, 256)

        def load_f(name, t=None):
            t = t or ft.take()
            ld = dma(sp, ft_sem[id(t)], v3(t.ap[:, 0:512], 2, 256), chunks(io[name], 256), w=(*t.last,))
            return t, v3(t.ap[:, 0:512], 2, 256), ld

        def mm256(ps, lhs, rhs, w, start=True, stop=True):
            for oc in range(2):
                for c in range(2):
                    t = pe.matmul(ps[:, oc * 512:oc * 512 + 256], lhs[:, c, oc * 128:oc * 128 + 128], rhs[:, c, :],
                        start=start and c == 0, stop=stop and c == 1, w=(*w,))
            return t

        def two(ps):
            return ps.rearrange("p (a b) -> p a b", a=2)[:, :, 0:256]

        def prepare():
            r = {}
            wi, wi_v, t1 = load_f("Wi")
            wl1, wl1_v, t2 = load_f("Wl1T")
            ps = units.take()
            t = mm256(ps.ap, wi_v, wl1_v, (t1, t2, *ps.last))
            a, b = evac(w1p_h, w1p_l, two(ps.ap), t)
            units.give(ps, a, b)
            r["w1p"] = b
            ps = units.take()
            for oc in range(2):
                for c in range(2):
                    t = pe.matmul(ps.ap[:, oc:oc + 1], wl1_v[:, c, oc * 128:oc * 128 + 128], bi_c[:, c:c + 1],
                        start=c == 0, stop=c == 1, w=(w_small, *ps.last))
            r["b1p"] = ve.tensor_tensor(cols[:, 24:26], ps.ap[:, 0:2], bl1_c, ALU.add, w=(t,))
            units.give(ps, r["b1p"])
            ft.give(wi, t)
            ft.give(wl1, t)
            wl2, wl2_v, t1 = load_f("Wl2T")
            a, b = split(wl2_h, wl2_l, wl2_v, t1)
            r["wl2"] = b
            ft.give(wl2, a, b)
            return r

        P = prepare()
        b1p = cols[:, 24:26]

        gram = units.take()

        def hidden(kT, n, acc, *w):
            yield room(f=1, r=2, u=1)
            f, fh, fl = ft.take(), rt.take(), rt.take()
            ps = units.take()
            for oc in range(2):
                t = wide(ps.ap[:, oc * 512:oc * 512 + n], w1p_h, w1p_l, kT[0].ap, kT[1].ap, n,
                         (*w, P["w1p"], *ps.last), oc)
            rt.give(kT[0], t)
            rt.give(kT[1], t)
            yield t
            for oc in range(2):
                for dst in (f, fh):
                    a = act.activation(dst.ap[:, oc * 512:oc * 512 + n], ps.ap[:, oc * 512:oc * 512 + n], ACT.Silu,
                        bias=b1p[:, oc:oc + 1], w=(t, P["b1p"], *dst.last))
            units.give(ps, a)
            yield a
            tl = None
            for oc in range(2):
                s = slice(oc * 512, oc * 512 + n)
                tl = ve.tensor_tensor(fl.ap[:, s], f.ap[:, s], f32(fh.ap[:, s]), ALU.subtract, w=(a, *fl.last))
            ft.give(f, tl)
            yield tl
            yield room(f=1, r=1, u=1)
            h, hh = ft.take(), rt.take()
            ps = units.take()
            for oc in range(2):
                t = wide(ps.ap[:, oc * 512:oc * 512 + n], wl2_h, wl2_l, fh.ap, fl.ap, n,
                         (tl, P["wl2"], *ps.last), oc)
            rt.give(fh, t)
            rt.give(fl, t)
            yield t
            m = n if n == 512 else 10
            for oc in range(2):
                a1 = act.activation(h.ap[:, oc * 512:oc * 512 + m], ps.ap[:, oc * 512:oc * 512 + m], ACT.Silu,
                    bias=bl2_c[:, oc:oc + 1], accum_out=acc[oc], w=(t, w_small, *h.last))
            if n == 512:
                for oc in range(2):
                    a = act.activation(hh.ap[:, oc * 512:oc * 512 + n], ps.ap[:, oc * 512:oc * 512 + n], ACT.Silu,
                        bias=bl2_c[:, oc:oc + 1], w=(*hh.last,))
            else:
                a = a1
            units.give(ps, a)
            return h, hh, a1, a

        def slots_of_memory():
            x, kt = ft.take(), ft.take()
            z = ve.memset(x.ap[:, 0:256], 0.0, w=(*x.last,))
            ld = dma(sp, ft_sem[id(x)], x.ap[0:10, 0:256], io["P"], w=(z,))
            s = sm.take()
            a = act.activation(x.ap[:, 256:512], x.ap[:, 0:256], ACT.Square, accum_out=s.ap[:, 0:1], w=(ld, z))
            b = po.tensor_tensor(s.ap[:, 1:2], s.ap[:, 0:1], half[:, 4:5], ALU.pow, w=(a, C["pool"]))
            b = ve.tensor_scalar(s.ap[:, 2:3], s.ap[:, 1:2], 1e-12, None, ALU.max, w=(b,))
            b = ve.reciprocal(s.ap[:, 3:4], s.ap[:, 2:3], w=(b,))
            kn = ve.tensor_scalar(x.ap[:, 512:768], x.ap[:, 0:256], s.ap[:, 3:4], None, ALU.mult, w=(b,))
            sm.give(s, kn)
            ps = units.take()
            for c in range(2):
                t = pe.transpose(ps.ap[:, c * 512:c * 512 + 128], x.ap[:, 512 + c * 128:512 + c * 128 + 128], ident[:,
                    :], w=(kn, C["ident"], *ps.last))
            kh, kl = rt.take(), rt.take()
            for c in range(2):
                q = slice(c * 512, c * 512 + 128)
                a, b = evac(kh.ap[:, q], kl.ap[:, q], ps.ap[:, q], t)
            units.give(ps, a, b)
            hg = hidden((kh, kl), 128, [hsum[:, 0, 16:17], hsum[:, 1, 16:17]], a, b)
            while True:
                try:
                    y = next(hg)
                    assert not callable(y) or y()
                except StopIteration as e:
                    h, hh, a1, _ = e.value
                    break
            rt.give(hh, *hh.last)
            ps = units.take()
            for c in range(2):
                t = pe.transpose(ps.ap[0:10, c * 128:c * 128 + 128], h.ap[:, c * 512:c * 512 + 10], ident[:, :],
                    w=(a1, *ps.last))
            ft.give(h, t)
            rh, rl, ll = rt.take(), rt.take(), rt.take()
            z = ve.memset(kt.ap, 0.0, w=(*kt.last,))
            z1 = ve.tensor_copy(kt.ap[0:10, 0:256], ps.ap[0:10, 0:256], w=(z, t))
            z2 = ve.tensor_copy(kt.ap[:, 256:512], x.ap[:, 512:768], w=(kn, z))
            z3 = ve.tensor_scalar(kt.ap[0:10, 512:768], ps.ap[0:10, 0:256], 8.0, None, ALU.mult, w=(z2,))
            units.give(ps, z3)
            a, b = split(rh.ap[:, 0:512], rl.ap[:, 0:512], kt.ap[:, 0:512], z1, z2, *rh.last, *rl.last)
            a, b2 = split(ll.ap[:, 0:256], ll.ap[:, 256:512], kt.ap[:, 512:768], z3, *ll.last)
            ft.give(kt, a, b, b2)
            ft.give(x, z2, a)
            for c in range(2):
                t = three(gram.ap[:, c * 512:(c + 1) * 512],
                          [(ll.ap[:, c * 128:c * 128 + 128], ll.ap[:, 256 + c * 128:256 + c * 128 + 128],
                            rh.ap[:, 0:512], rl.ap[:, 0:512])], True, False, (b, b2, *gram.last))
            for q in (rh, rl, ll):
                rt.give(q, t)
            return a1

        pt = slots_of_memory()
        hstore = {}

        def first(g):
            yield room(f=3)
            x, ld = load_x(io["x"], g)
            kn = ft.take()
            yield ld
            s = sm.take()
            mv = v3(s.ap[:, 0:8], 4, 2)
            xv = v3(x.ap, 4, 256)
            c4 = slice(4 * g, 4 * g + 4)
            t, _ = stats(xv, mv, ld, *s.last)
            t0 = ve.tensor_copy(mean[:, c4], mv[:, :, 0], w=(t,))
            yield t
            r = rsqrt(rstd[:, c4], mv[:, :, 1], s.ap[:, 8:12], t)
            a = po.tensor_tensor(s.ap[:, 12:16], mv[:, :, 1], half[:, 4:8], ALU.pow, w=(t,))
            a = po.tensor_tensor(s.ap[:, 16:20], s.ap[:, 12:16], rstd[:, c4], ALU.mult, w=(a, r))
            yield a
            b = ve.tensor_scalar(s.ap[:, 20:24], s.ap[:, 16:20], 16.0, 1e-12, ALU.mult, ALU.max, w=(a,))
            b = ve.reciprocal(s.ap[:, 24:28], s.ap[:, 20:24], w=(b,))
            b = ve.tensor_tensor(s.ap[:, 28:32], s.ap[:, 24:28], rstd[:, c4], ALU.mult, w=(b,))
            t = norm(v3(kn.ap, 4, 256), xv, mean[:, c4], s.ap[:, 28:32], b, t0, *kn.last)
            sm.give(s, t)
            ft.give(x, t)
            yield t
            knv = v3(kn.ap, 4, 256)
            kh, kl, a, b, tt = yield from turned(knv, t)
            yield b
            h, hh, a1, a = yield from hidden((kh, kl), 512, [hsum[:, 0, g:g + 1], hsum[:, 1, g:g + 1]], a, b)
            yield room(r=5, u=1)
            hl = rt.take()
            rows_h, rows_l = [rt.take(), rt.take()], [rt.take(), rt.take()]
            ps = units.take()
            tp = to_tokens(ps.ap, h.ap, a1, *ps.last)
            for k in range(2):
                rv, lv = v3(rows_h[k].ap, 2, 512), v3(rows_l[k].ap, 2, 512)
                ka = act.activation(rv[:, :, 256:512], knv[:, 2 * k:2 * k + 2, :], ACT.Copy, w=(t, *rows_h[k].last))
                kb = po.tensor_tensor(lv[:, :, 256:512], knv[:, 2 * k:2 * k + 2, :], f32(rv[:, :, 256:512]),
                    ALU.subtract, w=(ka, *rows_l[k].last))
            ft.give(kn, tt, kb)
            yield tp
            for k in range(2):
                rv, lv = v3(rows_h[k].ap, 2, 512), v3(rows_l[k].ap, 2, 512)
                src = v3(ps.ap[:, k * 512:(k + 1) * 512], 2, 256)
                a_, b_ = evac(rv[:, :, 0:256], lv[:, :, 0:256], src, tp, *rows_l[k].last)
            units.give(ps, a_, b_)
            b = ve.tensor_tensor(hl.ap, h.ap, f32(hh.ap), ALU.subtract, w=(a, *hl.last))
            ft.give(h, tp, b)
            o1 = dma(sp, rt_sem[id(hh)], f32(d_h[g, :, 0, :]), f32(hh.ap), w=(a,), store=True)
            o2 = dma(sp, rt_sem[id(hl)], f32(d_h[g, :, 1, :]), f32(hl.ap), w=(b,), store=True)
            hstore[g] = (o1, o2)
            rt.give(hh, o1, b)
            rt.give(hl, o2)
            yield (b_, kb)
            for i in range(4):
                rh, rl = rows_h[i // 2].ap, rows_l[i // 2].ap
                o = (i % 2) * 512
                gram_n[0] += 1
                for c in range(2):
                    t = three(gram.ap[:, c * 512:(c + 1) * 512],
                              [(rh[:, o + c * 128:o + c * 128 + 128], rl[:, o + c * 128:o + c * 128 + 128],
                                rh[:, o:o + 512], rl[:, o:o + 512])], False, gram_n[0] == 4 * G, (a_, b_, kb))
            for q in rows_h + rows_l:
                rt.give(q, t)
            first_done[g] = t

        gram_n = [0]
        first_done = {}
        sent = [[], []]
        run([first(g) for g in range(G)], 3, "first")

        def middle():
            wo, wo_v, t_wo = load_f("WoT")
            mwt, mwt_v, t_mwt = load_f("mem_WT")
            wit, wit_v, t_wit = load_f("WiT")
            mw, mw_v, t_mw = load_f("mem_W")
            wg2, wg2_v, t_wg2 = load_f("Wg2T")
            wg1, wg1_v, t_wg1 = load_f("Wg1T")
            a, b = split(wg1_h, wg1_l, wg1_v, t_wg1)
            ft.give(wg1, a, b)
            wg1_t = b
            rep = ft.take()
            for c in range(2):
                a = ve.tensor_copy(rep.ap[:, c * 128:(c + 1) * 128], memb_c[:, c:c + 1].to_broadcast([128, 128]),
                    w=(w_small, *rep.last))
            ps = units.take()
            for c in range(2):
                t = pe.matmul(ps.ap[:, 0:256], rep.ap[:, c * 128:(c + 1) * 128], wo_v[:, c, :], start=c == 0,
                    stop=c == 1, w=(a, t_wo, *ps.last))
            for oc in range(2):
                for c in range(2):
                    t = pe.matmul(ps.ap[:, 512 + oc:513 + oc], wo_v[:, c, oc * 128:oc * 128 + 128], memb_c[:,
                        c:c + 1], start=c == 0, stop=c == 1)
            cb = ve.tensor_tensor(bias_mg[:, 0:256], ps.ap[:, 0:256], bo_r, ALU.add, w=(t,))
            b = ve.tensor_tensor(cols[:, 26:28], ps.ap[:, 512:514], bo_c, ALU.add, w=(cb,))
            for c in range(2):
                d = ve.tensor_copy(rep.ap[:, 256 + c * 128:256 + (c + 1) * 128], cols[:,
                    26 + c:27 + c].to_broadcast([128, 128]), w=(b,))
            units.give(ps, b)
            ps = units.take()
            for c in range(2):
                t = pe.matmul(ps.ap[:, 0:256], rep.ap[:, 256 + c * 128:256 + (c + 1) * 128], wg2_v[:, c, :],
                    start=c == 0, stop=c == 1, w=(d, t_wg2, *ps.last))
            bg = ve.tensor_tensor(bias_mg[:, 256:512], ps.ap[:, 0:256], bg_r, ALU.add, w=(t,))
            units.give(ps, bg)
            ft.give(rep, t)
            a = ve.tensor_scalar(cols[:, 28:29], cols[:, 22:23], -1.0, 1.0, ALU.mult, ALU.add, w=(w_small,))
            sc = ve.tensor_scalar(cols[:, 29:30], cols[:, 23:24], 2.0 / (N_MEM * 256), None, ALU.mult)
            mws = ve.tensor_scalar(mw_v, mw_v, cols[:, 28:29], None, ALU.mult, w=(a, t_mw))
            p8 = ve.tensor_scalar(hsum[:, :, 17:18], hsum[:, :, 16:17], 8.0, None, ALU.mult, w=(pt,))
            hs = ve.tensor_reduce(cols[:, 30:32], hsum[:, :, 0:16], AX.X, ALU.add, w=(hs_done[0],))
            hs = ve.tensor_tensor(cols[:, 32:34], cols[:, 30:32], hsum[:, :, 17], ALU.add, w=(hs, p8))
            r0 = ve.tensor_tensor(mb_row[0:1, 0:256], mb_row[0:1, 0:256], mb_row[0:1, 256:512], ALU.subtract,
                w=(w_small,))
            gs = ft.take()
            ga = act.activation(gs.ap, gram.ap, ACT.Copy, w=(*first_done.values(), *gs.last))
            units.give(gram, ga)
            ps = units.take()
            for c in range(2):
                t = pe.matmul(ps.ap[0:1, c * 128:c * 128 + 128], cols[:, 32 + c:33 + c], ident[:, :], start=True,
                    stop=True, w=(hs, *ps.last))
            hr = ve.tensor_copy(mb_row[0:1, 256:512], ps.ap[0:1, 0:256], w=(t, r0))
            for c in range(2):
                for q in range(2):
                    t = pe.transpose(ps.ap[:, 512 + q * 256 + c * 128:512 + q * 256 + c * 128 + 128], gs.ap[:,
                        c * 512 + 256 + q * 128:c * 512 + 256 + q * 128 + 128], ident[:, :], w=(ga,))
            g2 = ft.take()
            gt = ve.tensor_scalar(g2.ap[:, 0:512], ps.ap[:, 512:1024], -1.0, None, ALU.mult, w=(t, *g2.last))
            units.give(ps, gt, hr)
            g2v = v3(g2.ap[:, 0:512], 2, 256)
            gsv = v3(gs.ap, 2, 512)
            ps = units.take()
            for m in range(2):
                o = ps.ap[:, m * 512:m * 512 + 256]
                for c in range(2):
                    pe.matmul(o, mwt_v[:, c, m * 128:m * 128 + 128], gsv[:, c, 0:256], start=c == 0, stop=False,
                        w=(ga, t_mwt, *ps.last))
                for c in range(2):
                    pe.matmul(o, wit_v[:, c, m * 128:m * 128 + 128], g2v[:, c, :], start=False, stop=False, w=(gt,
                        t_wit))
                t = pe.matmul(o, mb_row[0:1, m * 128:m * 128 + 128], mb_row[0:1, 256:512], start=False, stop=True,
                    w=(hr, r0))
            wn = ve.scalar_tensor_tensor(mw_v, two(ps.ap), cols[:, 29:30], mw_v, ALU.mult, ALU.add, w=(t, sc, mws))
            units.give(ps, wn)
            for q in (mwt, wit, gs, g2):
                ft.give(q, t)
            ps, ps2 = units.take(), units.take()
            t = mm256(ps.ap, wo_v, mw_v, (wn, t_wo, *ps.last))
            t2 = mm256(ps2.ap, mw_v, wo_v, (wn, *ps2.last))
            a1 = ft.take()
            a1v = v3(a1.ap[:, 0:512], 2, 256)
            b1 = act.activation(a1v, two(ps.ap), ACT.Copy, w=(t, *a1.last))
            units.give(ps, b1)
            ea, eb = evac(a12_h[:, :, 0:256], a12_l[:, :, 0:256], two(ps2.ap), t2)
            units.give(ps2, ea, eb)
            ft.give(mw, t2)
            ft.give(wo, t2)
            ps = units.take()
            t = mm256(ps.ap, a1v, wg2_v, (b1, t_wg2, *ps.last))
            fa, fb = evac(a12_h[:, :, 256:512], a12_l[:, :, 256:512], two(ps.ap), t)
            units.give(ps, fa, fb)
            ft.give(a1, t)
            ft.give(wg2, t)
            return (eb, fb, wg1_t), bg

        bias_mg = rows[:, 10:12, :].rearrange("p a b -> p (a b)")
        hs_done = [Token(act, len(act.ops) - 1)]
        A12_t, bmg_t = middle()
        WA = ff_weights(0, io["W1T"], io["W2T"])

        last_group = {}

        def load_h(g):
            hh, hl = rt.take(), rt.take()
            t1 = dma(sp, rt_sem[id(hh)], f32(hh.ap), f32(d_h[g, :, 0, :]), w=(*hh.last, hstore[g][0]))
            t2 = dma(sp, rt_sem[id(hl)], f32(hl.ap), f32(d_h[g, :, 1, :]), w=(*hl.last, hstore[g][1]))
            return hh, hl, t1, t2

        def affine(x, gr, br, *w):
            a = po.tensor_tensor(x, x, gr.unsqueeze(1).to_broadcast([128, 4, 256]), ALU.mult, w=(*w,))
            return po.tensor_tensor(x, x, br.unsqueeze(1).to_broadcast([128, 4, 256]), ALU.add, w=(a,))

        def layernorm(dst, x, *w):
            yield sm.has()
            s = sm.take()
            mv = v3(s.ap[:, 0:8], 4, 2)
            t, _ = stats(x, mv, *w, *s.last)
            yield t
            r = rsqrt(s.ap[:, 12:16], mv[:, :, 1], s.ap[:, 8:12], t)
            yield r
            t = norm(dst, x, mv[:, :, 0], s.ap[:, 12:16], r)
            sm.give(s, t)
            return t

        at_window = [0]

        def second(g):
            yield lambda: at_window[0] == g and len(ft.idle) >= 5
            xl = ft.take()
            xlv = v3(xl.ap, 4, 256)
            ld = dma(sp, ft_sem[id(xl)], xlv, tok_rows(io["x"], g), w=(*xl.last,))
            yield ld
            c4 = slice(4 * g, 4 * g + 4)
            tx = norm(xlv, xlv, mean[:, c4], rstd[:, c4], ld)
            yield tx
            th = ve.tensor_copy(halo[:, 0, :], halo[:, 4, :], w=(*halo_free,)) if g % 2 else None
            th = ve.tensor_copy(halo[:, 1:5, :], xlv[96:128, :, :], w=(tx, *halo_free, *([th] if th else [])))
            yield units.has()
            ps = units.take()
            t = transposes(ps.ap, xlv, tx, *ps.last)
            yield t
            xT = ft.take()
            ta = act.activation(xT.ap, ps.ap, ACT.Copy, w=(t, *xT.last))
            units.give(ps, ta)
            yield ta
            yield units.has()
            ps = units.take()
            for i in range(4):
                for part in range(2):
                    for c in range(2):
                        q = xT.ap[:, c * 512 + i * 128:c * 512 + i * 128 + 128]
                        if part:
                            k = q
                        elif i:
                            k = xT.ap[:, c * 512 + i * 128 - 32:c * 512 + i * 128]
                        elif g % 2:
                            k = last_group["xT"].ap[:, c * 512 + 480:c * 512 + 512]
                        else:
                            k = xT.ap[:, c * 512:c * 512 + 32]
                        o = ps.ap[:, i * 256 + 32 * part:i * 256 + (160 if part else 32)]
                        t = pe.matmul(o, q, k, start=c == 0 and part == 0 and i % 2 == 0, stop=c == 1,
                            skip_group_check=True, w=(ta, *ps.last))
            if g % 2:
                ft.give(last_group["xT"], t)
                ft.give(xT, t)
            else:
                last_group["xT"] = xT
            yield t
            yield room(f=2, s=2)
            sc, pT = ft.take(), ft.take()
            scv = v3(sc.ap[:, 0:640], 4, 160)
            psv = v3(ps.ap, 4, 256)[:, :, 0:160]
            s = sm.take()
            n0 = 0 if g % 2 else 1
            if n0:
                a = ve.tensor_tensor(scv[:, 0, :], psv[:, 0, :], mask[:, 1, :], ALU.add, w=(t, C["mask"], *sc.last))
            a = ve.tensor_tensor(scv[:, n0:4, :], psv[:, n0:4, :], mask[:, 0, :].unsqueeze(1).to_broadcast([128,
                4 - n0, 160]), ALU.add, w=(t, C["mask"], *sc.last))
            units.give(ps, a)
            b = ve.tensor_reduce(s.ap[:, 0:4], scv, AX.X, ALU.max, w=(a, *s.last))
            b = ve.tensor_scalar(s.ap[:, 4:8], s.ap[:, 0:4], -1.0 / 16.0, None, ALU.mult, w=(b,))
            yield b
            for i in range(4):
                ex = act.activation(scv[:, i, :], scv[:, i, :], ACT.Exp, bias=s.ap[:, 4 + i:5 + i], scale=1.0 / 16.0,
                    accum_out=s.ap[:, 8 + i:9 + i], w=(b,))
            yield ex
            ri = ve.reciprocal(s.ap[:, 12:16], s.ap[:, 8:12], w=(ex,))
            yield units.has()
            ps = units.take()
            for i in range(4):
                t = pe.transpose(ps.ap[:, i * 128:(i + 1) * 128], scv[:, i, 32:160], ident[:, :], w=(ex, *ps.last))
                t = pe.transpose(ps.ap[0:32, 512 + i * 128:512 + (i + 1) * 128], scv[:, i, 0:32], ident[:, :])
            ft.give(sc, t)
            yield t
            ta = act.activation(pT.ap[:, 0:512], ps.ap[:, 0:512], ACT.Copy, w=(t, *pT.last))
            tb = act.activation(pT.ap[0:32, 512:1024], ps.ap[0:32, 512:1024], ACT.Copy)
            units.give(ps, tb)
            yield tb
            yield units.has()
            ps = units.take()
            for i in range(4):
                o = ps.ap[:, i * 256:(i + 1) * 256]
                first_of_batch = i == 0 and g % 2 == 0
                pe.matmul(o, pT.ap[:, i * 128:(i + 1) * 128], xlv[:, i, :], start=i % 2 == 0, stop=first_of_batch,
                    skip_group_check=True, w=(ta, tb, *ps.last))
                if not first_of_batch:
                    before = halo[:, i, :]
                    t = pe.matmul(o, pT.ap[0:32, 512 + i * 128:512 + (i + 1) * 128], before, start=False, stop=True,
                        skip_group_check=True, w=(th,))
            halo_free[:] = [t]
            ft.give(pT, t)
            at_window[0] += 1
            yield t
            for i in range(4):
                a = ve.scalar_tensor_tensor(xlv[:, i, :], ps.ap[:, i * 256:(i + 1) * 256], s.ap[:, 12 + i:13 + i],
                    xlv[:, i, :], ALU.mult, ALU.add, w=(t, ri))
            units.give(ps, a)
            sm.give(s, a)
            t = yield from layernorm(xlv, xlv, a)
            x1 = xl
            x1v = xlv
            yield t
            t1 = affine(x1v, g1_r, be1_r, t, w_small)
            yield t1
            yield at_gate.free
            yield room(f=3, r=4)
            at_gate.enter()
            hh, hl, th1, th2 = load_h(g)
            mg = [ft.take(), ft.take()]
            d = ft.take()
            x1h, x1l, a, b, _ = yield from turned(x1v, t1)
            yield (b, th2)
            for k in range(2):
                yield units.has()
                ps = units.take()
                for i in (2 * k, 2 * k + 1):
                    q = slice((i % 2) * 512, (i % 2) * 512 + 512)
                    three(ps.ap[:, q], [(hh.ap[:, c * 512 + i * 128:c * 512 + i * 128 + 128],
                                         hl.ap[:, c * 512 + i * 128:c * 512 + i * 128 + 128],
                                         a12_h[:, c, :], a12_l[:, c, :]) for c in range(2)], True, False,
                          (th1, th2, *A12_t, *ps.last))
                    q = slice((i % 2) * 512 + 256, (i % 2) * 512 + 512)
                    t = three(ps.ap[:, q], [(x1h.ap[:, c * 512 + i * 128:c * 512 + i * 128 + 128],
                                             x1l.ap[:, c * 512 + i * 128:c * 512 + i * 128 + 128],
                                             wg1_h[:, c, :], wg1_l[:, c, :]) for c in range(2)], False, True, (a, b))
                yield t
                pv = v3(ps.ap, 2, 512)
                for n in (1, 0):
                    to = v3(mg[n].ap, 4, 256)[:, 2 * k:2 * k + 2, :]
                    m = ve.tensor_tensor(to, pv[:, :, n * 256:n * 256 + 256], bias_mg[:,
                        n * 256:n * 256 + 256].unsqueeze(1).to_broadcast([128, 2, 256]), ALU.add, w=(t, bmg_t,
                            *mg[n].last))
                units.give(ps, m)
            for q in (hh, hl, x1h, x1l):
                rt.give(q, t)
            yield m
            mo, gt = mg
            th = act.activation(gt.ap, gt.ap, ACT.Tanh, scale=0.5, w=(m,))
            td = po.tensor_tensor(d.ap, x1.ap, mo.ap, ALU.subtract, w=(m, *d.last))
            yield td
            ts = ve.tensor_tensor(mo.ap, x1.ap, mo.ap, ALU.add, w=(td,))
            ft.give(x1, ts)
            u = ve.scalar_tensor_tensor(d.ap, gt.ap, 1.0, d.ap, ALU.add, ALU.mult, w=(th, td))
            ft.give(gt, u)
            r = ve.scalar_tensor_tensor(mo.ap, d.ap, 0.5, mo.ap, ALU.mult, ALU.add, w=(u, ts))
            ft.give(d, r)
            at_gate.leave()
            x2 = mo
            x2v = v3(x2.ap, 4, 256)
            t = yield from layernorm(x2v, x2v, r)
            yield t
            t2 = affine(x2v, g2_r, be2_r, t)
            yield t2
            yield at_ff.free
            at_ff.enter()
            x2h, x2l, a, b, t = yield from turned(x2v, t2)
            tb = po.tensor_tensor(x2v, x2v, b2_r.unsqueeze(1).to_broadcast([128, 4, 256]), ALU.add, w=(t,))
            yield b
            done = {}
            yield from ff(x2h.ap, x2l.ap, WA, ACT.Silu, b1_c, done, a, b)
            rt.give(x2h, done["x"])
            rt.give(x2l, done["x"])
            at_ff.leave()
            o = done["o"]
            r = ve.tensor_tensor(x2.ap, x2.ap, o.ap, ALU.add, w=(done["t"], tb))
            units.give(o, r)
            ff_done[g] = done["t"]
            t = yield from layernorm(x2v, x2v, r)
            yield t
            t = affine(x2v, g3_r, be3_r, t)
            yield lambda: pay.idle and len(ft.idle) >= 4 and at_tail[0] == g
            p = pay.take()
            pv = p.ap
            x, tk, df = ft.take(), ft.take(), ft.take()
            xv = v3(x.ap, 4, 256)
            ld = dma(sp, ft_sem[id(x)], xv, tok_rows(io["x"], g), w=(*x.last,))
            yield t
            t = yield from layernorm(x2v, x2v, t)
            tn = ve.tensor_tensor(pv[:, :, 0:256], x2v, xv, ALU.add, w=(t, ld, *p.last))
            ft.give(x2, tn)
            ft.give(x, tn)
            yield sm.has(2)
            s = sm.take()
            mv = v3(s.ap[:, 0:8], 4, 2)
            t, _ = stats(pv[:, :, 0:256], mv, tn, *s.last)
            yield t
            r = rsqrt(s.ap[:, 12:16], mv[:, :, 1], s.ap[:, 8:12], t)
            b = po.tensor_tensor(s.ap[:, 16:20], s.ap[:, 12:16], s.ap[:, 12:16], ALU.mult, w=(r,))
            b = po.tensor_tensor(s.ap[:, 20:24], s.ap[:, 16:20], mv[:, :, 1], ALU.mult, w=(b,))
            b = rsqrt(s.ap[:, 24:28], s.ap[:, 20:24], s.ap[:, 28:32], b)
            b = po.tensor_tensor(s.ap[:, 32:36], s.ap[:, 24:28], s.ap[:, 12:16], ALU.mult, w=(b,))
            yield b
            t1 = ve.tensor_copy(pv[:, :, 256], mv[:, :, 0], w=(t,))
            t2 = ve.tensor_copy(pv[:, :, 257], s.ap[:, 12:16], w=(r,))
            t3 = ve.tensor_copy(pv[:, :, 258], s.ap[:, 32:36], w=(b,))
            t4 = ve.tensor_copy(pv[:, :, 260].bitcast(U), ids[:, c4].bitcast(U), w=(C["pool"],))
            t4 = ve.memset(pv[:, :, 261:264], 0.0)
            tkv = v3(tk.ap, 4, 256)
            t = norm(tkv, pv[:, :, 0:256], mv[:, :, 0], s.ap[:, 32:36], b, *tk.last)
            tq = po.tensor_tensor(df.ap, pv[:, :, 0:256], tkv, ALU.add, w=(t, *df.last))
            od = dma(sp, ft_sem[id(df)], tok_rows(d_x1, g), v3(df.ap, 4, 256), w=(tq,), store=True)
            ft.give(df, od)
            sm.give(s, t, t2, t3)
            x1_default.append(od)
            yield t
            yield room(f=1, u=1)
            ps = units.take()
            tT = ft.take()
            tt = transposes(ps.ap, tkv, t, *ps.last)
            ft.give(tk, tt, tq)
            yield tt
            for c in range(2):
                ta = act.activation(tT.ap[:, c * 512:(c + 1) * 512], ps.ap[:, c * 512:(c + 1) * 512], ACT.Identity,
                    scale=lng_c[:, c:c + 1], bias=lnb_c[:, c:c + 1], w=(tt, *tT.last))
            units.give(ps, ta)
            at_tail[0] += 1
            yield ta
            yield sm.has()
            s = sm.take()
            su = s.ap[:, 0:4].bitcast(U)
            lx, t_s, t_w = yield from route(0, g, 512, tT.ap, gwT, su, pv[:, :, 259], ta, *s.last)
            ft.give(tT, lx)
            yield t_w
            for i in range(4):
                tz = scatter(scat_sem[id(p)], d_p1, su[:, i:i + 1], pv[:, i, :], E * 512 - 1, w=(t_s, t_w, t1, t2, t3,
                    t4, filled))
            pay.give(p, tz)
            sm.give(s, tz)
            sent[0].append(tz)

        at_gate, at_ff, at_tail = Turn(1), Turn(2), [0]
        halo = sb("halo", [32, 5, 256])
        halo_free = []
        ff_done = {}
        x1_default = []
        W0, job_done = {}, {}

        def prefetch0(n):
            w = ff_done.values() if n == 1 else ((job_done[(512, n - 2, 0)],) if n > 1 else ())
            W0[n] = ff_weights((n + 1) % 2, io["wi"][n], io["wo"][n], *w,
                               w2_waits=[x for b in borrowed for x in b.last] if n == 0 else ())

        def reclaim(when):
            yield when
            for b in borrowed:
                yield lambda: b in rt.idle
                rt.idle.remove(b)

        def early0():
            yield from reclaim(lambda: at_window[0] >= G - 2)
            prefetch0(0)

        gens = [second(g) for g in range(G)]
        run(gens[:G - 3] + [early0()] + gens[G - 3:], 5, "second")

        for t in lent[3:5]:
            t.last = list(ff_done.values())
            rt.idle.append(t)

        def job(e_, i, cap, src, ready, WF, func, bias, dst, gate_only):
            yield pay.has()
            p = pay.take()
            pv = p.ap
            r0 = e_ * cap + i * 512
            ld = dma(sp, pay_sem[id(p)], pv, src[r0:r0 + 512, :].rearrange("(t p) n -> p t n", p=128), w=(*p.last,
                *ready))
            yield ld
            yield lambda: len(ft.idle) >= 2 and at_ff.free()
            at_ff.enter()
            tk = ft.take()
            tkv = v3(tk.ap, 4, 256)
            sc = 258 if not gate_only else 257
            for k in range(4):
                t = ve.tensor_scalar(tkv[:, k, :], pv[:, k, 0:256], pv[:, k, 256:257], pv[:, k, sc:sc + 1],
                    ALU.subtract, ALU.mult, w=(ld, *tk.last))
            yield t
            if gate_only:
                th, tl, a, b, tt = yield from turned(tkv, t)
            else:
                yield room(f=1, r=2, u=1)
                th, tl, f = rt.take(), rt.take(), ft.take()
                ps = units.take()
                tt = transposes(ps.ap, tkv, t, *ps.last)
                yield tt
                for d in (th, f):
                    for c in range(2):
                        a = act.activation(d.ap[:, c * 512:(c + 1) * 512], ps.ap[:, c * 512:(c + 1) * 512],
                            ACT.Identity, scale=lng_c[:, c:c + 1], bias=lnb_c[:, c:c + 1], w=(tt, *d.last))
                units.give(ps, a)
                yield a
                b = ve.tensor_tensor(tl.ap, f.ap, f32(th.ap), ALU.subtract, w=(a, *tl.last))
                ft.give(f, b)
            ft.give(tk, tt)
            yield b
            W = WF()
            done = {}
            yield from ff(th.ap, tl.ap, W, func, bias, done, a, b)
            rt.give(th, done["x"])
            rt.give(tl, done["x"])
            at_ff.leave()
            o = done["o"]
            job_done[(cap, e_, i)] = done["t"]
            yield room(f=1, s=2)
            q = ft.take()
            qv = v3(q.ap, 4, 256)
            s = sm.take()
            mv = v3(s.ap[:, 0:8], 4, 2)
            if gate_only:
                t = ve.tensor_tensor(qv, v3(o.ap, 4, 256), W["b2"].unsqueeze(1).to_broadcast([128, 4, 256]), ALU.add,
                    w=(done["t"], W["tb2"], *q.last))
                units.give(o, t)
                W["free_b2"].last.append(t)
                W["added"] += 1
                t, _ = stats(qv, mv, t, *s.last)
                gt = pv[:, :, 259]
                yield t
                b = po.tensor_tensor(s.ap[:, 16:20], gt, gt, ALU.mult, w=(ld,))
                b = po.tensor_tensor(s.ap[:, 20:24], s.ap[:, 16:20], mv[:, :, 1], ALU.mult, w=(b, t))
                b = rsqrt(s.ap[:, 24:28], s.ap[:, 20:24], s.ap[:, 28:32], b)
                b = po.tensor_tensor(s.ap[:, 12:16], s.ap[:, 24:28], gt, ALU.mult, w=(b,))
            else:
                for k in range(4):
                    t = ve.tensor_scalar(qv[:, k, :], pv[:, k, 0:256], pv[:, k, 256:257], pv[:, k, 257:258],
                        ALU.subtract, ALU.mult, w=(*q.last,))
                for k in range(4):
                    t = ve.scalar_tensor_tensor(qv[:, k, :], o.ap[:, k * 256:(k + 1) * 256], pv[:, k, 259:260], qv[:,
                        k, :], ALU.mult, ALU.add, w=(done["t"], t))
                units.give(o, t)
                t, _ = stats(qv, mv, t, *s.last)
                yield t
                b = rsqrt(s.ap[:, 12:16], mv[:, :, 1], s.ap[:, 8:12], t)
            yield b
            t = norm(qv, qv, mv[:, :, 0], s.ap[:, 12:16], b)
            sm.give(s, t)
            yield t
            t = po.tensor_tensor(qv, qv, pv[:, :, 0:256], ALU.add, w=(t,))
            yield sm.has()
            s = sm.take()
            su = s.ap[:, 0:4].bitcast(U)
            tn = ve.tensor_copy(su, pv[:, :, 260].bitcast(U), w=(ld, *s.last))
            pay.give(p, t, tn)
            yield t
            for k in range(4):
                z = scatter(scat_sem[id(q)], dst, su[:, k:k + 1], qv[:, k, :], T - 1, w=(t, tn, *defaults[cap]))
            ft.give(q, z)
            sm.give(s, z)
            defaults[(cap, "last")].append(z)

        defaults = {512: list(x1_default), (512, "last"): [], (1024, "last"): []}

        def one0(n):
            yield lambda: n in W0
            yield from job(n, 0, 512, d_p1, sent[0], lambda: W0[n], ACT.Gelu, None, d_x1, False)
            if n + 2 < E:
                prefetch0(n + 2)

        prefetch0(1)
        wq_h, wq_l = v3(small[:, 0:1536], 2, 768), v3(small[:, 1536:3072], 2, 768)
        def layer1():
            st = stage.take()
            ld = dma(sp, stage_sem[id(st)], v3(st.ap[:, 0:1536], 2, 768), chunks(io["WqkvT"], 768), w=(*st.last,))
            a, b = split(small[:, 0:1536], small[:, 1536:3072], st.ap[:, 0:1536], ld,
                *ff_done.values())
            stage.give(st, a, b)
            wout, wout_v, t_wout = load_f("WoutT")
            return b, wout, wout_v, t_wout

        wq_t, wout, wout_v, t_wout = layer1()
        if stop != "A":
            run([one0(n) for n in range(E)], 3, "experts0")

        for t in lent[3:5]:
            rt.idle.remove(t)
        free2 = [x for t in lent[3:5] for x in t.last]
        kw = [(v3(small[:, 3072 + i * 1032:3072 + i * 1032 + 516], 2, 258),
               v3(small[:, 3072 + i * 1032 + 516:3072 + (i + 1) * 1032], 2, 258)) for i in range(2)]

        def attn1(bt):
            grp = []
            yield lambda: at_qkv[0] == bt
            kvps = None
            for j in range(2):
                g = 2 * bt + j
                yield room(f=4, r=6)
                x, ld = load_x(d_x1, g, *defaults[(512, "last")])
                xv = v3(x.ap, 4, 256)
                xn = ft.take()
                yield ld
                t = yield from layernorm(v3(xn.ap, 4, 256), xv, ld, *xn.last)
                yield t
                xh, xl, a, b, t = yield from turned(v3(xn.ap, 4, 256), t)
                ft.give(xn, t)
                yield b
                yield room(f=1, r=2, u=1)
                ps = units.take()
                q, qh, ql = ft.take(), rt.take(), rt.take()
                for oc in range(2):
                    t = wide(ps.ap[:, oc * 512:(oc + 1) * 512], wq_h, wq_l, xh.ap, xl.ap, 512, (a, b, wq_t, *ps.last),
                        oc)
                yield t
                tq = ve.tensor_scalar(q.ap, ps.ap, 0.0, 1e-6, ALU.max, ALU.add, w=(t, *q.last))
                units.give(ps, tq)
                yield tq
                q1, q2 = split(qh.ap, ql.ap, q.ap, tq, *qh.last, *ql.last, engine="p")
                ft.give(q, q1, q2)
                grp.append((x, xv, qh, ql, q1, q2))
                for k in range(2):
                    yield room(f=1, r=2, u=1)
                    ps = units.take()
                    f, fh, fl = ft.take(), rt.take(), rt.take()
                    for i in (2 * k, 2 * k + 1):
                        t = three(ps.ap[:, (i % 2) * 512:(i % 2) * 512 + 512],
                                  [(xh.ap[:, c * 512 + i * 128:c * 512 + i * 128 + 128],
                                    xl.ap[:, c * 512 + i * 128:c * 512 + i * 128 + 128],
                                    wq_h[:, c, 256:768], wq_l[:, c, 256:768]) for c in range(2)], True, True,
                                  (*ps.last,))
                    if k == 1:
                        rt.give(xh, t)
                        rt.give(xl, t)
                    yield t
                    pv, fv, hv, lv = (v3(z.ap, 2, 512) for z in (ps, f, fh, fl))
                    t1 = ve.tensor_scalar(fv[:, :, 0:256], pv[:, :, 0:256], 0.0, 1e-6, ALU.max, ALU.add, w=(t, *f.last))
                    t2 = act.activation(fv[:, :, 256:512], pv[:, :, 256:512], ACT.Copy, w=(t1,))
                    units.give(ps, t1, t2)
                    yield t2
                    a1 = act.activation(fh.ap, f.ap, ACT.Copy, w=(t1, t2, *fh.last))
                    yield a1
                    b1 = (po, ve)[k].tensor_tensor(fl.ap, f.ap, f32(fh.ap), ALU.subtract, w=(a1, *fl.last))
                    ft.give(f, a1, b1)
                    yield b1
                    if kvps is None:
                        yield units.has(2)
                        kvps = units.take()
                    for i in range(2):
                        st0 = j == 0 and k == 0 and i == 0
                        last = j == 1 and k == 1 and i == 1
                        for c in range(2):
                            vh, vl = (z[:, i, 256 + c * 128:256 + c * 128 + 128] for z in (hv, lv))
                            three(kvps.ap[:, c * 256:(c + 1) * 256], [(vh, vl, hv[:, i, 0:256], lv[:, i, 0:256])],
                                  st0 and c == 0, last, (a1, b1, *kvps.last))
                        for c in range(2):
                            kh_, kl_ = (z[:, i, c * 128:c * 128 + 128] for z in (hv, lv))
                            o = kvps.ap[:, 512 + 2 * c:514 + 2 * c]
                            pe.matmul(o, kh_, oner[:, :], start=st0 and c == 0, stop=False, skip_group_check=True,
                                w=(C["oner"],))
                            t = pe.matmul(o, kl_, oner[:, :], start=False, stop=last, skip_group_check=True)
                    rt.give(fh, t)
                    rt.give(fl, t)
            at_qkv[0] += 1
            yield t
            yield ft.has()
            kvf = ft.take()
            kt = act.activation(kvf.ap[:, 0:512], kvps.ap[:, 0:512], ACT.Copy, w=(t, *kvf.last))
            kt2 = act.activation(kvf.ap[:, 512:516], kvps.ap[:, 512:516], ACT.Copy)
            units.give(kvps, kt2)
            yield kt2
            yield lambda: units.idle and (bt < 2 or bt - 2 in kw_free)
            ps = units.take()
            t = mm256(ps.ap, v3(kvf.ap[:, 0:512], 2, 256), wout_v, (kt, t_wout, *ps.last))
            kh, kl = kw[bt % 2]
            yield t
            kf = kw_free[bt - 2] if bt > 1 else ()
            a, b = evac(kh[:, :, 0:256], kl[:, :, 0:256], two(ps.ap), t, *kf, *free2)
            units.give(ps, a, b)
            kc = v3(kvf.ap[:, 512:516], 2, 2)
            a2, b2 = split(kh[:, :, 256:258], kl[:, :, 256:258], kc, kt2)
            ft.give(kvf, a2, b2, t)
            yield b2
            for j in range(2):
                g = 2 * bt + j
                x, xv, qh, ql, q1, q2 = grp[j]
                yield room(f=1, s=2)
                r = ft.take()
                rv = v3(r.ap, 4, 256)
                s = sm.take()
                for k in range(2):
                    yield units.has()
                    ps = units.take()
                    for i in (2 * k, 2 * k + 1):
                        t = three(ps.ap[:, (i % 2) * 512:(i % 2) * 512 + 258],
                                  [(qh.ap[:, c * 512 + i * 128:c * 512 + i * 128 + 128],
                                    ql.ap[:, c * 512 + i * 128:c * 512 + i * 128 + 128],
                                    kh[:, c, :], kl[:, c, :]) for c in range(2)], True, True,
                                  (q1, q2, a, b, a2, b2, *ps.last))
                    yield t
                    pv = v3(ps.ap, 2, 512)
                    z0 = s.ap[:, 4 * k:4 * k + 2]
                    z1 = s.ap[:, 4 * k + 2:4 * k + 4]
                    d = ve.tensor_scalar(z0, pv[:, :, 256], 1e-6, None, ALU.add, w=(t, *s.last))
                    d = ve.reciprocal(z1, z0, w=(d,))
                    for i in range(2):
                        m = ve.scalar_tensor_tensor(rv[:, 2 * k + i, :], pv[:, i, 0:256], z1[:, i:i + 1], bout_r,
                            ALU.mult, ALU.add, w=(d, w_small, *r.last))
                    units.give(ps, m)
                rt.give(qh, t)
                rt.give(ql, t)
                sm.give(s, m)
                if j == 1:
                    kw_free[bt] = (t,)
                yield m
                t = yield from layernorm(rv, rv, m)
                yield pay.has()
                p = pay.take()
                pv = p.ap
                tn = ve.tensor_tensor(pv[:, :, 0:256], rv, xv, ALU.add, w=(t, *p.last))
                ft.give(r, tn)
                ft.give(x, tn)
                od = dma(sp, out_sem[id(p)], tok_rows(out, g), pv[:, :, 0:256], w=(tn,), store=True)
                out_default.append(od)
                yield sm.has(2)
                s = sm.take()
                mv = v3(s.ap[:, 0:8], 4, 2)
                t, _ = stats(pv[:, :, 0:256], mv, tn, *s.last)
                yield t
                rr = rsqrt(s.ap[:, 12:16], mv[:, :, 1], s.ap[:, 8:12], t)
                yield rr
                c4 = slice(4 * g, 4 * g + 4)
                t1 = ve.tensor_copy(pv[:, :, 256], mv[:, :, 0], w=(t,))
                t4 = ve.tensor_copy(pv[:, :, 260].bitcast(U), ids[:, c4].bitcast(U))
                t4 = ve.memset(pv[:, :, 261:264], 0.0)
                t4 = ve.memset(pv[:, :, 258], 0.0)
                t2 = ve.tensor_copy(pv[:, :, 257], s.ap[:, 12:16], w=(rr,))
                yield ft.has(2)
                xn = ft.take()
                tT = ft.take()
                t = norm(v3(xn.ap, 4, 256), pv[:, :, 0:256], mv[:, :, 0], s.ap[:, 12:16], rr, *xn.last)
                sm.give(s, t, t2)
                yield t
                yield units.has()
                ps = units.take()
                tt = transposes(ps.ap, v3(xn.ap, 4, 256), t, *ps.last)
                ft.give(xn, tt)
                yield tt
                ta = act.activation(tT.ap, ps.ap, ACT.Copy, w=(tt, *tT.last))
                units.give(ps, ta)
                yield ta
                yield sm.has(2)
                s = sm.take()
                su = s.ap[:, 0:4].bitcast(U)
                lx, t_s, t_w = yield from route(1, g, 1024, tT.ap, wgT, su, pv[:, :, 259], ta, *s.last)
                ft.give(tT, lx)
                yield t_w
                for i in range(4):
                    tz = scatter(scat_sem[id(p)], d_p2, su[:, i:i + 1], pv[:, i, :], E * 1024 - 1, w=(t_s, t_w, t1,
                        t2, t4))
                pay.give(p, tz, od)
                sm.give(s, tz)
                sent[1].append(tz)

        at_qkv, kw_free = [0], {}
        out_default = []
        if stop not in ("A", "A1", "B"):
            for b in borrowed:
                b.last = [job_done[(512, 6, 0)]]
            rt.idle += borrowed
            b1e = sb("b1e", [128, 64])
            b1e_t = dma(sp, s_b1, b1e[:, :], io["eb1_c"])
            b2e = [Tile(rows[:, i, :], "b2e") for i in range(2)]
            s_b2 = [new_sem(f"s_b2{i}") for i in range(2)]
            W1 = {}

            def prefetch1(n):
                w = (job_done[(1024, n - 2, 0)], job_done[(1024, n - 2, 1)]) if n > 1 else (job_done[(512, 6 + n, 0)],)
                W = ff_weights((n + 1) % 2, io["w1"][n], io["w2"][n], *w,
                               w2_waits=[x for b in borrowed for x in b.last] if n == 0 else ())
                bt = b2e[n % 2]
                W["b2"], W["free_b2"], W["added"] = bt.ap, bt, 0
                W["tb2"] = dma(sp, s_b2[n % 2], bt.ap, io["eb2"][n].partition_broadcast(128), w=(*bt.last, *w))
                W1[n] = W

            def early1():
                yield from reclaim(lambda: at_qkv[0] == 8)
                prefetch1(0)

            prefetch1(1)
            run([attn1(bt) for bt in range(7)] + [early1(), attn1(7)], 3, "attn1")
            ft.give(wout, *[])
            small_free = [t for v in kw_free.values() for t in v]
            for t in lent:
                t.last = small_free
                rt.idle.append(t)
            defaults[1024] = list(out_default)
            def one1(n, i):
                yield lambda: n in W1
                yield from job(n, i, 1024, d_p2, sent[1], lambda: W1[n], ACT.Relu,
                               b1e[:, 8 * n:8 * n + 8], out, True)
                if i == 1 and n + 2 < E:
                    yield lambda: W1[n]["added"] == 2
                    prefetch1(n + 2)

            act.activation(cols[:, 61:62], cols[:, 60:61], ACT.Copy, w=(b1e_t,))
            run([one1(n, i) for n in range(E) for i in range(2)], 3, "experts1")

        if stop:
            t = dma(sp, s_b1, out, d_x1, w=(*stores,), store=True)

        for q in (pe, act, ve, po, sp):
            q.number()
        block = ctx.enter_context(nc.Block())

        @block.tensor
        def _(eng):
            pe.write(eng)

        @block.scalar
        def _(eng):
            act.write(eng)

        @block.vector
        def _(eng):
            ve.write(eng)

        @block.gpsimd
        def _(eng):
            po.write(eng)

        @block.sync
        def _(eng):
            sp.write(eng)
            for sem in {id(t.sem): t.sem for t in stores}.values():
                eng.wait_ge(sem, landed[id(sem)])


def layouts(i):
    import numpy as np

    def t(a):
        return np.ascontiguousarray(np.asarray(a).T)

    def c(a):
        return np.ascontiguousarray(np.asarray(a).reshape(-1, 128).T)

    a = {k[8:]: np.asarray(v) for k, v in i.items() if k.startswith("L0_attn_")}
    f = {k[7:]: np.asarray(v) for k, v in i.items() if k.startswith("L0_ffn_")}
    q = {k[8:]: np.asarray(v) for k, v in i.items() if k.startswith("L1_attn_")}
    e = {k[7:]: np.asarray(v) for k, v in i.items() if k.startswith("L1_ffn_")}
    wg = t(a["Wg"])
    return {
        "x": a["x"].reshape(8192, 256), "P": a["P"], "mem_b": a["mem_b"], "bi": a["bi"],
        "mem_b_c": c(a["mem_b"]), "bi_c": c(a["bi"]), "bl1_c": c(a["bl1"]), "bl2_c": c(a["bl2"]), "bo_c": c(a["bo"]),
        "b1_c": c(a["b1"]), "ln_g_c": c(f["ln_gamma"]), "ln_b_c": c(f["ln_beta"]),
        "fgate": a["fgate"], "lrate": a["lrate"],
        "g1": a["g1"], "be1": a["be1"], "g2": a["g2"], "be2": a["be2"], "g3": a["g3"], "be3": a["be3"],
        "b2": a["b2"], "bo": a["bo"], "bg": a["bg"], "b_out": q["b_out"],
        "Wi": a["Wi"], "WiT": t(a["Wi"]), "Wl1T": t(a["Wl1"]), "Wl2T": t(a["Wl2"]), "WoT": t(a["Wo"]),
        "mem_W": a["mem_W"], "mem_WT": t(a["mem_W"]),
        "Wg1T": np.ascontiguousarray(wg[0:256]), "Wg2T": np.ascontiguousarray(wg[256:512]),
        "W1T": t(a["W1"]), "W2T": t(a["W2"]),
        "gate_wT": t(f["gate_weight"]), "wi": f["wi"], "wo": f["wo"],
        "WqkvT": t(q["W_qkv"]), "WoutT": t(q["W_out"]),
        "wg": e["wg"], "w1": e["w1"], "w2": e["w2"],
        "eb1_c": c(e["b1"]), "eb2": e["b2"],
    }


def kernel(**inputs):
    import numpy as np
    import concourse.bacc as bacc
    from concourse.bass_utils import run_bass_kernel_spmd

    nc = bacc.Bacc("TRN2", target_bir_lowering=False, num_devices=1)
    arrays, io = {}, {}
    for name, a in layouts(inputs).items():
        a = np.ascontiguousarray(a)
        arrays["in_" + name] = a
        io[name] = nc.dram_tensor("in_" + name, a.shape, mybir.dt.from_np(a.dtype), kind="ExternalInput").ap()
    io["out"] = nc.dram_tensor("out_x", (T, H), F, kind="ExternalOutput").ap()
    build(nc, io)
    r = run_bass_kernel_spmd(nc, [arrays], core_ids=[0])
    return r.results[0]["out_x"].reshape(8, 1024, 256)
```

```python
from contextlib import ExitStack

import concourse.bass as bass
from concourse import mybir

F = mybir.dt.float32
R = mybir.dt.float32r
BF = mybir.dt.bfloat16
U = mybir.dt.uint32
I = mybir.dt.int32
ALU = mybir.AluOpType
ACT = mybir.ActivationFunctionType
AX = mybir.AxisListType

T = 8192
H = 256
G = 16
E = 8
PW = 264
EPS = 1e-5
N_MEM = 8 * 1034
NEG = -1.0e30
FAR = 1.0e6


class Token:

    def __init__(self, queue, at):
        self.queue, self.at = queue, at

    def when(self):
        return self.queue.end[self.at]


class Landed:

    def __init__(self, sem, value, end):
        self.sem, self.value, self.end = sem, value, end

    def when(self):
        return self.end


def wide_of(ap):
    n = 1
    for k in ap.shape[1:]:
        n *= k
    return n


class Engine:

    def __init__(self, sem, per=1.0, fixed=60):
        self.sem, self.ops, self.marked = sem, [], set()
        self.per, self.fixed, self.clock, self.end = per, fixed, 0, []

    def put(self, fn, w, cost, sem=None):
        for t in w:
            if isinstance(t, Token):
                t.queue.marked.add(t.at)
        assert all(isinstance(t, (Token, Landed)) for t in w)
        self.ops.append((fn, w, sem))
        start = max([self.clock] + [t.when() + 60 for t in w])
        self.clock = start + cost
        self.end.append(self.clock)
        return Token(self, len(self.ops) - 1)

    def cost(self, out, k=1.0):
        return self.fixed + self.per * k * wide_of(out)

    def matmul(self, out, lhsT, rhs, w=(), **k):
        c = wide_of(out) * (0.42 if rhs.dtype != F else 1.68)
        return self.put(lambda e: e.matmul(out, lhsT, rhs, **k), w, c)

    def transpose(self, out, in_, identity, w=()):
        return self.put(lambda e: e.transpose(out, in_, identity), w, wide_of(out) * 0.84)

    def activation(self, out, in_, func, w=(), **k):
        return self.put(lambda e: e.activation(out, in_, func, **k), w, self.cost(out))

    def tensor_tensor(self, out, in0, in1, op, w=()):
        return self.put(lambda e: e.tensor_tensor(out, in0, in1, op), w, self.cost(out, 80 if op == ALU.pow else 1))

    def tensor_scalar(self, out, in0, s1, s2, op0, op1=ALU.bypass, w=()):
        return self.put(lambda e: e.tensor_scalar(out, in0, s1, s2, op0, op1), w, self.cost(out))

    def scalar_tensor_tensor(self, out, in0, s, in1, op0, op1, w=()):
        return self.put(lambda e: e.scalar_tensor_tensor(out, in0, s, in1, op0, op1), w, self.cost(out, 1.2))

    def tensor_reduce(self, out, in_, axis, op, w=()):
        return self.put(lambda e: e.tensor_reduce(out, in_, axis, op), w, self.cost(in_))

    def tensor_copy(self, out, in_, w=()):
        return self.put(lambda e: e.tensor_copy(out, in_), w, self.cost(out, 0.5))

    def reciprocal(self, out, in_, w=()):
        return self.put(lambda e: e.reciprocal(out, in_), w, self.cost(out))

    def memset(self, out, value, w=()):
        return self.put(lambda e: e.memset(out, value), w, self.cost(out, 0.5))

    def bn_stats(self, out, in_, w=()):
        return self.put(lambda e: e.bn_stats(out, in_), w, self.cost(in_))

    def bn_aggr(self, out, in_, w=()):
        return self.put(lambda e: e.bn_aggr(out, in_), w, 75)

    def iota(self, out, w=(), **k):
        return self.put(lambda e: e.iota(out, **k), w, self.cost(out))

    def affine_select(self, w=(), **k):
        return self.put(lambda e: e.affine_select(**k), w, 300)

    def number(self):
        self.count, n = [], 0
        for i in range(len(self.ops)):
            n += i in self.marked
            self.count.append(n)

    def write(self, eng):
        seen = {}
        for i, (fn, w, sem) in enumerate(self.ops):
            need = {}
            for t in w:
                s, v = (t.queue.sem, t.queue.count[t.at]) if isinstance(t, Token) else (t.sem, t.value)
                if v > max(seen.get(id(s), 0), need.get(id(s), (None, 0))[1]):
                    need[id(s)] = (s, v)
            for k, (s, v) in need.items():
                eng.wait_ge(s, v)
                seen[k] = v
            ins = fn(eng)
            if sem is not None:
                ins.then_inc(sem, 16)
            elif i in self.marked:
                ins.then_inc(self.sem, 1)


class Tile:

    def __init__(self, ap, name):
        self.ap, self.last, self.held, self.name = ap, [], False, name


class Store:

    def __init__(self, tiles):
        self.idle = list(tiles)
        self.name = tiles[0].name

    def take(self):
        assert self.idle, "no tile left: " + self.name
        t = self.idle.pop(0)
        t.held = True
        return t

    def give(self, t, *last):
        assert t.held
        t.held = False
        t.last = list(last)
        self.idle.append(t)

    def has(self, n=1):
        return lambda: len(self.idle) >= n


class Turn:

    def __init__(self, n):
        self.n = n

    def free(self):
        return self.n > 0

    def enter(self):
        assert self.n > 0
        self.n -= 1

    def leave(self):
        self.n += 1


def ready_at(y):
    if y is None:
        return 0
    return y.when() if isinstance(y, (Token, Landed)) else max(t.when() for t in y)


def run(gens, live_max, name=""):
    live, i = [], 0
    while live or i < len(gens):
        while i < len(gens) and len(live) < live_max:
            live.append([0, None, gens[i], i])
            i += 1
        able = [x for x in live if x[1] is None or x[1]()]
        assert able, "all wait: " + name
        x = min(able, key=lambda x: (x[0], x[3]))
        x[1] = None
        try:
            y = next(x[2])
            if callable(y):
                x[1] = y
            else:
                x[0] = ready_at(y)
        except StopIteration:
            live.remove(x)


KA, KB, KC, KD = 5, 3, 6, 3


def build(nc, io, stop=None):
    ctx = ExitStack()
    with ctx:
        def sb(name, shape, dt=F):
            return ctx.enter_context(nc.sbuf_tensor(name, shape, dt))

        def new_sem(name):
            return ctx.enter_context(nc.semaphore(name))

        def dram(name, shape, dt=F):
            return nc.dram_tensor(name, shape, dt, kind="Internal").ap()

        pe, act, ve, po, sp = (Engine(new_sem("q_" + n), per, fixed) for n, per, fixed in (
            ("pe", 0, 0), ("act", 0.83, 100), ("dve", 1.05, 60), ("pool", 2.1, 130), ("sp", 0, 0)))

        landed = {}
        stores = []

        def sent_on(sem, store, end):
            landed[id(sem)] = landed.get(id(sem), 0) + 16
            t = Landed(sem, landed[id(sem)], end)
            if store:
                stores.append(t)
            return t

        def dma(queue, sem, dst, src, w=(), store=False):
            queue.put(lambda e: e.dma_start(dst, src), w, 60, sem)
            return sent_on(sem, store, queue.clock + 4500)

        def scatter(sem, dst, idx, src, bound, w=()):
            po.put(lambda e: e.indirect_dma_start(dst, bass.IndirectOffsetOnAxis(idx, 0), src, None,
                                                  bounds_check=bound, oob_is_err=False), w, 1040, sem)
            return sent_on(sem, True, po.clock + 3000)

        def tiles(name, n, shape, dt=F):
            whole = sb(name, [128, n] + shape, dt)
            return Store([Tile(whole[:, i], name) for i in range(n)])

        d_h = dram("d_h", [G, 128, 2, 1024], R)
        d_p1 = dram("d_p1", [E * 512, PW])
        d_p2 = dram("d_p2", [E * 1024, PW])
        d_x1 = dram("d_x1", [T, H])
        out = io["out"]

        units = Store([Tile(ctx.enter_context(nc.psum_tensor(f"ps{i}", [128, 1024], F))[:, :], "psum")
                       for i in range(4)])

        wslot = [sb(f"wslot{i}", [128, 8192], R) for i in range(2)]
        small = sb("small", [128, 5200], R)
        stage = tiles("stage", 1, [2048])
        ft = tiles("ft", 11, [1024])
        rt = tiles("rt", 9, [1024], R)
        borrowed = [[Tile(wslot[n][:, i * 1024:(i + 1) * 1024], "rt") for i in range(8)] for n in range(2)]
        lent = [Tile(small[:, i * 1024:(i + 1) * 1024], "rt") for i in range(5)]
        tiles_w = ft.idle + rt.idle
        rt.idle += borrowed[0] + borrowed[1]
        pay = tiles("pay", 2, [4, PW])
        ident = sb("ident", [128, 128])
        tri = sb("tri", [128, 128], BF)
        ones = sb("ones", [128, 128], BF)
        oner = sb("oner", [128, 2], R)
        mask = sb("mask", [128, 2, 160])
        desc = sb("desc", [128, 8])
        offs = sb("offs", [128, 2, 8])
        ids = sb("ids", [128, 64], I)
        half = sb("half", [128, 8])
        ecol = sb("ecol", [128, 32])
        mean = sb("mean", [128, 64])
        rstd = sb("rstd", [128, 64])
        ks = sb("ks", [128, 64])
        base = sb("base", [128, 2, 8])
        hsum = sb("hsum", [128, 2, 18])
        cols = sb("cols", [128, 64])
        rows = sb("rows", [128, 12, 256])
        bst = tiles("bst", 3, [4, 6])
        sm = tiles("sm", 8, [64])
        rtl = tiles("rtl", 6, [64])
        ohs = tiles("ohs", 2, [32], BF)

        def setup():
            c = {}
            a = po.memset(ident[:, :], 0.0)
            c["ident"] = po.affine_select(out=ident[:, :], in_=ident[:, :], compare_op=ALU.not_equal, fill=1.0,
                base=0, pattern=[[-1, 128]], channel_multiplier=1, w=(a,))
            a = ve.memset(ones[:, :], 1.0)
            c["tri"] = po.affine_select(out=tri[:, :], in_=ones[:, :], compare_op=ALU.is_gt, fill=0.0, base=0,
                pattern=[[1, 128]], channel_multiplier=-1, w=(a,))
            a = ve.memset(mask[:, :, :], 0.0)
            b = po.affine_select(out=mask[:, :, :], in_=mask[:, :, :], compare_op=ALU.is_ge, fill=NEG, base=32,
                pattern=[[0, 2], [-1, 160]], channel_multiplier=1, w=(a,))
            b = po.affine_select(out=mask[:, :, :], in_=mask[:, :, :], compare_op=ALU.is_ge, fill=NEG, base=-16,
                pattern=[[0, 2], [1, 160]], channel_multiplier=-1, w=(b,))
            c["mask"] = po.memset(mask[:, 1, 0:32], NEG, w=(b,))
            po.iota(desc[:, :], pattern=[[-1, 8]], base=8, channel_multiplier=0, allow_small_or_imprecise_dtypes=True)
            po.iota(offs[:, 0, :], pattern=[[512, 8]], base=0, channel_multiplier=0,
                allow_small_or_imprecise_dtypes=True)
            po.iota(offs[:, 1, :], pattern=[[1024, 8]], base=0, channel_multiplier=0,
                allow_small_or_imprecise_dtypes=True)
            po.iota(ids[:, :], pattern=[[128, 64]], base=0, channel_multiplier=1)
            po.memset(half[:, 0:4], -0.5)
            po.memset(half[:, 4:8], 0.5)
            po.memset(base[:, :, :], 0.0)
            c["pool"] = po.memset(ecol[:, :], 2.718281828459045)
            a = ve.memset(cols[:, 60:61], 0.0)
            c["oner"] = act.activation(oner[:, :], ones[:, 0:2], ACT.Copy, w=(a,))
            return c

        C = setup()

        s_w = new_sem("s_w")

        def load(dst, src, *w):
            return dma(sp, s_w, dst, src, w=(*w,))

        def col(at, name, n=2):
            load(cols[:, at:at + n], io[name])
            return cols[:, at:at + n]

        col(0, "cols_c", 22)
        memb_c, bi_c, bl1_c, bl2_c, bo_c = (cols[:, 2 * i:2 * i + 2] for i in range(5))
        b1_c, lng_c, lnb_c = cols[:, 10:18], cols[:, 18:20], cols[:, 20:22]
        load(cols[:, 22:23], io["fgate"].partition_broadcast(128))
        w_small = load(cols[:, 23:24], io["lrate"].partition_broadcast(128))
        g1_r, be1_r, g2_r, be2_r, g3_r, be3_r, b2_r, bo_r, bg_r, bout_r = (rows[:, i, :] for i in range(10))
        mb_row = sb("mb_row", [1, 512])
        gwT = sb("gwT", [128, 2, 8])
        wgT = sb("wgT", [128, 2, 8])
        s_late = new_sem("s_late")

        def load_late():
            def late(dst, src):
                return dma(sp, s_late, dst, src)

            late(rows[:, 0:10, :].rearrange("p a b -> p (a b)"), io["rows"].partition_broadcast(128))
            late(mb_row[0:1, 0:256], io["mem_b"].partition_broadcast(1))
            late(mb_row[0:1, 256:512], io["bi"].partition_broadcast(1))
            late(gwT[:, :, :], io["gate_wT"].rearrange("(c p) e -> p c e", p=128))
            return late(wgT[:, :, :], io["wg"].rearrange("(c p) e -> p c e", p=128))

        def f32(ap):
            return ap.bitcast(F)

        def v3(ap, a, b):
            return ap.rearrange("p (a b) -> p a b", a=a, b=b)

        def split(hi, lo, src, *w, engine="v"):
            a = act.activation(hi, src, ACT.Copy, w=(*w,))
            put = ve if engine == "v" else po
            b = put.tensor_tensor(lo, src, f32(hi), ALU.subtract, w=(a,))
            return a, b

        def evac(hi, lo, ps, *w):
            a = act.activation(hi, ps, ACT.Copy, w=(*w,))
            b = ve.tensor_tensor(lo, ps, f32(hi), ALU.subtract, w=(a,))
            return a, b

        def evac_(hi, lo, ps, *w):
            n = 512
            a0 = act.activation(hi[:, 0:n], ps[:, 0:n], ACT.Copy, w=(*w,))
            a1 = act.activation(hi[:, n:2 * n], ps[:, n:2 * n], ACT.Copy)
            yield a0
            b0 = ve.tensor_tensor(lo[:, 0:n], ps[:, 0:n], f32(hi[:, 0:n]), ALU.subtract, w=(a0,))
            b1 = ve.tensor_tensor(lo[:, n:2 * n], ps[:, n:2 * n], f32(hi[:, n:2 * n]), ALU.subtract, w=(a1,))
            return a1, b1

        def turned(x, t, lo_hi=True):
            yield room(r=2)
            yield units.has()
            h, l = rt.take(), rt.take()
            ps = units.take()
            tt = transposes(ps.ap, x, t, *ps.last)
            yield tt
            a, b = yield from evac_(h.ap, l.ap, ps.ap, tt, *h.last, *l.last)
            units.give(ps, a, b)
            return h, l, a, b, tt

        def room(f=0, r=0, u=0, s=0):
            return lambda: (len(ft.idle) >= f and len(rt.idle) >= r and len(units.idle) >= u
                            and len(sm.idle) >= s)

        stage_sem = {id(t): new_sem(f"s_st{i}") for i, t in enumerate(stage.idle)}

        def chunks(ap, n):
            return ap.rearrange("(c p) n -> p c n", p=128)

        def ff_weights(slot, w1, w2, *w, w2_waits=()):
            s = wslot[slot]
            parts = dict(w1h=v3(s[:, 0:2048], 2, 1024), w1l=v3(s[:, 2048:4096], 2, 1024),
                         w2h=v3(s[:, 4096:6144], 8, 256), w2l=v3(s[:, 6144:8192], 8, 256))
            st = stage.take()
            t = dma(sp, stage_sem[id(st)], v3(st.ap, 2, 1024), chunks(w1, 1024), w=(*st.last,))
            a, b = split(s[:, 0:2048], s[:, 2048:4096], st.ap, t, *w)
            stage.give(st, a, b)
            parts["t1"] = b
            st2 = stage.take()
            t = dma(sp, stage_sem[id(st2)], v3(st2.ap, 8, 256), chunks(w2, 256), w=(*st2.last,))
            a, b = split(s[:, 4096:6144], s[:, 6144:8192], st2.ap, t, *w, *w2_waits)
            stage.give(st2, a, b)
            parts["t2"] = b
            return parts

        def stats(x, out_mv, *w):
            st = bst.take()
            t = None
            for i in range(4):
                t = ve.bn_stats(st.ap[:, i, :], x[:, i, :], w=(*w, *st.last))
            w = ()
            for i in range(4):
                b = ve.bn_aggr(out_mv[:, i, :], st.ap[:, i, :], w=(t,))
            bst.give(st, b)
            return b, t

        def rsqrt(dst, var, tmp, *w):
            a = po.tensor_scalar(tmp, var, EPS, None, ALU.add, w=(*w,))
            return po.tensor_tensor(dst, tmp, half[:, 0:4], ALU.pow, w=(a, C["pool"]))

        def norm(dst, x, m, r, *w):
            for i in range(4):
                t = ve.tensor_scalar(dst[:, i, :], x[:, i, :], m[:, i:i + 1], r[:, i:i + 1], ALU.subtract, ALU.mult,
                    w=(*w,))
            return t

        def transposes(ps, x, *w, n=4):
            for i in range(n):
                for c in range(2):
                    t = pe.transpose(ps[:, c * 512 + i * 128:c * 512 + i * 128 + 128], x[:, i, c * 128:(c + 1) * 128],
                        ident[:, :], w=(*w, C["ident"]))
            return t

        def to_tokens(ps, xT, *w):
            for i in range(4):
                for c in range(2):
                    t = pe.transpose(ps[:, i * 256 + c * 128:i * 256 + c * 128 + 128], xT[:,
                        c * 512 + i * 128:c * 512 + i * 128 + 128], ident[:, :], w=(*w, C["ident"]))
            return t

        def three(o, pairs, start, stop, w=()):
            ops = []
            for lh, ll, rh, rl in pairs:
                ops += [(lh, rh), (lh, rl), (ll, rh)]
            for j, (a, b) in enumerate(ops):
                t = pe.matmul(o, a, b, start=start and j == 0, stop=stop and j == len(ops) - 1, skip_group_check=True,
                    w=(*w,))
            return t

        def wide(ps, wh, wl, xh, xl, n, w, oc):
            return three(ps, [(wh[:, c, oc * 128:oc * 128 + 128], wl[:, c, oc * 128:oc * 128 + 128],
                               xh[:, c * 512:c * 512 + n], xl[:, c * 512:c * 512 + n]) for c in range(2)],
                         True, True, w)

        def ff(xh, xl, W, func, bias, done, *w):
            o = None

            def second(j, fh, fl, th, tl):
                for i in range(4):
                    for k in range(2):
                        c = 2 * j + k
                        t = three(o.ap[:, i * 256:(i + 1) * 256],
                                  [(fh.ap[:, k * 512 + i * 128:k * 512 + i * 128 + 128],
                                    fl.ap[:, k * 512 + i * 128:k * 512 + i * 128 + 128],
                                    W["w2h"][:, c, :], W["w2l"][:, c, :])],
                                  j == 0 and k == 0 and i % 2 == 0, j == 3 and k == 1,
                                  (th, tl, W["t2"], *o.last))
                rt.give(fh, t)
                rt.give(fl, t)
                return t

            def low(j, f, fh, fl, aa):
                ts = []
                for k in range(2):
                    s = slice(k * 512, (k + 1) * 512)
                    ts.append((ve if (j + k) % 4 else po).tensor_tensor(fl.ap[:, s], f.ap[:, s], f32(fh.ap[:, s]),
                        ALU.subtract, w=(aa[k], *fl.last)))
                ft.give(f, *ts)
                return ts

            acts, lows = [], []
            for j in range(4):
                yield room(f=1, r=2, u=2 if o is None else 1)
                if o is None:
                    o = units.take()
                f, fh, fl = ft.take(), rt.take(), rt.take()
                ps = units.take()
                ts = []
                for k in range(2):
                    ts.append(wide(ps.ap[:, k * 512:(k + 1) * 512], W["w1h"], W["w1l"], xh, xl, 512,
                                   (*w, W["t1"], *ps.last), 2 * j + k))
                last_in = ts[1]
                if acts:
                    q = acts.pop(0)
                    yield q[4][0]
                    lows.append((q[0], q[2], q[3], *low(*q)))
                yield ts[0]
                aa = []
                for k in range(2):
                    b = bias[:, 2 * j + k:2 * j + k + 1] if bias is not None else 0.0
                    s = slice(k * 512, (k + 1) * 512)
                    th = act.activation(fh.ap[:, s], ps.ap[:, s], func, bias=b, w=(ts[k], *fh.last))
                    a = act.activation(f.ap[:, s], ps.ap[:, s], func, bias=b, w=(*f.last,))
                    aa.append(a)
                units.give(ps, a)
                acts.append((j, f, fh, fl, aa))
                if lows:
                    q = lows.pop(0)
                    yield q[3]
                    second(*q)
            q = acts.pop(0)
            yield q[4][0]
            q = (q[0], q[2], q[3], *low(*q))
            yield q[3]
            done["x"] = last_in
            done["t"] = second(*q)
            done["o"] = o
            yield done["t"]

        routed = [0, 0]

        def route(which, g, cap, xT, wT, dst_slot, dst_w, *w):
            yield lambda: routed[which] == g
            yield units.has()
            yield lambda: len(rtl.idle) >= 2 and len(ohs.idle) >= 1 and len(sm.idle) >= 1
            ps = units.take()
            for i in range(4):
                for c in range(2):
                    t = pe.matmul(ps.ap[:, i * 8:i * 8 + 8], xT[:, c * 512 + i * 128:c * 512 + i * 128 + 128], wT[:,
                        c, :], start=c == 0, stop=c == 1, w=(w_late, *w, *ps.last))
            last_x = t
            lg, cd, s, oh = rtl.take(), rtl.take(), sm.take(), ohs.take()
            L, X = v3(lg.ap[:, 0:32], 4, 8), v3(lg.ap[:, 32:64], 4, 8)
            code, sl = v3(cd.ap[:, 0:32], 4, 8), v3(cd.ap[:, 32:64], 4, 8)
            mx, cm, se = s.ap[:, 0:4], s.ap[:, 4:8], s.ap[:, 8:12]
            slf = s.ap[:, 12:16]
            yield t
            t = ve.tensor_copy(L, v3(ps.ap[:, 0:32], 4, 8), w=(t, *lg.last))
            units.give(ps, t)
            t1 = ve.tensor_reduce(mx, L, AX.X, ALU.max, w=(t, *s.last))
            mxb = mx.unsqueeze(2).to_broadcast([128, 4, 8])
            t2 = ve.tensor_tensor(X, L, mxb, ALU.subtract, w=(t1,))
            t3 = ve.tensor_scalar(code, X, 0.0, None, ALU.is_equal, w=(t2, *cd.last))
            tp = po.tensor_tensor(lg.ap[:, 0:32], ecol[:, :], lg.ap[:, 32:64], ALU.pow, w=(t2, C["pool"]))
            t4 = ve.tensor_tensor(code, code, desc[:, :].unsqueeze(1).to_broadcast([128, 4, 8]), ALU.mult, w=(t3,))
            t5 = ve.tensor_reduce(cm, code, AX.X, ALU.max, w=(t4,))
            t6 = ve.tensor_tensor(v3(oh.ap, 4, 8), code, cm.unsqueeze(2).to_broadcast([128, 4, 8]), ALU.is_equal,
                w=(t5, *oh.last))
            yield t6
            yield units.has()
            ps = units.take()
            for i in range(5):
                ops = [(ones, k) for k in range(min(i, 4))] + ([(tri, i)] if i < 4 else [])
                for n, (m, k) in enumerate(ops):
                    t = pe.matmul(ps.ap[:, i * 8:i * 8 + 8], m[:, :], oh.ap[:, k * 8:k * 8 + 8], start=n == 0,
                        stop=n == len(ops) - 1, w=(t6, C["tri"], *ps.last))
            yield t
            t1 = ve.tensor_tensor(sl, v3(ps.ap[:, 0:32], 4, 8), base[:, which, :].unsqueeze(1).to_broadcast([128, 4,
                8]), ALU.add, w=(t, base_t[which], C["pool"]))
            t2 = ve.tensor_tensor(base[:, which, :], base[:, which, :], ps.ap[:, 32:40], ALU.add, w=(t1,))
            base_t[which] = t2
            units.give(ps, t2)
            t3 = ve.tensor_scalar(code, sl, float(cap), FAR, ALU.is_ge, ALU.mult, w=(t1,))
            t4 = ve.tensor_tensor(sl, sl, offs[:, which, :].unsqueeze(1).to_broadcast([128, 4, 8]), ALU.add, w=(t3,))
            t5 = ve.tensor_tensor(sl, sl, code, ALU.add, w=(t4,))
            t6 = ve.tensor_tensor(sl, sl, v3(oh.ap, 4, 8), ALU.mult, w=(t5,))
            t7 = ve.tensor_reduce(slf, sl, AX.X, ALU.add, w=(t6,))
            t8 = ve.tensor_copy(dst_slot, slf, w=(t7,))
            t9 = ve.tensor_reduce(se, L, AX.X, ALU.add, w=(tp,))
            t10 = ve.reciprocal(dst_w, se, w=(t9,))
            ohs.give(oh, t6)
            rtl.give(lg, t10)
            rtl.give(cd, t8)
            sm.give(s, t10)
            routed[which] += 1
            return last_x, t8, t10

        base_t = [C["pool"], C["pool"]]

        pay_sem = {id(t): new_sem(f"s_pay{i}") for i, t in enumerate(pay.idle)}
        ft_sem = {id(t): new_sem(f"s_ft{i}") for i, t in enumerate(tiles_w + borrowed[0] + borrowed[1] + lent)}
        rt_sem = ft_sem
        out_sem = {id(t): new_sem(f"s_out{i}") for i, t in enumerate(pay.idle)}
        scat_sem = {id(t): new_sem(f"s_sc{i}") for i, t in enumerate(pay.idle + ft.idle)}
        s_b1 = new_sem("s_b1")
        s_fill = new_sem("s_fill")

        def tok_rows(ap, g):
            return ap[g * 512:(g + 1) * 512, :].rearrange("(t p) n -> p t n", p=128)

        def load_x(src, g, *w):
            t = ft.take()
            ld = dma(sp, ft_sem[id(t)], v3(t.ap, 4, 256), tok_rows(src, g), w=(*t.last, *w))
            return t, ld

        def filling():
            f = pay.take()
            a = ve.memset(f.ap[:, :, :], 0.0)
            b = ve.memset(f.ap[:, :, 260:261].bitcast(U), 1000000, w=(a,))
            for d, n in ((d_p1, E), (d_p2, 2 * E)):
                for i in range(n):
                    t = dma(sp, s_fill, tok_rows(d, i), f.ap[:, :, :], w=(b,), store=True)
                    if i % 2:
                        yield
            pay.give(f, t)
            filled.append(t)

        filled = []
        fills = filling()

        w1p_h, w1p_l = v3(small[:, 0:512], 2, 256), v3(small[:, 512:1024], 2, 256)
        wl2_h, wl2_l = v3(small[:, 1024:1536], 2, 256), v3(small[:, 1536:2048], 2, 256)
        a12_h, a12_l = v3(small[:, 2048:3072], 2, 512), v3(small[:, 3072:4096], 2, 512)
        wg1_h, wg1_l = v3(small[:, 4096:4608], 2, 256), v3(small[:, 4608:5120], 2, 256)

        def load_f(name, t=None):
            t = t or ft.take()
            ld = dma(sp, ft_sem[id(t)], v3(t.ap[:, 0:512], 2, 256), chunks(io[name], 256), w=(*t.last,))
            return t, v3(t.ap[:, 0:512], 2, 256), ld

        def mm256(ps, lhs, rhs, w, start=True, stop=True):
            for oc in range(2):
                for c in range(2):
                    t = pe.matmul(ps[:, oc * 512:oc * 512 + 256], lhs[:, c, oc * 128:oc * 128 + 128], rhs[:, c, :],
                        start=start and c == 0, stop=stop and c == 1, w=(*w,))
            return t

        def two(ps):
            return ps.rearrange("p (a b) -> p a b", a=2)[:, :, 0:256]

        def prepare():
            r = {}
            wi, wi_v, t1 = load_f("Wi")
            wl1, wl1_v, t2 = load_f("Wl1T")
            ps = units.take()
            t = mm256(ps.ap, wi_v, wl1_v, (t1, t2, *ps.last))
            a, b = evac(w1p_h, w1p_l, two(ps.ap), t)
            units.give(ps, a, b)
            r["w1p"] = b
            ps = units.take()
            for oc in range(2):
                for c in range(2):
                    t = pe.matmul(ps.ap[:, oc:oc + 1], wl1_v[:, c, oc * 128:oc * 128 + 128], bi_c[:, c:c + 1],
                        start=c == 0, stop=c == 1, w=(w_small, *ps.last))
            r["b1p"] = ve.tensor_tensor(cols[:, 24:26], ps.ap[:, 0:2], bl1_c, ALU.add, w=(t,))
            units.give(ps, r["b1p"])
            ft.give(wi, t)
            ft.give(wl1, t)
            wl2, wl2_v, t1 = load_f("Wl2T")
            a, b = split(wl2_h, wl2_l, wl2_v, t1)
            r["wl2"] = b
            ft.give(wl2, a, b)
            return r

        P = prepare()
        b1p = cols[:, 24:26]

        gram = units.take()

        def hidden(kT, n, acc, *w):
            yield room(f=1, r=2, u=1)
            f, fh, fl = ft.take(), rt.take(), rt.take()
            ps = units.take()
            for oc in range(2):
                t = wide(ps.ap[:, oc * 512:oc * 512 + n], w1p_h, w1p_l, kT[0].ap, kT[1].ap, n,
                         (*w, P["w1p"], *ps.last), oc)
            rt.give(kT[0], t)
            rt.give(kT[1], t)
            yield t
            for oc in range(2):
                for dst in (f, fh):
                    a = act.activation(dst.ap[:, oc * 512:oc * 512 + n], ps.ap[:, oc * 512:oc * 512 + n], ACT.Silu,
                        bias=b1p[:, oc:oc + 1], w=(t, P["b1p"], *dst.last))
            units.give(ps, a)
            yield a
            tl = None
            for oc in range(2):
                s = slice(oc * 512, oc * 512 + n)
                tl = ve.tensor_tensor(fl.ap[:, s], f.ap[:, s], f32(fh.ap[:, s]), ALU.subtract, w=(a, *fl.last))
            ft.give(f, tl)
            yield tl
            yield room(f=1, r=1, u=1)
            h, hh = ft.take(), rt.take()
            ps = units.take()
            for oc in range(2):
                t = wide(ps.ap[:, oc * 512:oc * 512 + n], wl2_h, wl2_l, fh.ap, fl.ap, n,
                         (tl, P["wl2"], *ps.last), oc)
            rt.give(fh, t)
            rt.give(fl, t)
            yield t
            m = n if n == 512 else 10
            for oc in range(2):
                a1 = act.activation(h.ap[:, oc * 512:oc * 512 + m], ps.ap[:, oc * 512:oc * 512 + m], ACT.Silu,
                    bias=bl2_c[:, oc:oc + 1], accum_out=acc[oc], w=(t, w_small, *h.last))
            if n == 512:
                for oc in range(2):
                    a = act.activation(hh.ap[:, oc * 512:oc * 512 + n], ps.ap[:, oc * 512:oc * 512 + n], ACT.Silu,
                        bias=bl2_c[:, oc:oc + 1], w=(*hh.last,))
            else:
                a = a1
            units.give(ps, a)
            return h, hh, a1, a

        def slots_of_memory():
            yield room(f=4, r=5, u=1)
            x, kt = ft.take(), ft.take()
            z = ve.memset(x.ap[:, 0:256], 0.0, w=(*x.last,))
            ld = dma(sp, ft_sem[id(x)], x.ap[0:10, 0:256], io["P"], w=(z,))
            s = sm.take()
            a = act.activation(x.ap[:, 256:512], x.ap[:, 0:256], ACT.Square, accum_out=s.ap[:, 0:1], w=(ld, z))
            b = po.tensor_tensor(s.ap[:, 1:2], s.ap[:, 0:1], half[:, 4:5], ALU.pow, w=(a, C["pool"]))
            b = ve.tensor_scalar(s.ap[:, 2:3], s.ap[:, 1:2], 1e-12, None, ALU.max, w=(b,))
            b = ve.reciprocal(s.ap[:, 3:4], s.ap[:, 2:3], w=(b,))
            kn = ve.tensor_scalar(x.ap[:, 512:768], x.ap[:, 0:256], s.ap[:, 3:4], None, ALU.mult, w=(b,))
            sm.give(s, kn)
            yield kn
            yield room(r=2, u=1)
            ps = units.take()
            for c in range(2):
                t = pe.transpose(ps.ap[:, c * 512:c * 512 + 128], x.ap[:, 512 + c * 128:512 + c * 128 + 128], ident[:,
                    :], w=(kn, C["ident"], *ps.last))
            kh, kl = rt.take(), rt.take()
            for c in range(2):
                q = slice(c * 512, c * 512 + 128)
                a, b = evac(kh.ap[:, q], kl.ap[:, q], ps.ap[:, q], t, *kh.last, *kl.last)
            units.give(ps, a, b)
            h, hh, a1, _ = yield from hidden((kh, kl), 128, [hsum[:, 0, 16:17], hsum[:, 1, 16:17]], a, b)
            rt.give(hh, *hh.last)
            yield a1
            yield room(r=3, u=1)
            ps = units.take()
            for c in range(2):
                t = pe.transpose(ps.ap[0:10, c * 128:c * 128 + 128], h.ap[:, c * 512:c * 512 + 10], ident[:, :],
                    w=(a1, *ps.last))
            ft.give(h, t)
            rh, rl, ll = rt.take(), rt.take(), rt.take()
            z = ve.memset(kt.ap, 0.0, w=(*kt.last,))
            z1 = ve.tensor_copy(kt.ap[0:10, 0:256], ps.ap[0:10, 0:256], w=(z, t))
            z2 = ve.tensor_copy(kt.ap[:, 256:512], x.ap[:, 512:768], w=(kn, z))
            z3 = ve.tensor_scalar(kt.ap[0:10, 512:768], ps.ap[0:10, 0:256], 8.0, None, ALU.mult, w=(z2,))
            units.give(ps, z3)
            a, b = split(rh.ap[:, 0:512], rl.ap[:, 0:512], kt.ap[:, 0:512], z1, z2, *rh.last, *rl.last)
            a, b2 = split(ll.ap[:, 0:256], ll.ap[:, 256:512], kt.ap[:, 512:768], z3, *ll.last)
            ft.give(kt, a, b, b2)
            ft.give(x, z2, a)
            for c in range(2):
                t = three(gram.ap[:, c * 512:(c + 1) * 512],
                          [(ll.ap[:, c * 128:c * 128 + 128], ll.ap[:, 256 + c * 128:256 + c * 128 + 128],
                            rh.ap[:, 0:512], rl.ap[:, 0:512])], True, False, (b, b2, *gram.last))
            for q in (rh, rl, ll):
                rt.give(q, t)
            slots_done.append(a1)

        slots_done = []
        hstore = {}

        def first(g):
            yield room(f=3)
            x, ld = load_x(io["x"], g)
            kn = ft.take()
            yield ld
            s = sm.take()
            mv = v3(s.ap[:, 0:8], 4, 2)
            xv = v3(x.ap, 4, 256)
            c4 = slice(4 * g, 4 * g + 4)
            t, _ = stats(xv, mv, ld, *s.last)
            t0 = ve.tensor_copy(mean[:, c4], mv[:, :, 0], w=(t,))
            yield t
            r = rsqrt(rstd[:, c4], mv[:, :, 1], s.ap[:, 8:12], t)
            a = po.tensor_tensor(s.ap[:, 12:16], mv[:, :, 1], half[:, 4:8], ALU.pow, w=(t,))
            a = po.tensor_tensor(s.ap[:, 16:20], s.ap[:, 12:16], rstd[:, c4], ALU.mult, w=(a, r))
            yield a
            b = ve.tensor_scalar(s.ap[:, 20:24], s.ap[:, 16:20], 16.0, 1e-12, ALU.mult, ALU.max, w=(a,))
            b = ve.reciprocal(s.ap[:, 24:28], s.ap[:, 20:24], w=(b,))
            b = ve.tensor_tensor(s.ap[:, 28:32], s.ap[:, 24:28], rstd[:, c4], ALU.mult, w=(b,))
            t = norm(v3(kn.ap, 4, 256), xv, mean[:, c4], s.ap[:, 28:32], b, t0, *kn.last)
            sm.give(s, t)
            ft.give(x, t)
            yield t
            knv = v3(kn.ap, 4, 256)
            kh, kl, a, b, tt = yield from turned(knv, t)
            yield b
            h, hh, a1, a = yield from hidden((kh, kl), 512, [hsum[:, 0, g:g + 1], hsum[:, 1, g:g + 1]], a, b)
            yield room(r=5, u=1)
            hl = rt.take()
            rows_h, rows_l = [rt.take(), rt.take()], [rt.take(), rt.take()]
            ps = units.take()
            tp = to_tokens(ps.ap, h.ap, a1, *ps.last)
            for k in range(2):
                rv, lv = v3(rows_h[k].ap, 2, 512), v3(rows_l[k].ap, 2, 512)
                ka = act.activation(rv[:, :, 256:512], knv[:, 2 * k:2 * k + 2, :], ACT.Copy, w=(t, *rows_h[k].last))
                kb = po.tensor_tensor(lv[:, :, 256:512], knv[:, 2 * k:2 * k + 2, :], f32(rv[:, :, 256:512]),
                    ALU.subtract, w=(ka, *rows_l[k].last))
            ft.give(kn, tt, kb)
            yield tp
            for k in range(2):
                rv, lv = v3(rows_h[k].ap, 2, 512), v3(rows_l[k].ap, 2, 512)
                src = v3(ps.ap[:, k * 512:(k + 1) * 512], 2, 256)
                a_, b_ = evac(rv[:, :, 0:256], lv[:, :, 0:256], src, tp, *rows_l[k].last)
            units.give(ps, a_, b_)
            b = ve.tensor_tensor(hl.ap, h.ap, f32(hh.ap), ALU.subtract, w=(a, *hl.last))
            ft.give(h, tp, b)
            o1 = dma(sp, rt_sem[id(hh)], f32(d_h[g, :, 0, :]), f32(hh.ap), w=(a,), store=True)
            o2 = dma(sp, rt_sem[id(hl)], f32(d_h[g, :, 1, :]), f32(hl.ap), w=(b,), store=True)
            hstore[g] = (o1, o2)
            rt.give(hh, o1, b)
            rt.give(hl, o2)
            yield (b_, kb)
            yield lambda: slots_done
            for i in range(4):
                rh, rl = rows_h[i // 2].ap, rows_l[i // 2].ap
                o = (i % 2) * 512
                gram_n[0] += 1
                for c in range(2):
                    t = three(gram.ap[:, c * 512:(c + 1) * 512],
                              [(rh[:, o + c * 128:o + c * 128 + 128], rl[:, o + c * 128:o + c * 128 + 128],
                                rh[:, o:o + 512], rl[:, o:o + 512])], False, gram_n[0] == 4 * G, (a_, b_, kb))
            for q in rows_h + rows_l:
                rt.give(q, t)
            first_done[g] = t
            next(fills, None)

        gram_n = [0]
        first_done = {}
        sent = [[], []]
        w_late = load_late()

        def middle():
            yield lambda: len(first_done) >= G - 2
            yield room(f=4)

            def load_two(n1, n2):
                q = ft.take()
                for k, n in enumerate((n1, n2)):
                    v = v3(q.ap[:, k * 512:(k + 1) * 512], 2, 256)
                    ld = dma(sp, ft_sem[id(q)], v, chunks(io[n], 256), w=(*q.last,))
                return q, v3(q.ap[:, 0:512], 2, 256), v3(q.ap[:, 512:1024], 2, 256), ld

            qa, wo_v, mwt_v, t_wo = load_two("WoT", "mem_WT")
            qb, wit_v, mw_v, t_wit = load_two("WiT", "mem_W")
            qc, wg2_v, wg1_v, t_wg2 = load_two("Wg2T", "Wg1T")
            t_mwt, t_mw = t_wo, t_wit
            yield t_wg2
            a, wg1_t = split(wg1_h, wg1_l, wg1_v, t_wg2)
            c_free = (a, wg1_t)
            rep = ft.take()
            for c in range(2):
                a = ve.tensor_copy(rep.ap[:, c * 128:(c + 1) * 128], memb_c[:, c:c + 1].to_broadcast([128, 128]),
                    w=(w_small, *rep.last))
            yield units.has()
            ps = units.take()
            for c in range(2):
                t = pe.matmul(ps.ap[:, 0:256], rep.ap[:, c * 128:(c + 1) * 128], wo_v[:, c, :], start=c == 0,
                    stop=c == 1, w=(a, t_wo, *ps.last))
            for oc in range(2):
                for c in range(2):
                    t = pe.matmul(ps.ap[:, 512 + oc:513 + oc], wo_v[:, c, oc * 128:oc * 128 + 128], memb_c[:,
                        c:c + 1], start=c == 0, stop=c == 1)
            cb = ve.tensor_tensor(bias_mg[:, 0:256], ps.ap[:, 0:256], bo_r, ALU.add, w=(t, w_late))
            b = ve.tensor_tensor(cols[:, 26:28], ps.ap[:, 512:514], bo_c, ALU.add, w=(cb,))
            for c in range(2):
                d = ve.tensor_copy(rep.ap[:, 256 + c * 128:256 + (c + 1) * 128], cols[:,
                    26 + c:27 + c].to_broadcast([128, 128]), w=(b,))
            units.give(ps, b)
            yield units.has()
            ps = units.take()
            for c in range(2):
                t = pe.matmul(ps.ap[:, 0:256], rep.ap[:, 256 + c * 128:256 + (c + 1) * 128], wg2_v[:, c, :],
                    start=c == 0, stop=c == 1, w=(d, t_wg2, *ps.last))
            bg = ve.tensor_tensor(bias_mg[:, 256:512], ps.ap[:, 0:256], bg_r, ALU.add, w=(t,))
            units.give(ps, bg)
            ft.give(rep, t)
            a = ve.tensor_scalar(cols[:, 28:29], cols[:, 22:23], -1.0, 1.0, ALU.mult, ALU.add, w=(w_small,))
            sc = ve.tensor_scalar(cols[:, 29:30], cols[:, 23:24], 2.0 / (N_MEM * 256), None, ALU.mult)
            mws = ve.tensor_scalar(mw_v, mw_v, cols[:, 28:29], None, ALU.mult, w=(a, t_mw))
            yield lambda: len(first_done) == G
            p8 = ve.tensor_scalar(hsum[:, :, 17:18], hsum[:, :, 16:17], 8.0, None, ALU.mult, w=(*slots_done,))
            hs = ve.tensor_reduce(cols[:, 30:32], hsum[:, :, 0:16], AX.X, ALU.add, w=(Token(act, len(act.ops) - 1),))
            hs = ve.tensor_tensor(cols[:, 32:34], cols[:, 30:32], hsum[:, :, 17], ALU.add, w=(hs, p8))
            r0 = ve.tensor_tensor(mb_row[0:1, 0:256], mb_row[0:1, 0:256], mb_row[0:1, 256:512], ALU.subtract,
                w=(w_late,))
            yield room(f=2)
            gs = ft.take()
            ga = act.activation(gs.ap, gram.ap, ACT.Copy, w=(*first_done.values(), *gs.last))
            units.give(gram, ga)
            yield units.has()
            ps = units.take()
            for c in range(2):
                t = pe.matmul(ps.ap[0:1, c * 128:c * 128 + 128], cols[:, 32 + c:33 + c], ident[:, :], start=True,
                    stop=True, w=(hs, *ps.last))
            hr = ve.tensor_copy(mb_row[0:1, 256:512], ps.ap[0:1, 0:256], w=(t, r0))
            for c in range(2):
                for q in range(2):
                    t = pe.transpose(ps.ap[:, 512 + q * 256 + c * 128:512 + q * 256 + c * 128 + 128], gs.ap[:,
                        c * 512 + 256 + q * 128:c * 512 + 256 + q * 128 + 128], ident[:, :], w=(ga,))
            g2 = ft.take()
            gt = ve.tensor_scalar(g2.ap[:, 0:512], ps.ap[:, 512:1024], -1.0, None, ALU.mult, w=(t, *g2.last))
            units.give(ps, gt, hr)
            g2v = v3(g2.ap[:, 0:512], 2, 256)
            gsv = v3(gs.ap, 2, 512)
            yield units.has()
            ps = units.take()
            for m in range(2):
                o = ps.ap[:, m * 512:m * 512 + 256]
                for c in range(2):
                    pe.matmul(o, mwt_v[:, c, m * 128:m * 128 + 128], gsv[:, c, 0:256], start=c == 0, stop=False,
                        w=(ga, t_mwt, *ps.last))
                for c in range(2):
                    pe.matmul(o, wit_v[:, c, m * 128:m * 128 + 128], g2v[:, c, :], start=False, stop=False, w=(gt,
                        t_wit))
                t = pe.matmul(o, mb_row[0:1, m * 128:m * 128 + 128], mb_row[0:1, 256:512], start=False, stop=True,
                    w=(hr, r0))
            wn = ve.scalar_tensor_tensor(mw_v, two(ps.ap), cols[:, 29:30], mw_v, ALU.mult, ALU.add, w=(t, sc, mws))
            units.give(ps, wn)
            ft.give(gs, t)
            yield wn
            yield units.has(2)
            ps, ps2 = units.take(), units.take()
            t = mm256(ps.ap, wo_v, mw_v, (wn, t_wo, *ps.last))
            t2 = mm256(ps2.ap, mw_v, wo_v, (wn, *ps2.last))
            a1v = v3(g2.ap[:, 512:1024], 2, 256)
            b1 = act.activation(a1v, two(ps.ap), ACT.Copy, w=(t,))
            units.give(ps, b1)
            ea, eb = evac(a12_h[:, :, 0:256], a12_l[:, :, 0:256], two(ps2.ap), t2)
            units.give(ps2, ea, eb)
            ft.give(qa, t2)
            ft.give(qb, t2)
            yield units.has()
            ps = units.take()
            t = mm256(ps.ap, a1v, wg2_v, (b1, t_wg2, *ps.last))
            fa, fb = evac(a12_h[:, :, 256:512], a12_l[:, :, 256:512], two(ps.ap), t)
            units.give(ps, fa, fb)
            ft.give(g2, t)
            ft.give(qc, t, *c_free)
            A12_t.extend([eb, fb, wg1_t])
            bmg_t.append(bg)

        bias_mg = rows[:, 10:12, :].rearrange("p a b -> p (a b)")
        A12_t, bmg_t, WA = [], [], {}

        def reclaim(tiles, when):
            yield when
            for b in tiles:
                yield lambda: b in rt.idle
                rt.idle.remove(b)

        def slot_free(n):
            return [x for b in borrowed[n] for x in b.last]

        def weights_a():
            yield from reclaim(borrowed[0], lambda: len(first_done) >= G - 1)
            WA.update(ff_weights(0, io["W1T"], io["W2T"], *slot_free(0)))

        last_group = {}

        def load_h(g):
            hh, hl = rt.take(), rt.take()
            t1 = dma(sp, rt_sem[id(hh)], f32(hh.ap), f32(d_h[g, :, 0, :]), w=(*hh.last, hstore[g][0]))
            t2 = dma(sp, rt_sem[id(hl)], f32(hl.ap), f32(d_h[g, :, 1, :]), w=(*hl.last, hstore[g][1]))
            return hh, hl, t1, t2

        def affine(x, gr, br, *w):
            a = po.tensor_tensor(x, x, gr.unsqueeze(1).to_broadcast([128, 4, 256]), ALU.mult, w=(*w,))
            return po.tensor_tensor(x, x, br.unsqueeze(1).to_broadcast([128, 4, 256]), ALU.add, w=(a,))

        def layernorm(dst, x, *w):
            yield sm.has()
            s = sm.take()
            mv = v3(s.ap[:, 0:8], 4, 2)
            t, _ = stats(x, mv, *w, *s.last)
            yield t
            r = rsqrt(s.ap[:, 12:16], mv[:, :, 1], s.ap[:, 8:12], t)
            yield r
            t = norm(dst, x, mv[:, :, 0], s.ap[:, 12:16], r)
            sm.give(s, t)
            return t

        at_window = [0]

        def second(g):
            yield lambda: g in first_done and at_window[0] == g and len(ft.idle) >= 5
            xl = ft.take()
            xlv = v3(xl.ap, 4, 256)
            ld = dma(sp, ft_sem[id(xl)], xlv, tok_rows(io["x"], g), w=(*xl.last,))
            yield ld
            c4 = slice(4 * g, 4 * g + 4)
            tx = norm(xlv, xlv, mean[:, c4], rstd[:, c4], ld)
            yield tx
            th = ve.tensor_copy(halo[:, 0, :], halo[:, 4, :], w=(*halo_free,)) if g % 2 else None
            th = ve.tensor_copy(halo[:, 1:5, :], xlv[96:128, :, :], w=(tx, *halo_free, *([th] if th else [])))
            yield units.has()
            ps = units.take()
            t = transposes(ps.ap, xlv, tx, *ps.last)
            yield t
            xT = ft.take()
            ta = act.activation(xT.ap, ps.ap, ACT.Copy, w=(t, *xT.last))
            units.give(ps, ta)
            yield ta
            yield units.has()
            ps = units.take()
            for i in range(4):
                for part in range(2):
                    for c in range(2):
                        q = xT.ap[:, c * 512 + i * 128:c * 512 + i * 128 + 128]
                        if part:
                            k = q
                        elif i:
                            k = xT.ap[:, c * 512 + i * 128 - 32:c * 512 + i * 128]
                        elif g % 2:
                            k = last_group["xT"].ap[:, c * 512 + 480:c * 512 + 512]
                        else:
                            k = xT.ap[:, c * 512:c * 512 + 32]
                        o = ps.ap[:, i * 256 + 32 * part:i * 256 + (160 if part else 32)]
                        t = pe.matmul(o, q, k, start=c == 0 and part == 0 and i % 2 == 0, stop=c == 1,
                            skip_group_check=True, w=(ta, *ps.last))
            if g % 2:
                ft.give(last_group["xT"], t)
                ft.give(xT, t)
            else:
                last_group["xT"] = xT
            yield t
            yield room(f=2, s=2)
            sc, pT = ft.take(), ft.take()
            scv = v3(sc.ap[:, 0:640], 4, 160)
            psv = v3(ps.ap, 4, 256)[:, :, 0:160]
            s = sm.take()
            n0 = 0 if g % 2 else 1
            if n0:
                a = ve.tensor_tensor(scv[:, 0, :], psv[:, 0, :], mask[:, 1, :], ALU.add, w=(t, C["mask"], *sc.last))
            a = ve.tensor_tensor(scv[:, n0:4, :], psv[:, n0:4, :], mask[:, 0, :].unsqueeze(1).to_broadcast([128,
                4 - n0, 160]), ALU.add, w=(t, C["mask"], *sc.last))
            units.give(ps, a)
            b = ve.tensor_reduce(s.ap[:, 0:4], scv, AX.X, ALU.max, w=(a, *s.last))
            b = ve.tensor_scalar(s.ap[:, 4:8], s.ap[:, 0:4], -1.0 / 16.0, None, ALU.mult, w=(b,))
            yield b
            for i in range(4):
                ex = act.activation(scv[:, i, :], scv[:, i, :], ACT.Exp, bias=s.ap[:, 4 + i:5 + i], scale=1.0 / 16.0,
                    accum_out=s.ap[:, 8 + i:9 + i], w=(b,))
            yield ex
            ri = ve.reciprocal(s.ap[:, 12:16], s.ap[:, 8:12], w=(ex,))
            yield units.has()
            ps = units.take()
            for i in range(4):
                t = pe.transpose(ps.ap[:, i * 128:(i + 1) * 128], scv[:, i, 32:160], ident[:, :], w=(ex, *ps.last))
                t = pe.transpose(ps.ap[0:32, 512 + i * 128:512 + (i + 1) * 128], scv[:, i, 0:32], ident[:, :])
            ft.give(sc, t)
            yield t
            ta = act.activation(pT.ap[:, 0:512], ps.ap[:, 0:512], ACT.Copy, w=(t, *pT.last))
            tb = act.activation(pT.ap[0:32, 512:1024], ps.ap[0:32, 512:1024], ACT.Copy)
            units.give(ps, tb)
            yield tb
            yield units.has()
            ps = units.take()
            for i in range(4):
                o = ps.ap[:, i * 256:(i + 1) * 256]
                first_of_batch = i == 0 and g % 2 == 0
                pe.matmul(o, pT.ap[:, i * 128:(i + 1) * 128], xlv[:, i, :], start=i % 2 == 0, stop=first_of_batch,
                    skip_group_check=True, w=(ta, tb, *ps.last))
                if not first_of_batch:
                    before = halo[:, i, :]
                    t = pe.matmul(o, pT.ap[0:32, 512 + i * 128:512 + (i + 1) * 128], before, start=False, stop=True,
                        skip_group_check=True, w=(th,))
            halo_free[:] = [t]
            ft.give(pT, t)
            at_window[0] += 1
            yield t
            for i in range(4):
                a = ve.scalar_tensor_tensor(xlv[:, i, :], ps.ap[:, i * 256:(i + 1) * 256], s.ap[:, 12 + i:13 + i],
                    xlv[:, i, :], ALU.mult, ALU.add, w=(t, ri))
            units.give(ps, a)
            sm.give(s, a)
            t = yield from layernorm(xlv, xlv, a)
            x1 = xl
            x1v = xlv
            yield t
            t1 = affine(x1v, g1_r, be1_r, t, w_late)
            yield t1
            yield lambda: at_gate.free() and A12_t
            yield room(f=3, r=4)
            at_gate.enter()
            hh, hl, th1, th2 = load_h(g)
            mg = [ft.take(), ft.take()]
            d = ft.take()
            x1h, x1l, a, b, _ = yield from turned(x1v, t1)
            yield (b, th2)
            for k in range(2):
                yield units.has()
                ps = units.take()
                for i in (2 * k, 2 * k + 1):
                    q = slice((i % 2) * 512, (i % 2) * 512 + 512)
                    three(ps.ap[:, q], [(hh.ap[:, c * 512 + i * 128:c * 512 + i * 128 + 128],
                                         hl.ap[:, c * 512 + i * 128:c * 512 + i * 128 + 128],
                                         a12_h[:, c, :], a12_l[:, c, :]) for c in range(2)], True, False,
                          (th1, th2, *A12_t, *ps.last))
                    q = slice((i % 2) * 512 + 256, (i % 2) * 512 + 512)
                    t = three(ps.ap[:, q], [(x1h.ap[:, c * 512 + i * 128:c * 512 + i * 128 + 128],
                                             x1l.ap[:, c * 512 + i * 128:c * 512 + i * 128 + 128],
                                             wg1_h[:, c, :], wg1_l[:, c, :]) for c in range(2)], False, True, (a, b))
                yield t
                pv = v3(ps.ap, 2, 512)
                for n in (1, 0):
                    to = v3(mg[n].ap, 4, 256)[:, 2 * k:2 * k + 2, :]
                    m = ve.tensor_tensor(to, pv[:, :, n * 256:n * 256 + 256], bias_mg[:,
                        n * 256:n * 256 + 256].unsqueeze(1).to_broadcast([128, 2, 256]), ALU.add, w=(t, *bmg_t,
                            *mg[n].last))
                units.give(ps, m)
            for q in (hh, hl, x1h, x1l):
                rt.give(q, t)
            yield m
            mo, gt = mg
            th = act.activation(gt.ap, gt.ap, ACT.Tanh, scale=0.5, w=(m,))
            td = po.tensor_tensor(d.ap, x1.ap, mo.ap, ALU.subtract, w=(m, *d.last))
            yield td
            ts = ve.tensor_tensor(mo.ap, x1.ap, mo.ap, ALU.add, w=(td,))
            ft.give(x1, ts)
            u = ve.scalar_tensor_tensor(d.ap, gt.ap, 1.0, d.ap, ALU.add, ALU.mult, w=(th, td))
            ft.give(gt, u)
            r = ve.scalar_tensor_tensor(mo.ap, d.ap, 0.5, mo.ap, ALU.mult, ALU.add, w=(u, ts))
            ft.give(d, r)
            at_gate.leave()
            x2 = mo
            x2v = v3(x2.ap, 4, 256)
            t = yield from layernorm(x2v, x2v, r)
            yield t
            t2 = affine(x2v, g2_r, be2_r, t)
            yield t2
            yield lambda: at_ff.free() and WA
            at_ff.enter()
            x2h, x2l, a, b, t = yield from turned(x2v, t2)
            tb = po.tensor_tensor(x2v, x2v, b2_r.unsqueeze(1).to_broadcast([128, 4, 256]), ALU.add, w=(t,))
            yield b
            done = {}
            yield from ff(x2h.ap, x2l.ap, WA, ACT.Silu, b1_c, done, a, b)
            rt.give(x2h, done["x"])
            rt.give(x2l, done["x"])
            at_ff.leave()
            o = done["o"]
            r = ve.tensor_tensor(x2.ap, x2.ap, o.ap, ALU.add, w=(done["t"], tb))
            units.give(o, r)
            ff_done[g] = done["t"]
            t = yield from layernorm(x2v, x2v, r)
            yield t
            t = affine(x2v, g3_r, be3_r, t)
            yield lambda: pay.idle and len(ft.idle) >= 4 and at_tail[0] == g
            p = pay.take()
            pv = p.ap
            x, tk, df = ft.take(), ft.take(), ft.take()
            xv = v3(x.ap, 4, 256)
            ld = dma(sp, ft_sem[id(x)], xv, tok_rows(io["x"], g), w=(*x.last,))
            yield t
            t = yield from layernorm(x2v, x2v, t)
            tn = ve.tensor_tensor(pv[:, :, 0:256], x2v, xv, ALU.add, w=(t, ld, *p.last))
            ft.give(x2, tn)
            ft.give(x, tn)
            yield sm.has(2)
            s = sm.take()
            mv = v3(s.ap[:, 0:8], 4, 2)
            t, _ = stats(pv[:, :, 0:256], mv, tn, *s.last)
            yield t
            r = rsqrt(s.ap[:, 12:16], mv[:, :, 1], s.ap[:, 8:12], t)
            b = po.tensor_tensor(s.ap[:, 16:20], s.ap[:, 12:16], s.ap[:, 12:16], ALU.mult, w=(r,))
            b = po.tensor_tensor(s.ap[:, 20:24], s.ap[:, 16:20], mv[:, :, 1], ALU.mult, w=(b,))
            b = rsqrt(s.ap[:, 24:28], s.ap[:, 20:24], s.ap[:, 28:32], b)
            b = po.tensor_tensor(s.ap[:, 32:36], s.ap[:, 24:28], s.ap[:, 12:16], ALU.mult, w=(b,))
            yield b
            t1 = ve.tensor_copy(pv[:, :, 256], mv[:, :, 0], w=(t,))
            t2 = ve.tensor_copy(pv[:, :, 257], s.ap[:, 12:16], w=(r,))
            t3 = ve.tensor_copy(pv[:, :, 258], s.ap[:, 32:36], w=(b,))
            t4 = ve.tensor_copy(pv[:, :, 260].bitcast(U), ids[:, c4].bitcast(U), w=(C["pool"],))
            t4 = ve.memset(pv[:, :, 261:264], 0.0)
            tkv = v3(tk.ap, 4, 256)
            t = norm(tkv, pv[:, :, 0:256], mv[:, :, 0], s.ap[:, 32:36], b, *tk.last)
            tq = po.tensor_tensor(df.ap, pv[:, :, 0:256], tkv, ALU.add, w=(t, *df.last))
            od = dma(sp, ft_sem[id(df)], tok_rows(d_x1, g), v3(df.ap, 4, 256), w=(tq,), store=True)
            ft.give(df, od)
            sm.give(s, t, t2, t3)
            x1_default.append(od)
            yield t
            yield room(f=1, u=1)
            ps = units.take()
            tT = ft.take()
            tt = transposes(ps.ap, tkv, t, *ps.last)
            ft.give(tk, tt, tq)
            yield tt
            for c in range(2):
                ta = act.activation(tT.ap[:, c * 512:(c + 1) * 512], ps.ap[:, c * 512:(c + 1) * 512], ACT.Identity,
                    scale=lng_c[:, c:c + 1], bias=lnb_c[:, c:c + 1], w=(tt, *tT.last))
            units.give(ps, ta)
            at_tail[0] += 1
            yield ta
            yield sm.has()
            s = sm.take()
            su = s.ap[:, 0:4].bitcast(U)
            lx, t_s, t_w = yield from route(0, g, 512, tT.ap, gwT, su, pv[:, :, 259], ta, *s.last)
            ft.give(tT, lx)
            yield t_w
            for i in range(4):
                tz = scatter(scat_sem[id(p)], d_p1, su[:, i:i + 1], pv[:, i, :], E * 512 - 1, w=(t_s, t_w, t1, t2, t3,
                    t4, *filled))
            pay.give(p, tz)
            sm.give(s, tz)
            sent[0].append(tz)

        at_gate, at_ff, at_tail = Turn(1), Turn(2), [0]
        halo = sb("halo", [32, 5, 256])
        halo_free = []
        ff_done = {}
        x1_default = []
        W0, job_done = {}, {}

        def prefetch0(n):
            w = slot_free(1) if n == 0 else ff_done.values() if n == 1 else (job_done[(512, n - 2, 0)],)
            W0[n] = ff_weights((n + 1) % 2, io["wi"][n], io["wo"][n], *w)

        def early0():
            yield from reclaim(borrowed[1], lambda: at_window[0] >= G - 2)
            prefetch0(0)

        gens = [second(g) for g in range(G)]
        run([slots_of_memory()] + [first(g) for g in range(G)] + [middle(), weights_a()]
            + gens[:G - 3] + [early0()] + gens[G - 3:], KA, "layer 0")

        for t in lent[3:5]:
            t.last = list(ff_done.values())
            rt.idle.append(t)

        def job(e_, i, cap, src, ready, WF, func, bias, dst, gate_only):
            yield pay.has()
            p = pay.take()
            pv = p.ap
            r0 = e_ * cap + i * 512
            ld = dma(sp, pay_sem[id(p)], pv, src[r0:r0 + 512, :].rearrange("(t p) n -> p t n", p=128), w=(*p.last,
                *ready))
            yield ld
            yield lambda: len(ft.idle) >= 2 and at_ff.free()
            at_ff.enter()
            tk = ft.take()
            tkv = v3(tk.ap, 4, 256)
            sc = 258 if not gate_only else 257
            for k in range(4):
                t = ve.tensor_scalar(tkv[:, k, :], pv[:, k, 0:256], pv[:, k, 256:257], pv[:, k, sc:sc + 1],
                    ALU.subtract, ALU.mult, w=(ld, *tk.last))
            yield t
            if gate_only:
                th, tl, a, b, tt = yield from turned(tkv, t)
            else:
                yield room(f=1, r=2, u=1)
                th, tl, f = rt.take(), rt.take(), ft.take()
                ps = units.take()
                tt = transposes(ps.ap, tkv, t, *ps.last)
                yield tt
                for d in (th, f):
                    for c in range(2):
                        a = act.activation(d.ap[:, c * 512:(c + 1) * 512], ps.ap[:, c * 512:(c + 1) * 512],
                            ACT.Identity, scale=lng_c[:, c:c + 1], bias=lnb_c[:, c:c + 1], w=(tt, *d.last))
                units.give(ps, a)
                yield a
                b = ve.tensor_tensor(tl.ap, f.ap, f32(th.ap), ALU.subtract, w=(a, *tl.last))
                ft.give(f, b)
            ft.give(tk, tt)
            yield b
            W = WF()
            done = {}
            yield from ff(th.ap, tl.ap, W, func, bias, done, a, b)
            rt.give(th, done["x"])
            rt.give(tl, done["x"])
            at_ff.leave()
            o = done["o"]
            job_done[(cap, e_, i)] = done["t"]
            yield room(f=1, s=2)
            q = ft.take()
            qv = v3(q.ap, 4, 256)
            s = sm.take()
            mv = v3(s.ap[:, 0:8], 4, 2)
            if gate_only:
                t = ve.tensor_tensor(qv, v3(o.ap, 4, 256), W["b2"].unsqueeze(1).to_broadcast([128, 4, 256]), ALU.add,
                    w=(done["t"], W["tb2"], *q.last))
                units.give(o, t)
                W["free_b2"].last.append(t)
                W["added"] += 1
                t, _ = stats(qv, mv, t, *s.last)
                gt = pv[:, :, 259]
                yield t
                b = po.tensor_tensor(s.ap[:, 16:20], gt, gt, ALU.mult, w=(ld,))
                b = po.tensor_tensor(s.ap[:, 20:24], s.ap[:, 16:20], mv[:, :, 1], ALU.mult, w=(b, t))
                b = rsqrt(s.ap[:, 24:28], s.ap[:, 20:24], s.ap[:, 28:32], b)
                b = po.tensor_tensor(s.ap[:, 12:16], s.ap[:, 24:28], gt, ALU.mult, w=(b,))
            else:
                for k in range(4):
                    t = ve.tensor_scalar(qv[:, k, :], pv[:, k, 0:256], pv[:, k, 256:257], pv[:, k, 257:258],
                        ALU.subtract, ALU.mult, w=(*q.last,))
                for k in range(4):
                    t = ve.scalar_tensor_tensor(qv[:, k, :], o.ap[:, k * 256:(k + 1) * 256], pv[:, k, 259:260], qv[:,
                        k, :], ALU.mult, ALU.add, w=(done["t"], t))
                units.give(o, t)
                t, _ = stats(qv, mv, t, *s.last)
                yield t
                b = rsqrt(s.ap[:, 12:16], mv[:, :, 1], s.ap[:, 8:12], t)
            yield b
            t = norm(qv, qv, mv[:, :, 0], s.ap[:, 12:16], b)
            sm.give(s, t)
            yield t
            t = po.tensor_tensor(qv, qv, pv[:, :, 0:256], ALU.add, w=(t,))
            yield sm.has()
            s = sm.take()
            su = s.ap[:, 0:4].bitcast(U)
            tn = ve.tensor_copy(su, pv[:, :, 260].bitcast(U), w=(ld, *s.last))
            pay.give(p, t, tn)
            yield t
            for k in range(4):
                z = scatter(scat_sem[id(q)], dst, su[:, k:k + 1], qv[:, k, :], T - 1, w=(t, tn, *defaults[cap]))
            ft.give(q, z)
            sm.give(s, z)
            defaults[(cap, "last")].append(z)

        defaults = {512: list(x1_default), (512, "last"): [], (1024, "last"): []}

        def one0(n):
            yield lambda: n in W0
            yield from job(n, 0, 512, d_p1, sent[0], lambda: W0[n], ACT.Gelu, None, d_x1, False)
            if n + 2 < E:
                prefetch0(n + 2)

        prefetch0(1)
        wq_h, wq_l = v3(small[:, 0:1536], 2, 768), v3(small[:, 1536:3072], 2, 768)
        def layer1():
            st = stage.take()
            ld = dma(sp, stage_sem[id(st)], v3(st.ap[:, 0:1536], 2, 768), chunks(io["WqkvT"], 768), w=(*st.last,))
            a, b = split(small[:, 0:1536], small[:, 1536:3072], st.ap[:, 0:1536], ld,
                *ff_done.values())
            stage.give(st, a, b)
            wout, wout_v, t_wout = load_f("WoutT")
            return b, wout, wout_v, t_wout

        wq_t, wout, wout_v, t_wout = layer1()
        if stop != "A":
            run([one0(n) for n in range(E)], KB, "experts0")

        for t in lent[3:5]:
            rt.idle.remove(t)
        free2 = [x for t in lent[3:5] for x in t.last]
        kw = [(v3(small[:, 3072 + i * 1032:3072 + i * 1032 + 516], 2, 258),
               v3(small[:, 3072 + i * 1032 + 516:3072 + (i + 1) * 1032], 2, 258)) for i in range(2)]

        def qkv(g):
            bt = g // 2
            yield room(f=4, r=4)
            x, ld = load_x(d_x1, g, *defaults[(512, "last")])
            xv = v3(x.ap, 4, 256)
            xn = ft.take()
            yield ld
            t = yield from layernorm(v3(xn.ap, 4, 256), xv, ld, *xn.last)
            yield t
            t_x = t
            xh, xl, a, b, t = yield from turned(v3(xn.ap, 4, 256), t)
            ft.give(xn, t)
            yield b
            yield room(f=1, r=2, u=1)
            ps = units.take()
            q, qh, ql = ft.take(), rt.take(), rt.take()
            for oc in range(2):
                t = wide(ps.ap[:, oc * 512:(oc + 1) * 512], wq_h, wq_l, xh.ap, xl.ap, 512, (a, b, wq_t, *ps.last),
                    oc)
            yield t
            tq = ve.tensor_scalar(q.ap, ps.ap, 0.0, 1e-6, ALU.max, ALU.add, w=(t, *q.last))
            units.give(ps, tq)
            yield tq
            q1, q2 = split(qh.ap, ql.ap, q.ap, tq, *qh.last, *ql.last, engine="p")
            ft.give(q, q1, q2)
            ft.give(x, t_x)
            grp[g] = (qh, ql, q1, q2)
            for k in range(2):
                yield room(f=1, r=2, u=1)
                ps = units.take()
                f, fh, fl = ft.take(), rt.take(), rt.take()
                for i in (2 * k, 2 * k + 1):
                    t = three(ps.ap[:, (i % 2) * 512:(i % 2) * 512 + 512],
                              [(xh.ap[:, c * 512 + i * 128:c * 512 + i * 128 + 128],
                                xl.ap[:, c * 512 + i * 128:c * 512 + i * 128 + 128],
                                wq_h[:, c, 256:768], wq_l[:, c, 256:768]) for c in range(2)], True, True,
                              (*ps.last,))
                if k == 1:
                    rt.give(xh, t)
                    rt.give(xl, t)
                yield t
                pv, fv, hv, lv = (v3(z.ap, 2, 512) for z in (ps, f, fh, fl))
                t1 = ve.tensor_scalar(fv[:, :, 0:256], pv[:, :, 0:256], 0.0, 1e-6, ALU.max, ALU.add, w=(t, *f.last))
                t2 = act.activation(fv[:, :, 256:512], pv[:, :, 256:512], ACT.Copy, w=(t1,))
                units.give(ps, t1, t2)
                yield t2
                a1 = act.activation(fh.ap, f.ap, ACT.Copy, w=(t1, t2, *fh.last))
                yield a1
                b1 = (po, ve)[k].tensor_tensor(fl.ap, f.ap, f32(fh.ap), ALU.subtract, w=(a1, *fl.last))
                ft.give(f, a1, b1)
                yield b1
                if n_kv.get(bt, 0) == 0:
                    yield lambda: len(units.idle) >= 2 and (n_kv.get(bt, 0) or kv_turn.free())
                    if n_kv.get(bt, 0) == 0:
                        kv_turn.enter()
                        kv[bt] = units.take()
                kvps = kv[bt]
                n_kv[bt] = n_kv.get(bt, 0) + 1
                for i in range(2):
                    st0 = n_kv[bt] == 1 and i == 0
                    last = n_kv[bt] == 4 and i == 1
                    for c in range(2):
                        vh, vl = (z[:, i, 256 + c * 128:256 + c * 128 + 128] for z in (hv, lv))
                        three(kvps.ap[:, c * 256:(c + 1) * 256], [(vh, vl, hv[:, i, 0:256], lv[:, i, 0:256])],
                              st0 and c == 0, last, (a1, b1, *kvps.last))
                    for c in range(2):
                        kh_, kl_ = (z[:, i, c * 128:c * 128 + 128] for z in (hv, lv))
                        o = kvps.ap[:, 512 + 2 * c:514 + 2 * c]
                        pe.matmul(o, kh_, oner[:, :], start=st0 and c == 0, stop=False, skip_group_check=True,
                            w=(C["oner"],))
                        t = pe.matmul(o, kl_, oner[:, :], start=False, stop=last, skip_group_check=True)
                rt.give(fh, t)
                rt.give(fl, t)
            if n_kv[bt] == 4:
                kv_done[bt] = t

        def kv_out(bt):
            yield lambda: n_kv.get(bt, 0) == 4
            kvps = kv[bt]
            t = kv_done[bt]
            yield t
            yield ft.has()
            kvf = ft.take()
            kt = act.activation(kvf.ap[:, 0:512], kvps.ap[:, 0:512], ACT.Copy, w=(t, *kvf.last))
            kt2 = act.activation(kvf.ap[:, 512:516], kvps.ap[:, 512:516], ACT.Copy)
            units.give(kvps, kt2)
            kv_turn.leave()
            yield kt2
            yield lambda: units.idle and (bt < 2 or len(kw_free.get(bt - 2, ())) == 2)
            ps = units.take()
            t = mm256(ps.ap, v3(kvf.ap[:, 0:512], 2, 256), wout_v, (kt, t_wout, *ps.last))
            kh, kl = kw[bt % 2]
            yield t
            kf = kw_free[bt - 2] if bt > 1 else ()
            a, b = evac(kh[:, :, 0:256], kl[:, :, 0:256], two(ps.ap), t, *kf, *free2)
            units.give(ps, a, b)
            kc = v3(kvf.ap[:, 512:516], 2, 2)
            a2, b2 = split(kh[:, :, 256:258], kl[:, :, 256:258], kc, kt2)
            ft.give(kvf, a2, b2, t)
            yield b2
            kw_t[bt] = (kh, kl, (a, b, a2, b2))

        def att_out(g):
            bt = g // 2
            yield lambda: bt in kw_t
            kh, kl, kt = kw_t[bt]
            qh, ql, q1, q2 = grp[g]
            yield room(f=2, s=2)
            r = ft.take()
            rv = v3(r.ap, 4, 256)
            s = sm.take()
            for k in range(2):
                yield units.has()
                ps = units.take()
                for i in (2 * k, 2 * k + 1):
                    t = three(ps.ap[:, (i % 2) * 512:(i % 2) * 512 + 258],
                              [(qh.ap[:, c * 512 + i * 128:c * 512 + i * 128 + 128],
                                ql.ap[:, c * 512 + i * 128:c * 512 + i * 128 + 128],
                                kh[:, c, :], kl[:, c, :]) for c in range(2)], True, True,
                              (q1, q2, *kt, *ps.last))
                yield t
                pv = v3(ps.ap, 2, 512)
                z0 = s.ap[:, 4 * k:4 * k + 2]
                z1 = s.ap[:, 4 * k + 2:4 * k + 4]
                d = ve.tensor_scalar(z0, pv[:, :, 256], 1e-6, None, ALU.add, w=(t, *s.last))
                d = ve.reciprocal(z1, z0, w=(d,))
                for i in range(2):
                    m = ve.scalar_tensor_tensor(rv[:, 2 * k + i, :], pv[:, i, 0:256], z1[:, i:i + 1], bout_r,
                        ALU.mult, ALU.add, w=(d, w_late, *r.last))
                units.give(ps, m)
            rt.give(qh, t)
            rt.give(ql, t)
            sm.give(s, m)
            kw_free.setdefault(bt, []).append(t)
            yield m
            x, ld = load_x(d_x1, g, *defaults[(512, "last")])
            xv = v3(x.ap, 4, 256)
            t = yield from layernorm(rv, rv, m)
            yield lambda: pay.idle and at_pay[0] == g
            at_pay[0] += 1
            p = pay.take()
            pv = p.ap
            tn = ve.tensor_tensor(pv[:, :, 0:256], rv, xv, ALU.add, w=(t, ld, *p.last))
            ft.give(r, tn)
            ft.give(x, tn)
            od = dma(sp, out_sem[id(p)], tok_rows(out, g), pv[:, :, 0:256], w=(tn,), store=True)
            out_default.append(od)
            yield sm.has(2)
            s = sm.take()
            mv = v3(s.ap[:, 0:8], 4, 2)
            t, _ = stats(pv[:, :, 0:256], mv, tn, *s.last)
            yield t
            rr = rsqrt(s.ap[:, 12:16], mv[:, :, 1], s.ap[:, 8:12], t)
            yield rr
            c4 = slice(4 * g, 4 * g + 4)
            t1 = ve.tensor_copy(pv[:, :, 256], mv[:, :, 0], w=(t,))
            t4 = ve.tensor_copy(pv[:, :, 260].bitcast(U), ids[:, c4].bitcast(U))
            t4 = ve.memset(pv[:, :, 261:264], 0.0)
            t4 = ve.memset(pv[:, :, 258], 0.0)
            t2 = ve.tensor_copy(pv[:, :, 257], s.ap[:, 12:16], w=(rr,))
            yield ft.has(2)
            xn = ft.take()
            tT = ft.take()
            t = norm(v3(xn.ap, 4, 256), pv[:, :, 0:256], mv[:, :, 0], s.ap[:, 12:16], rr, *xn.last)
            sm.give(s, t, t2)
            yield t
            yield units.has()
            ps = units.take()
            tt = transposes(ps.ap, v3(xn.ap, 4, 256), t, *ps.last)
            ft.give(xn, tt)
            yield tt
            ta = act.activation(tT.ap, ps.ap, ACT.Copy, w=(tt, *tT.last))
            units.give(ps, ta)
            yield ta
            yield sm.has(2)
            s = sm.take()
            su = s.ap[:, 0:4].bitcast(U)
            lx, t_s, t_w = yield from route(1, g, 1024, tT.ap, wgT, su, pv[:, :, 259], ta, *s.last)
            ft.give(tT, lx)
            yield t_w
            for i in range(4):
                tz = scatter(scat_sem[id(p)], d_p2, su[:, i:i + 1], pv[:, i, :], E * 1024 - 1, w=(t_s, t_w, t1,
                    t2, t4))
            pay.give(p, tz, od)
            sm.give(s, tz)
            sent[1].append(tz)

        kv, n_kv, kv_done, kw_t, kw_free, grp = {}, {}, {}, {}, {}, {}
        kv_turn, at_pay = Turn(1), [0]
        out_default = []
        if stop not in ("A", "A1", "B"):
            for n in range(2):
                for b in borrowed[n]:
                    b.last = [job_done[(512, 7 - n, 0)]]
                rt.idle += borrowed[n]
            b1e = sb("b1e", [128, 64])
            b1e_t = dma(sp, s_b1, b1e[:, :], io["eb1_c"])
            b2e = [Tile(rows[:, i, :], "b2e") for i in range(2)]
            s_b2 = [new_sem(f"s_b2{i}") for i in range(2)]
            W1 = {}

            def prefetch1(n):
                w = (job_done[(1024, n - 2, 0)], job_done[(1024, n - 2, 1)]) if n > 1 else slot_free(1 - n)
                W = ff_weights((n + 1) % 2, io["w1"][n], io["w2"][n], *w)
                bt = b2e[n % 2]
                W["b2"], W["free_b2"], W["added"] = bt.ap, bt, 0
                W["tb2"] = dma(sp, s_b2[n % 2], bt.ap, io["eb2"][n].partition_broadcast(128), w=(*bt.last, *w))
                W1[n] = W

            def early1():
                for n in range(2):
                    yield from reclaim(borrowed[1 - n], lambda: len(kw_t) == 8)
                    prefetch1(n)

            gens = []
            for bt in range(8):
                gens += [qkv(2 * bt), qkv(2 * bt + 1), kv_out(bt)]
                if bt == 7:
                    gens.append(early1())
                gens += [att_out(2 * bt), att_out(2 * bt + 1)]
            run(gens, KC, "layer 1 attention")
            ft.give(wout, *[])
            small_free = [t for v in kw_free.values() for t in v]
            for t in lent:
                t.last = small_free
                rt.idle.append(t)
            defaults[1024] = list(out_default)
            def one1(n, i):
                yield lambda: n in W1
                yield from job(n, i, 1024, d_p2, sent[1], lambda: W1[n], ACT.Relu,
                               b1e[:, 8 * n:8 * n + 8], out, True)
                if i == 1 and n + 2 < E:
                    yield lambda: W1[n]["added"] == 2
                    prefetch1(n + 2)

            act.activation(cols[:, 61:62], cols[:, 60:61], ACT.Copy, w=(b1e_t,))
            run([one1(n, i) for n in range(E) for i in range(2)], KD, "experts1")

        if stop:
            t = dma(sp, s_b1, out, d_x1, w=(*stores,), store=True)

        for q in (pe, act, ve, po, sp):
            q.number()
        block = ctx.enter_context(nc.Block())

        @block.tensor
        def _(eng):
            pe.write(eng)

        @block.scalar
        def _(eng):
            act.write(eng)

        @block.vector
        def _(eng):
            ve.write(eng)

        @block.gpsimd
        def _(eng):
            po.write(eng)

        @block.sync
        def _(eng):
            sp.write(eng)
            for sem in {id(t.sem): t.sem for t in stores}.values():
                eng.wait_ge(sem, landed[id(sem)])


def layouts(i):
    import numpy as np

    def t(a):
        return np.ascontiguousarray(np.asarray(a).T)

    def c(a):
        return np.ascontiguousarray(np.asarray(a).reshape(-1, 128).T)

    a = {k[8:]: np.asarray(v) for k, v in i.items() if k.startswith("L0_attn_")}
    f = {k[7:]: np.asarray(v) for k, v in i.items() if k.startswith("L0_ffn_")}
    q = {k[8:]: np.asarray(v) for k, v in i.items() if k.startswith("L1_attn_")}
    e = {k[7:]: np.asarray(v) for k, v in i.items() if k.startswith("L1_ffn_")}
    wg = t(a["Wg"])
    return {
        "x": a["x"].reshape(8192, 256), "P": a["P"], "mem_b": a["mem_b"], "bi": a["bi"],
        "cols_c": np.concatenate([c(a[k]) for k in ("mem_b", "bi", "bl1", "bl2", "bo", "b1")]
                                 + [c(f["ln_gamma"]), c(f["ln_beta"])], axis=1),
        "fgate": a["fgate"], "lrate": a["lrate"],
        "rows": np.concatenate([a[k] for k in ("g1", "be1", "g2", "be2", "g3", "be3", "b2", "bo", "bg")]
                               + [q["b_out"]]),
        "Wi": a["Wi"], "WiT": t(a["Wi"]), "Wl1T": t(a["Wl1"]), "Wl2T": t(a["Wl2"]), "WoT": t(a["Wo"]),
        "mem_W": a["mem_W"], "mem_WT": t(a["mem_W"]),
        "Wg1T": np.ascontiguousarray(wg[0:256]), "Wg2T": np.ascontiguousarray(wg[256:512]),
        "W1T": t(a["W1"]), "W2T": t(a["W2"]),
        "gate_wT": t(f["gate_weight"]), "wi": f["wi"], "wo": f["wo"],
        "WqkvT": t(q["W_qkv"]), "WoutT": t(q["W_out"]),
        "wg": e["wg"], "w1": e["w1"], "w2": e["w2"],
        "eb1_c": c(e["b1"]), "eb2": e["b2"],
    }


def kernel(**inputs):
    import numpy as np
    import concourse.bacc as bacc
    from concourse.bass_utils import run_bass_kernel_spmd

    nc = bacc.Bacc("TRN2", target_bir_lowering=False, num_devices=1)
    arrays, io = {}, {}
    for name, a in layouts(inputs).items():
        a = np.ascontiguousarray(a)
        arrays["in_" + name] = a
        io[name] = nc.dram_tensor("in_" + name, a.shape, mybir.dt.from_np(a.dtype), kind="ExternalInput").ap()
    io["out"] = nc.dram_tensor("out_x", (T, H), F, kind="ExternalOutput").ap()
    build(nc, io)
    r = run_bass_kernel_spmd(nc, [arrays], core_ids=[0])
    return r.results[0]["out_x"].reshape(8, 1024, 256)
```
